# Optimizing a Trainium2 kernel written in Bass

```python
import numpy as np
import jax
import jax.numpy as jnp

def _softmax(x, axis=-1):
    return jax.nn.softmax(x, axis=axis)

def _gelu(x):
    return jax.nn.gelu(x, approximate=True)

def _silu(x):
    return jax.nn.silu(x)

def _sigmoid(x):
    return jax.nn.sigmoid(x)

def _layernorm(x, axis=-1, eps=1e-05):
    m = jnp.mean(x, axis=axis, keepdims=True)
    v = jnp.var(x, axis=axis, keepdims=True)
    return (x - m) / jnp.sqrt(v + eps)

def _scatter_add(tgt, idx, src, axis=0):
    return tgt.at[idx].add(src)

def _segment_sum(src, seg, n):
    return jax.ops.segment_sum(src, seg, n)
kernel_name = 'mk_pixart_seq_d2_seqx_r2_ff9cdf'

def setup_inputs(seed: int=0):
    np.random.seed(seed)
    _w = jnp.asarray

    def _rec_inputs():
        import jax
        import jax.numpy as jnp
        _rk = jax.random.key(seed)
        x = -0.0003929 + 0.9999 * jax.random.normal(jax.random.fold_in(_rk, 1), (8, 512, 512), jnp.float32)
        _lenS = 512 - jax.random.randint(jax.random.fold_in(_rk, 7), (8,), 0, max(1, 512 // 4) + 1, jnp.int32)
        _lenS2 = 77 - jax.random.randint(jax.random.fold_in(_rk, 8), (8,), 0, max(1, 77 // 4) + 1, jnp.int32)
        _ctx_1024P = jax.random.normal(jax.random.fold_in(_rk, 11), (8, 16, 512), jnp.float32)
        _ctx_1024c = jax.random.dirichlet(jax.random.fold_in(_rk, 511), 0.3 * jnp.ones((16,), jnp.float32), (8, 77))
        _ctx_1024t = jnp.einsum('bsk,bkd->bsd', _ctx_1024c, _ctx_1024P)
        _ctx_1024t = _ctx_1024t * jax.lax.rsqrt(jnp.mean(jnp.square(_ctx_1024t)) + 1e-12) * 0.953939
        ctx_1024 = -1.39393e-06 + 0.999914 * (_ctx_1024t + 0.3 * jax.random.normal(jax.random.fold_in(_rk, 611), (8, 77, 512), jnp.float32))
        cond_1024 = -0.00920427 + 1.00102 * jax.random.normal(jax.random.fold_in(_rk, 12), (8, 512), jnp.float32)
        _validS = jnp.arange(512)[None, :] < _lenS[:, None]
        _validS2 = jnp.arange(77)[None, :] < _lenS2[:, None]
        _causal = jnp.tril(jnp.ones((512, 512), dtype=bool))
        mask_BxS2_bf1 = jnp.ones((8, 77), dtype=bool)
        mask_SxS_bk0 = jnp.logical_not(jnp.broadcast_to(_validS[0:1, :], (512, 512)))
        return (x, ctx_1024, cond_1024, mask_BxS2_bf1, mask_SxS_bk0)
    x, ctx_1024, cond_1024, mask_BxS2_bf1, mask_SxS_bk0 = _rec_inputs()

    def _L0_xcond_setup():
        import jax, jax.numpy as jnp
        import numpy as np
        EPS = 1e-05

        def _ada_ln(x, c, W_ss, b_ss):
            mu = jnp.mean(x, axis=-1, keepdims=True)
            var = jnp.mean((x - mu) ** 2, axis=-1, keepdims=True)
            h = (x - mu) / jnp.sqrt(var + EPS)
            ss = jax.nn.silu(c) @ W_ss + b_ss
            scale, bias = jnp.split(ss, 2, axis=-1)
            return (1.0 + scale)[:, None, :] * h + bias[:, None, :]
        key = jax.random.key(seed)
        ks = jax.random.split(key, 12)
        B, Lq, Lkv, H = (8, 1024, 256, 512)
        s = 0.02
        return {'x_q': jax.random.normal(ks[0], (B, Lq, H), jnp.float32), 'x_kv': jax.random.normal(ks[1], (B, Lkv, H), jnp.float32), 't_vec': jax.random.normal(ks[2], (B, H), jnp.float32), 'Wq': jax.random.normal(ks[3], (H, H), jnp.float32) * s, 'bq': jnp.zeros((H,), jnp.float32), 'Wkv': jax.random.normal(ks[4], (H, 2 * H), jnp.float32) * s, 'bkv': jnp.zeros((2 * H,), jnp.float32), 'Wp': jax.random.normal(ks[5], (H, H), jnp.float32) * s, 'bp': jnp.zeros((H,), jnp.float32), 'Wss_q': jax.random.normal(ks[6], (H, 2 * H), jnp.float32) * s, 'bss_q': jnp.zeros((2 * H,), jnp.float32), 'Wss_kv': jax.random.normal(ks[7], (H, 2 * H), jnp.float32) * s, 'bss_kv': jnp.zeros((2 * H,), jnp.float32)}
    _L0_xcond_all = _L0_xcond_setup()
    _L0_xcond_in = {k: v for k, v in _L0_xcond_all.items() if k in ('Wq', 'bq', 'Wkv', 'bkv', 'Wp', 'bp', 'Wss_q', 'bss_q', 'Wss_kv', 'bss_kv')}
    del _L0_xcond_all

    def _L1_xcond_setup():
        import jax, jax.numpy as jnp
        import numpy as np
        B, N, D, H, LC = (2, 512, 512, 16, 77)
        HD = D // H
        BLOCK = 16
        ROPE_BASE = 10000.0
        EPS = 1e-05

        def _block_diff_mask(n, block_size):
            idx = np.arange(2 * n)
            q = idx[:, None]
            kv = idx[None, :]
            fq = q >= n
            fkv = kv >= n
            bq = np.where(fq, (q - n) // block_size, q // block_size)
            bkv = np.where(fkv, (kv - n) // block_size, kv // block_size)
            block_diagonal = (bq == bkv) & (fq == fkv)
            offset_block_causal = (bq > bkv) & fkv & ~fq
            block_causal = (bq >= bkv) & fq & fkv
            return jnp.asarray(block_diagonal | offset_block_causal | block_causal)

        def _rope_tables(n):
            inv_freq = 1.0 / ROPE_BASE ** (np.arange(0, HD, 2, dtype=np.float32) / HD)
            freqs = np.outer(np.arange(n, dtype=np.float32), inv_freq)
            emb = np.concatenate([freqs, freqs], axis=-1)
            cos = jnp.asarray(np.cos(emb), jnp.float32)[None, :, None, :]
            sin = jnp.asarray(np.sin(emb), jnp.float32)[None, :, None, :]
            return (cos, sin)

        def _ln(x, w):
            xf = x.astype(jnp.float32)
            mu = jnp.mean(xf, axis=-1, keepdims=True)
            var = jnp.mean(jnp.square(xf - mu), axis=-1, keepdims=True)
            y = (xf - mu) * jax.lax.rsqrt(var + EPS)
            return y * w[None, None, :]

        def _apply_rope(t, cos, sin):
            t1, t2 = jnp.split(t, 2, axis=-1)
            rot = jnp.concatenate([-t2, t1], axis=-1)
            return t * cos + rot * sin

        def _attn(q, k, v, mask):
            scale = 1.0 / np.sqrt(HD)
            s = jnp.einsum('bqhd,bkhd->bhqk', q, k) * scale
            s = jnp.where(mask, s, jnp.finfo(s.dtype).min)
            a = jax.nn.softmax(s, axis=-1)
            return jnp.einsum('bhqk,bkhd->bqhd', a, v)
        key = jax.random.key(seed)
        ks = jax.random.split(key, 16)
        w = lambda k, shp: jax.random.normal(k, shp, jnp.float32) * 0.02
        inp = {'x': jax.random.normal(ks[0], (B, 2 * N, D), jnp.float32), 'cond_global': jax.random.normal(ks[1], (B, D), jnp.float32), 'cond_tokens': jax.random.normal(ks[2], (B, LC, D), jnp.float32), 'adaLN_W': w(ks[3], (D, 9 * D)), 'adaLN_b': w(ks[4], (9 * D,)), 'norm1_w': jnp.ones((D,), jnp.float32), 'qkv_W': w(ks[5], (D, 3 * D)), 'attn_out_W': w(ks[6], (D, D)), 'normc_w': jnp.ones((D,), jnp.float32), 'cq_W': w(ks[7], (D, D)), 'ck_W': w(ks[8], (D, D)), 'cv_W': w(ks[9], (D, D)), 'co_W': w(ks[10], (D, D)), 'norm2_w': jnp.ones((D,), jnp.float32), 'mlp_W1': w(ks[11], (D, 4 * D)), 'mlp_b1': w(ks[12], (4 * D,)), 'mlp_W2': w(ks[13], (4 * D, D)), 'mlp_b2': w(ks[14], (D,)), 'cond_kv_mask': jnp.ones((B, LC), bool), 'attn_mask': _block_diff_mask(N, BLOCK)}
        return inp
    _L1_xcond_all = _L1_xcond_setup()
    _L1_xcond_in = {k: v for k, v in _L1_xcond_all.items() if k in ('adaLN_W', 'adaLN_b', 'norm1_w', 'qkv_W', 'attn_out_W', 'normc_w', 'cq_W', 'ck_W', 'cv_W', 'co_W', 'norm2_w', 'mlp_W1', 'mlp_b1', 'mlp_W2', 'mlp_b2')}
    del _L1_xcond_all
    return {'x': x, 'ctx_1024': ctx_1024, 'cond_1024': cond_1024, 'mask_BxS2_bf1': mask_BxS2_bf1, 'mask_SxS_bk0': mask_SxS_bk0, 'L0_xcond_Wq': _L0_xcond_in['Wq'], 'L0_xcond_bq': _L0_xcond_in['bq'], 'L0_xcond_Wkv': _L0_xcond_in['Wkv'], 'L0_xcond_bkv': _L0_xcond_in['bkv'], 'L0_xcond_Wp': _L0_xcond_in['Wp'], 'L0_xcond_bp': _L0_xcond_in['bp'], 'L0_xcond_Wss_q': _L0_xcond_in['Wss_q'], 'L0_xcond_bss_q': _L0_xcond_in['bss_q'], 'L0_xcond_Wss_kv': _L0_xcond_in['Wss_kv'], 'L0_xcond_bss_kv': _L0_xcond_in['bss_kv'], 'L1_xcond_adaLN_W': _L1_xcond_in['adaLN_W'], 'L1_xcond_adaLN_b': _L1_xcond_in['adaLN_b'], 'L1_xcond_norm1_w': _L1_xcond_in['norm1_w'], 'L1_xcond_qkv_W': _L1_xcond_in['qkv_W'], 'L1_xcond_attn_out_W': _L1_xcond_in['attn_out_W'], 'L1_xcond_normc_w': _L1_xcond_in['normc_w'], 'L1_xcond_cq_W': _L1_xcond_in['cq_W'], 'L1_xcond_ck_W': _L1_xcond_in['ck_W'], 'L1_xcond_cv_W': _L1_xcond_in['cv_W'], 'L1_xcond_co_W': _L1_xcond_in['co_W'], 'L1_xcond_norm2_w': _L1_xcond_in['norm2_w'], 'L1_xcond_mlp_W1': _L1_xcond_in['mlp_W1'], 'L1_xcond_mlp_b1': _L1_xcond_in['mlp_b1'], 'L1_xcond_mlp_W2': _L1_xcond_in['mlp_W2'], 'L1_xcond_mlp_b2': _L1_xcond_in['mlp_b2']}

def reference(x, ctx_1024, cond_1024, mask_BxS2_bf1, mask_SxS_bk0, L0_xcond_Wq, L0_xcond_bq, L0_xcond_Wkv, L0_xcond_bkv, L0_xcond_Wp, L0_xcond_bp, L0_xcond_Wss_q, L0_xcond_bss_q, L0_xcond_Wss_kv, L0_xcond_bss_kv, L1_xcond_adaLN_W, L1_xcond_adaLN_b, L1_xcond_norm1_w, L1_xcond_qkv_W, L1_xcond_attn_out_W, L1_xcond_normc_w, L1_xcond_cq_W, L1_xcond_ck_W, L1_xcond_cv_W, L1_xcond_co_W, L1_xcond_norm2_w, L1_xcond_mlp_W1, L1_xcond_mlp_b1, L1_xcond_mlp_W2, L1_xcond_mlp_b2):
    import jax
    import jax.numpy as jnp

    def _L0_xcond_ref(x_q, x_kv, t_vec, Wq, bq, Wkv, bkv, Wp, bp, Wss_q, bss_q, Wss_kv, bss_kv):
        import jax, jax.numpy as jnp
        import numpy as np
        EPS = 1e-05

        def _ada_ln(x, c, W_ss, b_ss):
            mu = jnp.mean(x, axis=-1, keepdims=True)
            var = jnp.mean((x - mu) ** 2, axis=-1, keepdims=True)
            h = (x - mu) / jnp.sqrt(var + EPS)
            ss = jax.nn.silu(c) @ W_ss + b_ss
            scale, bias = jnp.split(ss, 2, axis=-1)
            return (1.0 + scale)[:, None, :] * h + bias[:, None, :]
        B, Lq, H = x_q.shape
        Lkv = x_kv.shape[1]
        nh = 16
        dh = H // nh
        xq = _ada_ln(x_q, t_vec, Wss_q, bss_q)
        xkv = _ada_ln(x_kv, t_vec, Wss_kv, bss_kv)
        q = (xq @ Wq + bq).reshape(B, Lq, nh, dh)
        kv = (xkv @ Wkv + bkv).reshape(B, Lkv, 2, nh, dh)
        k = kv[:, :, 0]
        v = kv[:, :, 1]
        scores = jnp.einsum('bqhd,bkhd->bhqk', q, k) / jnp.sqrt(jnp.float32(dh))
        attn = jax.nn.softmax(scores, axis=-1)
        out = jnp.einsum('bhqk,bkhd->bqhd', attn, v).reshape(B, Lq, H)
        return x_q + (out @ Wp + bp)

    def _L1_xcond_ref(x, cond_global, cond_tokens, adaLN_W, adaLN_b, norm1_w, qkv_W, attn_out_W, normc_w, cq_W, ck_W, cv_W, co_W, norm2_w, mlp_W1, mlp_b1, mlp_W2, mlp_b2, cond_kv_mask, attn_mask):
        import jax, jax.numpy as jnp
        import numpy as np
        B, N, D, H, LC = (2, 512, 512, 16, 77)
        HD = D // H
        BLOCK = 16
        ROPE_BASE = 10000.0
        EPS = 1e-05

        def _block_diff_mask(n, block_size):
            idx = np.arange(2 * n)
            q = idx[:, None]
            kv = idx[None, :]
            fq = q >= n
            fkv = kv >= n
            bq = np.where(fq, (q - n) // block_size, q // block_size)
            bkv = np.where(fkv, (kv - n) // block_size, kv // block_size)
            block_diagonal = (bq == bkv) & (fq == fkv)
            offset_block_causal = (bq > bkv) & fkv & ~fq
            block_causal = (bq >= bkv) & fq & fkv
            return jnp.asarray(block_diagonal | offset_block_causal | block_causal)

        def _rope_tables(n):
            inv_freq = 1.0 / ROPE_BASE ** (np.arange(0, HD, 2, dtype=np.float32) / HD)
            freqs = np.outer(np.arange(n, dtype=np.float32), inv_freq)
            emb = np.concatenate([freqs, freqs], axis=-1)
            cos = jnp.asarray(np.cos(emb), jnp.float32)[None, :, None, :]
            sin = jnp.asarray(np.sin(emb), jnp.float32)[None, :, None, :]
            return (cos, sin)

        def _ln(x, w):
            xf = x.astype(jnp.float32)
            mu = jnp.mean(xf, axis=-1, keepdims=True)
            var = jnp.mean(jnp.square(xf - mu), axis=-1, keepdims=True)
            y = (xf - mu) * jax.lax.rsqrt(var + EPS)
            return y * w[None, None, :]

        def _apply_rope(t, cos, sin):
            t1, t2 = jnp.split(t, 2, axis=-1)
            rot = jnp.concatenate([-t2, t1], axis=-1)
            return t * cos + rot * sin

        def _attn(q, k, v, mask):
            scale = 1.0 / np.sqrt(HD)
            s = jnp.einsum('bqhd,bkhd->bhqk', q, k) * scale
            s = jnp.where(mask, s, jnp.finfo(s.dtype).min)
            a = jax.nn.softmax(s, axis=-1)
            return jnp.einsum('bhqk,bkhd->bqhd', a, v)
        b, s, d = x.shape
        n = s // 2
        mod = (cond_global @ adaLN_W + adaLN_b)[:, None, :]
        sh_msa, sc_msa, g_msa, sh_x, sc_x, g_x, sh_mlp, sc_mlp, g_mlp = jnp.split(mod, 9, axis=-1)
        x_norm = _ln(x, norm1_w) * (1 + sc_msa) + sh_msa
        cos, sin = _rope_tables(n)

        def qkv(h):
            t = (h @ qkv_W).reshape(b, n, 3, H, HD)
            q, k, v = (t[:, :, 0], t[:, :, 1], t[:, :, 2])
            return (_apply_rope(q, cos, sin), _apply_rope(k, cos, sin), v)
        q1, k1, v1 = qkv(x_norm[:, :n])
        q2, k2, v2 = qkv(x_norm[:, n:])
        q = jnp.concatenate([q1, q2], axis=1)
        k = jnp.concatenate([k1, k2], axis=1)
        v = jnp.concatenate([v1, v2], axis=1)
        self_out = _attn(q, k, v, attn_mask[None, None]).reshape(b, s, d) @ attn_out_W
        x = x + g_msa * self_out
        xc = _ln(x, normc_w) * (1 + sc_x) + sh_x
        qc = (xc @ cq_W).reshape(b, s, H, HD)
        kc = (cond_tokens @ ck_W).reshape(b, LC, H, HD)
        vc = (cond_tokens @ cv_W).reshape(b, LC, H, HD)
        cross = _attn(qc, kc, vc, cond_kv_mask[:, None, None, :]).reshape(b, s, d) @ co_W
        x = x + g_x * cross
        xm = _ln(x, norm2_w) * (1 + sc_mlp) + sh_mlp
        h = jax.nn.gelu(xm @ mlp_W1 + mlp_b1, approximate=True)
        mlp_out = h @ mlp_W2 + mlp_b2
        return x + g_mlp * mlp_out
    x = _L0_xcond_ref(x, ctx_1024, cond_1024, L0_xcond_Wq, L0_xcond_bq, L0_xcond_Wkv, L0_xcond_bkv, L0_xcond_Wp, L0_xcond_bp, L0_xcond_Wss_q, L0_xcond_bss_q, L0_xcond_Wss_kv, L0_xcond_bss_kv)
    x = _L1_xcond_ref(x, cond_1024, ctx_1024, L1_xcond_adaLN_W, L1_xcond_adaLN_b, L1_xcond_norm1_w, L1_xcond_qkv_W, L1_xcond_attn_out_W, L1_xcond_normc_w, L1_xcond_cq_W, L1_xcond_ck_W, L1_xcond_cv_W, L1_xcond_co_W, L1_xcond_norm2_w, L1_xcond_mlp_W1, L1_xcond_mlp_b1, L1_xcond_mlp_W2, L1_xcond_mlp_b2, mask_BxS2_bf1, mask_SxS_bk0)
    return x

_drawn_inputs = setup_inputs


def setup_inputs(seed=0):
    import zlib

    import numpy as np

    out = dict(_drawn_inputs(seed))
    spreads = {'L0_xcond_bq': (0.0, 2.0),
     'L0_xcond_bkv': (0.0, 0.1),
     'L0_xcond_bp': (0.0, 0.1),
     'L0_xcond_bss_q': (0.0, 0.8),
     'L0_xcond_bss_kv': (0.0, 0.339),
     'L1_xcond_norm1_w': (1.0, 0.6),
     'L1_xcond_normc_w': (1.0, 0.6),
     'L1_xcond_norm2_w': (1.0, 0.6)}
    factors = {'L0_xcond_Wq': 6.356,
     'L0_xcond_Wss_q': 8.0,
     'L1_xcond_adaLN_b': 7.74,
     'L1_xcond_cq_W': 8.0,
     'L1_xcond_ck_W': 8.0,
     'L1_xcond_mlp_b1': 8.0,
     'L1_xcond_mlp_b2': 6.953}
    for name, (base, spread) in spreads.items():
        noise = np.random.default_rng([zlib.crc32(name.encode()), seed]).standard_normal(out[name].shape)
        drawn = base * np.exp(spread * noise) if base else spread * noise
        out[name] = jnp.asarray(drawn.astype(out[name].dtype))
    for name, factor in factors.items():
        out[name] = (out[name] * factor).astype(out[name].dtype)
    return out
```

```python
from contextlib import ExitStack

import numpy as np

import concourse.bass as bass
from concourse import mybir

F32 = mybir.dt.float32
F32R = mybir.dt.float32r
BF16 = mybir.dt.bfloat16
U8 = mybir.dt.uint8
ALU = mybir.AluOpType
ACT = mybir.ActivationFunctionType
AX_X = mybir.AxisListType.X

P = 128
B = 8
S = 512
D = 512
L = 77
NH = 16
HD = D // NH
KC = D // P
TT = S // P
HG = P // HD
NG = NH // HG
GL = HG * L
FF = 4 * D
NF = FF // P
EPS = 1e-5
SCALE = float(HD) ** -0.5
BIG = float(np.finfo(np.float32).max)
BIG16 = 3.3895313892515355e38
LAG = 3
PR = 8


class Count:

    def __init__(self, nc, ctx, name, per, unit=1, base=None):
        self.sem = ctx.enter_context(nc.semaphore(name))
        self.per, self.unit, self.base = per, unit, per if base is None else base

    @property
    def credit(self):
        return self.base * self.unit

    def at(self, b, k):
        return (b * self.per + (self.base + k)) * self.unit


PASSED = {}


def wait_apart(eng, sem, value):
    eng.wait_ge(sem, value)
    eng.sem_inc(PASSED[eng.engine], 1)


def one(ap3):
    return ap3.rearrange("o p d -> (o p) d")


def row(x, b):
    return one(x[bass.ds(b, 1)]).rearrange("(t p) d -> p t d", p=P)


def split_matmul(pe, out, lhs, rhs):
    terms = [(a, c) for (ah, al), (ch, cl) in zip(lhs, rhs) for a, c in ((ah, ch), (ah, cl), (al, ch))]
    for n, (a, c) in enumerate(terms):
        last = pe.matmul(out, a, c, start=n == 0, stop=n == len(terms) - 1)
    return last


class Kernel:
    pass


def prologue(nc, k):
    with ExitStack() as ctx:
        def sb(name, shape, dt=F32):
            return ctx.enter_context(nc.sbuf_tensor("p_" + name, shape, dt))

        def ps(name):
            return ctx.enter_context(nc.psum_tensor("p_ps_" + name, [P, 512], F32))

        used = []

        def sem(name):
            used.append(ctx.enter_context(nc.semaphore("p_" + name)))
            return used[-1]

        cond = sb("cond", [B, 2, D])
        cond_t = sb("cond_t", [P, 2, KC, 32])
        bias_rows = sb("bias_rows", [P, 4, D])
        mod_rows = sb("mod_rows", [P, 4, D])
        mod_cols = sb("mod_cols", [P, 4, KC, P])
        norm_w = sb("norm_w", [P, 3, KC])
        kv_mod = sb("kv_mod", [P, 2, KC, B])
        ring = [sb(f"w{n}", [P, KC, D]) for n in range(8)]
        wkv = sb("wkv", [P, KC, 2 * D])
        ck = ring[0]
        cv = ring[1]
        ctx_raw = sb("ctx_raw", [L, B, D])
        ctx_n = ring[4]
        ctx_nn = sb("ctx_nn", [L, B, D])
        ctx_t = sb("ctx_t", [P, 2, KC, B * L])
        stats = sb("stats", [L, B, 6])
        mv = sb("mv", [L, B, 2])
        rstd = sb("rstd", [L, B])
        var_eps = sb("var_eps", [L, B])
        half_l = sb("half_l", [L, B])
        bk = sb("bk", [P, KC])
        bv_rows = sb("bv_rows", [P, D])
        keys = [sb(f"keys{n}", [P, 4 * L]) for n in range(2)]
        vals = [sb(f"vals{n}", [P, D]) for n in range(2)]
        acc = [ps(f"acc{n}") for n in range(4)]
        tp = [ps(f"tp{n}") for n in range(4)]

        NB = 13
        cond_in, cond_silu, small_in, zeroed, ident_z = (sem(x) for x in ("cond_in", "cond_silu", "small_in", "zeroed", "ident_z"))
        bias_in, ctx_in, wkv_in, ck_in, cv_in = (sem(x) for x in ("bias_in", "ctx_in", "wkv_in", "ck_in", "cv_in"))
        w_in = [sem(f"w_in{n}") for n in range(8)]
        cond_tp, cond_td, rows_mm, rows_done, cols_tp, cols_done = (
            sem(x) for x in ("cond_tp", "cond_td", "rows_mm", "rows_done", "cols_tp", "cols_done"))
        mods, st_done, mv_done, ve_done, rstd_done, ctx_normed = (
            sem(x) for x in ("mods", "st_done", "mv_done", "ve_done", "rstd_done", "ctx_normed"))
        ctx_tp, ctx_raw_done, ctx_a, ctx_td = (sem(x) for x in ("ctx_tp", "ctx_raw_done", "ctx_a", "ctx_td"))
        k_mm, k_evac, v_mm, v_evac, gates_out = (sem(x) for x in ("k_mm", "k_evac", "v_mm", "v_evac", "gates_out"))
        k_out = [sem(f"k_out{n}") for n in range(2)]
        v_out = [sem(f"v_out{n}") for n in range(2)]

        blocks = []
        for w, bias, n, src in (("L0_xcond_Wss_q", "L0_xcond_bss_q", 2, 0), ("L0_xcond_Wss_kv", "L0_xcond_bss_kv", 2, 0),
                                ("L1_xcond_adaLN_W", "L1_xcond_adaLN_b", 9, 1)):
            blocks += [(k.ins[w], k.ins[bias], j * D, src) for j in range(n)]
        vtiles = [(t * P, min(P, B * L - t * P)) for t in range(-(-B * L // P))]
        engines = ExitStack()
        block = engines.enter_context(nc.Block())

        @block.sync
        def _(sp):
            sp.dma_start(cond[:, 1, :], k.ins["cond_1024"]).then_inc(cond_in, 16)
            for n in range(8):
                w, _, c0, _ = blocks[n]
                sp.dma_start(ring[n][:, :, :], w[:, c0:c0 + D].rearrange("(k p) n -> p k n", p=P)).then_inc(w_in[n], 16)
                if n == 3:
                    sp.dma_start(ctx_raw[:, :, :], k.ins["ctx_1024"].rearrange("b s d -> s b d")).then_inc(ctx_in, 16)
            sp.wait_ge(zeroed, 1)
            for n, (_, bias, c0, _) in enumerate(blocks):
                src = bias[c0:c0 + D].partition_broadcast(B)
                sp.dma_start(bias_rows[32 * (n % 4):32 * (n % 4) + B, n // 4, :], src).then_inc(bias_in, 16)
            for n, w in enumerate(("L1_xcond_norm1_w", "L1_xcond_normc_w", "L1_xcond_norm2_w")):
                sp.dma_start(norm_w[:, n, :], k.ins[w].rearrange("(c p) -> p c", p=P), allow_slow_non_contiguous=True).then_inc(small_in, 16)
            sp.dma_start(bk[:, :], k.ins["L0_xcond_bkv"][0:D].rearrange("(c p) -> p c", p=P), allow_slow_non_contiguous=True).then_inc(small_in, 16)
            sp.dma_start(bv_rows[:, :], k.ins["L0_xcond_bkv"][D:2 * D].partition_broadcast(P)).then_inc(small_in, 16)
            sp.dma_start(wkv[:, :, :], k.ins["L0_xcond_Wkv"].rearrange("(k p) n -> p k n", p=P)).then_inc(wkv_in, 16)
            for n in range(8, NB):
                sp.wait_ge(rows_mm, n // 4 - 1)
                w, _, c0, _ = blocks[n]
                sp.dma_start(ring[n % 8][:, :, :], w[:, c0:c0 + D].rearrange("(k p) n -> p k n", p=P)).then_inc(w_in[n % 8], 16)
            for n, g in enumerate((6, 9, 12)):
                sp.wait_ge(rows_done, g // 4 + 1)
                sp.dma_start(k.gates[n], mod_rows[32 * (g % 4):32 * (g % 4) + B, g // 4, :]).then_inc(gates_out, 16)
            sp.wait_ge(rows_mm, 4)
            sp.dma_start(ck[:, :, :], k.ins["L1_xcond_ck_W"].rearrange("(k p) n -> p k n", p=P)).then_inc(ck_in, 16)
            sp.dma_start(cv[:, :, :], k.ins["L1_xcond_cv_W"].rearrange("(k p) n -> p k n", p=P)).then_inc(cv_in, 16)
            n = 0
            for layer in range(2):
                for m in range(KC):
                    for half in range(2):
                        sp.wait_ge(k_evac, n + 1)
                        sp.dma_start(k.keys[layer][4 * half:4 * half + 4, m].rearrange("b p t -> p b t"),
                                     keys[n % 2][:, :].rearrange("p (b t) -> p b t", b=4)).then_inc(k_out[n % 2], 16)
                        n += 1
                for t, (t0, tn) in enumerate(vtiles):
                    n2 = layer * len(vtiles) + t
                    sp.wait_ge(v_evac, n2 + 1)
                    sp.dma_start(k.vals[layer][t0:t0 + tn, :], vals[n2 % 2][0:tn, :]).then_inc(v_out[n2 % 2], 16)
            sp.wait_ge(gates_out, 48)
            for s in k_out:
                sp.wait_ge(s, 16 * 8)
            for s in v_out:
                sp.wait_ge(s, 16 * len(vtiles))

        @block.gpsimd
        def _(pool):
            pool.memset(k.ident[:, :], 0.0).then_inc(ident_z, 1)
            pool.memset(bias_rows[:, :, :], 0.0).then_inc(zeroed, 1)
            pool.wait_ge(ident_z, 1)
            pool.affine_select(out=k.ident[:, :], in_=k.ident[:, :], compare_op=ALU.not_equal, fill=1.0, base=0,
                               pattern=[[-1, P]], channel_multiplier=1).then_inc(ident_z, 1)
            pool.memset(cond_t[:, :, :, :], 0.0).then_inc(zeroed, 1)
            pool.memset(mod_rows[:, 3, :], 0.0).then_inc(zeroed, 1)
            pool.memset(k.neg_half[:, :], -0.5)
            pool.memset(half_l[:, :], -0.5).then_inc(zeroed, 1)
            pool.wait_ge(zeroed, 4)
            pool.wait_ge(mv_done, B)
            pool.tensor_scalar(var_eps[:, :], mv[:, :, 1], EPS, None, ALU.add).then_inc(ve_done, 1)
            pool.wait_ge(ve_done, 1)
            pool.tensor_tensor(rstd[:, :], var_eps[:, :], half_l[:, :], ALU.pow).then_inc(rstd_done, 1)

        @block.scalar
        def _(act):
            act.wait_ge(cond_in, 16)
            act.activation(cond[:, 0, :], cond[:, 1, :], ACT.Silu).then_inc(cond_silu, 1)
            for n in range(8):
                act.wait_ge(ctx_tp, n + 1)
                act.copy(ctx_t[:, 0, n // 2, 4 * L * (n % 2):4 * L * (n % 2) + 4 * L], tp[n % 4][:, 0:4 * L]).then_inc(ctx_raw_done, 1)
            act.wait_ge(small_in, 16 * 5)
            for n in range(16):
                layer, m = n // 8, n % 8 // 2
                act.wait_ge(k_mm, n + 1)
                if n >= 2:
                    act.wait_ge(k_out[n % 2], 16 * (n // 2))
                if layer == 0:
                    act.activation(keys[n % 2][:, :], acc[n % 2][:, 0:4 * L], ACT.Identity, bias=bk[:, m:m + 1]).then_inc(k_evac, 1)
                else:
                    act.copy(keys[n % 2][:, :], acc[n % 2][:, 0:4 * L]).then_inc(k_evac, 1)

        @block.vector
        def _(dve):
            dve.wait_ge(cond_tp, 1)
            dve.wait_ge(zeroed, 2)
            dve.tensor_copy(cond_t[:, :, :, 0:B], tp[0][:, 0:2 * KC * B].rearrange("p (s c b) -> p s c b", s=2, c=KC)).then_inc(cond_td, 1)
            dve.wait_ge(ctx_in, 16)
            for b in range(B):
                dve.bn_stats(stats[:, b, :], ctx_raw[:, b, :]).then_inc(st_done, 1)
            for b in range(B):
                dve.wait_ge(st_done, b + 1)
                dve.bn_aggr(mv[:, b, :], stats[:, b, :]).then_inc(mv_done, 1)
            dve.wait_ge(rstd_done, 1)
            for b in range(B):
                dve.tensor_scalar(ctx_nn[:, b, :], ctx_raw[:, b, :], mv[:, b, 0:1], rstd[:, b:b + 1],
                                  ALU.subtract, ALU.mult).then_inc(ctx_normed, 1)
            dve.wait_ge(bias_in, 16 * NB)
            dve.wait_ge(zeroed, 3)
            for q in range(4):
                np_ = P if q < 3 else 32
                dve.wait_ge(rows_mm, q + 1)
                dve.tensor_tensor(mod_rows[0:np_, q, :], acc[q][0:np_, :], bias_rows[0:np_, q, :], ALU.add).then_inc(rows_done, 1)
            for q in range(4):
                dve.wait_ge(cols_tp, q + 1)
                dve.tensor_copy(mod_cols[:, q, :, 0:P if q < 3 else 32],
                                tp[q][:, :].rearrange("p (c n) -> p c n", c=KC)[:, :, 0:P if q < 3 else 32]).then_inc(cols_done, 1)
            dve.wait_ge(cols_done, 4)
            dve.wait_ge(small_in, 16 * 5)

            def vec(n):
                return mod_cols[:, n // 4, :, 32 * (n % 4):32 * (n % 4) + B]

            for dst, sc, sh in ((k.mod[0], 0, 1), (kv_mod, 2, 3)):
                dve.tensor_scalar(dst[:, 0, :, :], vec(sc), 1.0, None, ALU.add).then_inc(mods, 1)
                dve.tensor_copy(dst[:, 1, :, :], vec(sh)).then_inc(mods, 1)
            for n, (sc, sh) in enumerate(((5, 4), (8, 7), (11, 10))):
                dve.scalar_tensor_tensor(k.mod[1 + n][:, 0, :, :], vec(sc), 1.0, norm_w[:, n, :].unsqueeze(2).broadcast_to([P, KC, B]),
                                         ALU.add, ALU.mult).then_inc(mods, 1)
                dve.tensor_copy(k.mod[1 + n][:, 1, :, :], vec(sh)).then_inc(mods, 1)
            dve.wait_ge(mods, 4)
            for n in range(8, 16):
                c, half = (n - 8) // 2, n % 2
                out = ctx_t[:, 1, c, 4 * L * half:4 * L * half + 4 * L].rearrange("p (b t) -> p b t", b=4)
                bs = slice(4 * half, 4 * half + 4)
                dve.wait_ge(ctx_tp, n + 1)
                dve.tensor_tensor(out, tp[n % 4][:, 0:4 * L].rearrange("p (b t) -> p b t", b=4),
                                  kv_mod[:, 0, c, bs].unsqueeze(2).broadcast_to([P, 4, L]), ALU.mult).then_inc(ctx_a, 1)
                dve.wait_ge(ctx_a, n - 7)
                dve.tensor_tensor(out, out, kv_mod[:, 1, c, bs].unsqueeze(2).broadcast_to([P, 4, L]), ALU.add).then_inc(ctx_td, 1)
            for n in range(2 * len(vtiles)):
                tn = vtiles[n % len(vtiles)][1]
                dve.wait_ge(v_mm, n + 1)
                if n >= 2:
                    dve.wait_ge(v_out[n % 2], 16 * (n // 2))
                if n < len(vtiles):
                    dve.tensor_tensor(vals[n % 2][0:tn, :], acc[2 + n % 2][0:tn, :], bv_rows[0:tn, :], ALU.add).then_inc(v_evac, 1)
                else:
                    dve.tensor_copy(vals[n % 2][0:tn, :], acc[2 + n % 2][0:tn, :]).then_inc(v_evac, 1)

        @block.tensor
        def _(pe):
            pe.wait_ge(ident_z, 2)
            pe.wait_ge(cond_silu, 1)
            for s in range(2):
                for c in range(KC):
                    last = pe.transpose(tp[0][:, (s * KC + c) * B:(s * KC + c + 1) * B], cond[:, s, c * P:(c + 1) * P], k.ident[0:B, 0:B])
            last.then_inc(cond_tp, 1)
            pe.wait_ge(cond_td, 1)
            for q in range(4):
                mine = [n for n in range(4 * q, min(4 * q + 4, NB))]
                for n in mine:
                    pe.wait_ge(w_in[n % 8], 16 * (n // 8 + 1))
                for c in range(KC):
                    for n in mine:
                        r = 32 * (n % 4)
                        last = pe.matmul(acc[q][r:r + 32, :], cond_t[:, blocks[n][3], c, :], ring[n % 8][:, c, :],
                                         start=c == 0, stop=c == KC - 1)
                last.then_inc(rows_mm, 1)
            for q in range(4):
                n = P if q < 3 else 32
                pe.wait_ge(rows_done, q + 1)
                for c in range(KC):
                    last = pe.transpose(tp[q][:, c * P:c * P + n], mod_rows[0:n, q, c * P:(c + 1) * P], k.ident[0:n, 0:n])
                last.then_inc(cols_tp, 1)
            for n in range(16):
                src = ctx_raw if n < 8 else ctx_nn
                c, half = n % 8 // 2, n % 2
                if n == 0:
                    pe.wait_ge(ctx_in, 16)
                    pe.wait_ge(cols_done, 4)
                if n == 8:
                    pe.wait_ge(ctx_normed, B)
                if 4 <= n < 12:
                    pe.wait_ge(ctx_raw_done, n - 3)
                if n >= 12:
                    pe.wait_ge(ctx_a, n - 11)
                for j in range(4):
                    last = pe.transpose(tp[n % 4][:, j * L:(j + 1) * L], src[:, 4 * half + j, c * P:(c + 1) * P], k.ident[0:L, 0:L])
                last.then_inc(ctx_tp, 1)
            pe.wait_ge(wkv_in, 16)
            pe.wait_ge(ctx_td, 8)
            pe.wait_ge(rows_done, 4)
            for layer in range(2):
                if layer:
                    pe.wait_ge(ck_in, 16)
                    pe.wait_ge(cv_in, 16)
                wk = wkv if layer == 0 else ck
                for i in range(8):
                    n, m, half = layer * 8 + i, i // 2, i % 2
                    if n >= 2:
                        pe.wait_ge(k_evac, n - 1)
                    for c in range(KC):
                        last = pe.matmul(acc[n % 2][:, 0:4 * L], wk[:, c, m * P:(m + 1) * P],
                                         ctx_t[:, 1 - layer, c, 4 * L * half:4 * L * half + 4 * L], start=c == 0, stop=c == KC - 1)
                    last.then_inc(k_mm, 1)
                for t, (t0, tn) in enumerate(vtiles):
                    n = layer * len(vtiles) + t
                    if n >= 2:
                        pe.wait_ge(v_evac, n - 1)
                    for c in range(KC):
                        w = wkv[:, c, D:2 * D] if layer == 0 else cv[:, c, :]
                        last = pe.matmul(acc[2 + n % 2][0:tn, :], ctx_t[:, 1 - layer, c, t0:t0 + tn], w, start=c == 0, stop=c == KC - 1)
                    last.then_inc(v_mm, 1)

        engines.close()
        with nc.Block() as tidy:
            @tidy.sync
            def _(sp):
                for s in used:
                    sp.sem_clear(s)


class Norm:

    def __init__(self, nc, ctx, tag):
        def count(name, per, unit=1):
            return Count(nc, ctx, f"{tag}_{name}", per, unit)
        self.x_in = count("x_in", 1, 16)
        self.stats_done = count("stats_done", TT)
        self.mean_var = count("mean_var", TT)
        self.var_eps_done = count("var_eps_done", 1)
        self.rstd_done = count("rstd_done", 1)
        self.normed = count("normed", TT)
        self.mod_done = count("mod_done", 1)
        self.high = count("high", KC)
        self.low = count("low", KC)


def norm_stats(dve, nm, bf, n):
    dve.wait_ge(nm.x_in.sem, nm.x_in.at(n, 1))
    for t in range(TT):
        dve.bn_stats(bf["stats"][:, t, :], bf["x"][:, t, :]).then_inc(nm.stats_done.sem, 1)
    for t in range(TT):
        wait_apart(dve, nm.stats_done.sem, nm.stats_done.at(n, t + 1))
        dve.bn_aggr(bf["mv"][:, t, :], bf["stats"][:, t, :]).then_inc(nm.mean_var.sem, 1)


def norm_rstd(pool, nm, bf, n, neg_half):
    wait_apart(pool, nm.mean_var.sem, nm.mean_var.at(n, TT))
    pool.tensor_scalar(bf["var_eps"][:, :], bf["mv"][:, :, 1], EPS, None, ALU.add).then_inc(nm.var_eps_done.sem, 1)
    pool.wait_ge(nm.var_eps_done.sem, nm.var_eps_done.at(n, 1))
    pool.tensor_tensor(bf["rstd"][:, :], bf["var_eps"][:, :], neg_half[:, :], ALU.pow).then_inc(nm.rstd_done.sem, 1)


def norm_apply(dve, nm, bf, n):
    dve.wait_ge(nm.rstd_done.sem, nm.rstd_done.at(n, 1))
    for t in range(TT):
        dve.tensor_scalar(bf["x"][:, t, :], bf["x"][:, t, :], bf["mv"][:, t, 0:1], bf["rstd"][:, t:t + 1],
                          ALU.subtract, ALU.mult).then_inc(nm.normed.sem, 1)


def norm_buffers(sb):
    return {"x": sb("x", [P, TT, D]), "stats": sb("stats", [P, TT, 6]), "mv": sb("mv", [P, TT, 2]),
            "rstd": sb("rstd", [P, TT]), "var_eps": sb("var_eps", [P, TT]), "mod": sb("mod", [P, 2, KC, 1])}


def mod_copy(dve, nm, bf, mod, b, n, used, used_at):
    dve.wait_ge(used.sem, used_at)
    dve.tensor_copy(bf["mod"][:, :, :, :], mod[:, :, :, bass.ds(b, 1)]).then_inc(nm.mod_done.sem, 1)


def split(dve, nm, n, c, full, high, low):
    dve.tensor_copy(high, full).then_inc(nm.high.sem, 1)
    dve.wait_ge(nm.high.sem, nm.high.at(n, c + 1))
    dve.tensor_tensor(low, full, high.bitcast(F32), ALU.subtract).then_inc(nm.low.sem, 1)


class Weights:

    def __init__(self, nc, ctx, tag, stage):
        self.stage = stage
        self.chunk_in = [ctx.enter_context(nc.semaphore(f"{tag}_w_in{n}")) for n in range(4)]
        self.scaled = ctx.enter_context(nc.semaphore(f"{tag}_w_scaled"))
        self.high_done = ctx.enter_context(nc.semaphore(f"{tag}_w_high"))
        self.low_done = ctx.enter_context(nc.semaphore(f"{tag}_w_low"))

    def load(self, sp, chunks):
        for n, (src, _, _, _) in enumerate(chunks):
            if n >= 4:
                sp.wait_ge(self.low_done, n - 3)
            sp.dma_start(self.stage[:, n % 4, :], src).then_inc(self.chunk_in[n % 4], 16)

    def high(self, act, chunks):
        for n, (_, high, _, scale) in enumerate(chunks):
            act.wait_ge(self.chunk_in[n % 4], 16 * (n // 4 + 1))
            if scale != 1.0:
                act.mul(self.stage[:, n % 4, :], self.stage[:, n % 4, :], scale).then_inc(self.scaled, 1)
                act.wait_ge(self.scaled, 1 + sum(c[3] != 1.0 for c in chunks[:n]))
            act.copy(high, self.stage[:, n % 4, :]).then_inc(self.high_done, 1)

    def low(self, dve, chunks):
        for n, (_, high, low, _) in enumerate(chunks):
            dve.wait_ge(self.high_done, n + 1)
            dve.tensor_tensor(low, self.stage[:, n % 4, :], high.bitcast(F32), ALU.subtract).then_inc(self.low_done, 1)


def weight_chunks(w, cols, high, low, scale=1.0):
    return [(w[c * P:(c + 1) * P, cols], high[:, c, :], low[:, c, :], scale) for c in range(KC)]


class CrossCounts:
    def __init__(self, nc, ctx):
        def count(name, per, unit=1):
            return Count(nc, ctx, f"x_{name}", per, unit)
        self.norm = Norm(nc, ctx, "x")
        self.keys_in = count("keys_in", HG, 16)
        self.vals_in = count("vals_in", 1, 16)
        self.gate_in = count("gate_in", 1, 16)
        self.res_in = count("res_in", 1, 16)
        self.dense_mm = count("dense_mm", 8)
        self.dense_out = count("dense_out", 8)
        self.scored = count("scored", 16)
        self.masked = count("masked", 16)
        self.row_max = count("row_max", 16)
        self.shifted = count("shifted", 16)
        self.exped = count("exped", 16)
        self.summed = count("summed", 16)
        self.inverted = count("inverted", 16)
        self.probs = count("probs", 16)
        self.turned = count("turned", 16)
        self.turned_out = count("turned_out", 16)
        self.attended = count("attended", NG)
        self.att_high = count("att_high", NG)
        self.att_low = count("att_low", NG)
        self.projected = count("projected", TT)
        self.gated = count("gated", TT)
        self.added = count("added", TT)
        self.stored = Count(nc, ctx, "x_stored", 1, 16, base=0)


def cross_phase(nc, k, c, layer, src, dst):
    with ExitStack() as ctx:
        def sb(name, shape, dt=F32):
            return ctx.enter_context(nc.sbuf_tensor(f"x{layer}_" + name, shape, dt))

        def ps(name):
            return ctx.enter_context(nc.psum_tensor(f"x{layer}_ps_" + name, [P, 512], F32))

        off = layer * B
        nm = c.norm
        if layer == 0:
            wq, wo, mod, gate_op = "L0_xcond_Wq", "L0_xcond_Wp", k.mod[0], ALU.add
        else:
            wq, wo, mod, gate_op = "L1_xcond_cq_W", "L1_xcond_co_W", k.mod[2], ALU.mult
        bf = norm_buffers(sb)
        wqh, wql = sb("wqh", [P, KC, D], F32R), sb("wql", [P, KC, D], F32R)
        woh, wol = sb("woh", [P, KC, D], F32R), sb("wol", [P, KC, D], F32R)
        full = sb("full", [P, 2, S])
        xh, xl = sb("xh", [P, KC, S], F32R), sb("xl", [P, KC, S], F32R)
        queries = sb("queries", [P, NG, S])
        keys = sb("keys", [P, NG, GL])
        vals = sb("vals", [L, D])
        scores = sb("scores", [P, 2, GL])
        mx, sums, inv = sb("mx", [P, 2, HG]), sb("sums", [P, 4, HG]), sb("inv", [P, 4, HG])
        probs = sb("probs", [P, 8, GL])
        probs_t = sb("probs_t", [L, HG, S])
        ah, al = sb("ah", [P, NG, S], F32R), sb("al", [P, NG, S], F32R)
        gate = sb("gate", [P, D])
        gated = sb("gated", [P, 2, D])
        res = sb("res", [P, TT, D])
        bq = sb("bq", [P, KC])
        mask = sb("mask", [P, L])
        if layer == 1:
            mask_u8, ctx_mask = sb("mask_u8", [P, B * L], U8), sb("ctx_mask", [P, B * L])
        dense, score_ps, turn_ps = [ps(f"dense{n}") for n in range(2)], [ps(f"score{n}") for n in range(2)], [ps(f"turn{n}") for n in range(2)]
        att_ps, out_ps = ps("att"), ps("out")
        wt = Weights(nc, ctx, f"x{layer}", res)
        bq_in, keys_zeroed, mask_done = (ctx.enter_context(nc.semaphore(f"x{layer}_{x}")) for x in ("bq_in", "keys_zeroed", "mask_done"))
        mask_in = bq_in
        chunks = weight_chunks(k.ins[wq], slice(0, D), wqh, wql) + weight_chunks(k.ins[wo], slice(0, D), woh, wol)

        def heads4(ap):
            return ap.rearrange("p (h t) -> p h t", h=HG)

        def per_head(ap):
            return ap.unsqueeze(2).broadcast_to([P, HG, L])

        block = ctx.enter_context(nc.Block())

        def run(norm, query, attend, finish):
            def entry(b, before, after):
                attend(b, 0, None)
                if before:
                    attend(b - 1, None, NG - 1)
                if after:
                    norm(b + 1)
                if before:
                    finish(b - 1)
                for g in range(1, NG):
                    attend(b, g, None)
                    attend(b, None, g - 1)
                    if after:
                        query(b + 1, g - 1)
                if after:
                    query(b + 1, NG - 1)
            return entry

        def schedule(eng, norm, query, attend, finish):
            entry = run(norm, query, attend, finish)
            norm(0)
            for m in range(NG):
                query(0, m)
            entry(0, False, True)
            with eng.Fori(1, B - 1) as b:
                entry(b, True, True)
            entry(B - 1, True, False)
            attend(B - 1, None, NG - 1)
            finish(B - 1)

        @block.sync
        def _(sp):
            if layer == 0:
                sp.sem_inc(nm.x_in.sem, nm.x_in.credit)
                for q in (c.keys_in, c.vals_in, c.gate_in, c.res_in):
                    sp.sem_inc(q.sem, q.credit)

            def load_x(b):
                wait_apart(sp, c.dense_out.sem, c.dense_out.at(b + off, KC - 8))
                sp.dma_start(bf["x"][:, :, :], row(src, b)).then_inc(nm.x_in.sem, 16)

            def load_keys(b):
                wait_apart(sp, c.scored.sem, c.scored.at(b + off, 0))
                for r in range(HG):
                    rows = slice(HD * r, HD * r + HD)
                    sp.dma_start(keys[rows, :, r * L:(r + 1) * L],
                                 k.keys[layer][bass.ds(b, 1)].rearrange("o g p t -> (o p) g t")[rows]
                                 ).then_inc(c.keys_in.sem, 16)

            def load_vals(b):
                wait_apart(sp, c.attended.sem, c.attended.at(b + off, 0))
                sp.dma_start(vals[:, :], k.vals[layer][bass.ds(b * L, L), :]).then_inc(c.vals_in.sem, 16)

            def load_res(b, first=False):
                if layer == 1:
                    wait_apart(sp, c.gated.sem, c.gated.at(b + off, 0))
                    sp.dma_start(gate[:, :], k.gates[1][bass.ds(b, 1), :].rearrange("o n -> (o n)").partition_broadcast(P)).then_inc(c.gate_in.sem, 16)
                if not (layer == 0 and first):
                    wait_apart(sp, c.stored.sem, c.stored.at(b + off, 0))
                sp.dma_start(res[:, :, :], row(src, b)).then_inc(c.res_in.sem, 16)

            load_x(0)
            wt.load(sp, chunks)
            if layer == 0:
                sp.dma_start(bq[:, :], k.ins["L0_xcond_bq"].rearrange("(c p) -> p c", p=P), allow_slow_non_contiguous=True).then_inc(bq_in, 16)
                sp.dma_start(gate[:, :], k.ins["L0_xcond_bp"].partition_broadcast(P)).then_inc(c.gate_in.sem, 16)
            else:
                sp.dma_start(mask_u8[:, :], k.ins["mask_BxS2_bf1"].rearrange("b s -> (b s)").partition_broadcast(P)).then_inc(mask_in, 16)
            sp.wait_ge(keys_zeroed, 1)
            load_keys(0)
            load_vals(0)
            load_x(1)
            sp.wait_ge(wt.low_done, len(chunks))
            load_res(0, first=True)
            load_keys(1)
            load_vals(1)
            with sp.Fori(2, B) as b:
                load_x(b)
                load_res(b - 1)
                load_keys(b)
                load_vals(b)
            load_res(B - 1)

        @block.gpsimd
        def _(pool):
            pool.memset(keys[:, :, :], 0.0).then_inc(keys_zeroed, 1)
            if layer == 0:
                for q in (nm.var_eps_done, nm.rstd_done, c.probs, c.added):
                    pool.sem_inc(q.sem, q.credit)

            def norm(b):
                norm_rstd(pool, nm, bf, b + off, k.neg_half)

            def attend(b, g, gv):
                if g is None:
                    return
                for n in range(4 * g, 4 * g + 4):
                    slot = probs[:, g % 2 * 4 + n % 4, :]
                    pool.wait_ge(c.inverted.sem, c.inverted.at(b + off, n + 1))
                    pool.tensor_tensor(heads4(slot), heads4(slot), per_head(inv[:, n % 4, :]), ALU.mult).then_inc(c.probs.sem, 1)

            def finish(b):
                pool.wait_ge(c.res_in.sem, c.res_in.at(b + off, 1))
                for t in range(TT):
                    pool.wait_ge(c.gated.sem, c.gated.at(b + off, t + 1))
                    pool.tensor_tensor(res[:, t, :], res[:, t, :], gated[:, t % 2, :], ALU.add).then_inc(c.added.sem, 1)
                pool.wait_ge(c.added.sem, c.added.at(b + off, TT))
                pool.dma_start(row(dst, b), res[:, :, :]).then_inc(c.stored.sem, 16)

            schedule(pool, norm, lambda b, m: None, attend, finish)
            pool.wait_ge(c.stored.sem, c.stored.at(B - 1 + off, 1))

        @block.scalar
        def _(act):
            if layer == 0:
                for q in (c.dense_out, c.exped, c.turned_out, c.att_high):
                    act.sem_inc(q.sem, q.credit)
            wt.high(act, chunks)
            if layer == 0:
                act.wait_ge(bq_in, 16)

            def norm(b):
                n = b + off
                act.wait_ge(nm.mod_done.sem, nm.mod_done.at(n, 1))
                for ch in range(KC):
                    act.wait_ge(c.dense_mm.sem, c.dense_mm.at(n, ch + 1))
                    act.wait_ge(nm.low.sem, nm.low.at(n, ch - 1))
                    act.activation(full[:, ch % 2, :], dense[ch % 2][:, :], ACT.Identity, bias=bf["mod"][:, 1, ch, :],
                                   scale=bf["mod"][:, 0, ch, :]).then_inc(c.dense_out.sem, 1)

            def query(b, m):
                n = b + off
                act.wait_ge(c.dense_mm.sem, c.dense_mm.at(n, 5 + m))
                act.wait_ge(c.scored.sem, c.scored.at(n, 4 * m + 4 - 16))
                if layer == 0:
                    act.activation(queries[:, m, :], dense[m % 2][:, :], ACT.Identity, bias=bq[:, m:m + 1]).then_inc(c.dense_out.sem, 1)
                else:
                    act.copy(queries[:, m, :], dense[m % 2][:, :]).then_inc(c.dense_out.sem, 1)

            def attend(b, g, gv):
                n0 = b + off
                if g is not None:
                    act.wait_ge(c.turned.sem, c.turned.at(n0, 4 * (g - 1)))
                    for n in range(4 * g, 4 * g + 4):
                        act.wait_ge(c.shifted.sem, c.shifted.at(n0, n + 1))
                        act.activation(probs[:, g % 2 * 4 + n % 4, :], scores[:, n % 2, :], ACT.Exp, scale=SCALE).then_inc(c.exped.sem, 1)
                else:
                    act.wait_ge(c.attended.sem, c.attended.at(n0, gv))
                    for r in range(HG):
                        h = HG * gv + r
                        act.wait_ge(c.turned.sem, c.turned.at(n0, h + 1))
                        act.copy(probs_t[:, r, :], turn_ps[h % 2][0:L, :]).then_inc(c.turned_out.sem, 1)
                    act.wait_ge(c.attended.sem, c.attended.at(n0, gv + 1))
                    act.wait_ge(c.projected.sem, c.projected.at(n0, 0))
                    act.copy(ah[:, gv, :], att_ps[:, :]).then_inc(c.att_high.sem, 1)

            schedule(act, norm, query, attend, lambda b: None)

        @block.vector
        def _(dve):
            if layer == 0:
                for q in (nm.stats_done, nm.mean_var, nm.normed, nm.mod_done, nm.high, nm.low, c.row_max, c.shifted, c.summed,
                          c.inverted, c.att_low, c.gated):
                    dve.sem_inc(q.sem, q.credit)
            else:
                dve.sem_inc(c.masked.sem, c.masked.credit)
            wt.low(dve, chunks)
            if layer == 1:
                dve.wait_ge(mask_in, 16)
                dve.tensor_scalar(ctx_mask[:, :], mask_u8[:, :], BIG, -BIG, ALU.mult, ALU.add).then_inc(mask_done, 1)
                dve.wait_ge(mask_done, 1)

            def norm(b):
                n = b + off
                norm_stats(dve, nm, bf, n)
                mod_copy(dve, nm, bf, mod, b, n, c.dense_out, c.dense_out.at(n, KC - 8))
                norm_apply(dve, nm, bf, n)
                dve.wait_ge(c.dense_mm.sem, c.dense_mm.at(n, 0))
                for ch in range(KC):
                    dve.wait_ge(c.dense_out.sem, c.dense_out.at(n, ch + 1))
                    split(dve, nm, n, ch, full[:, ch % 2, :], xh[:, ch, :], xl[:, ch, :])

            def shift(b, n):
                n0 = b + off
                raw, out = heads4(score_ps[n % 2][:, 0:GL]), heads4(scores[:, n % 2, :])
                dve.wait_ge(c.scored.sem, c.scored.at(n0, n + 1))
                dve.wait_ge(c.exped.sem, c.exped.at(n0, n - 1))
                if layer == 1:
                    dve.tensor_tensor(out, raw, mask[:, :].unsqueeze(1).broadcast_to([P, HG, L]), ALU.add).then_inc(c.masked.sem, 1)
                    dve.wait_ge(c.masked.sem, c.masked.at(b, n + 1))
                    raw = out
                dve.tensor_reduce(mx[:, n % 2, :], raw, AX_X, ALU.max).then_inc(c.row_max.sem, 1)
                dve.wait_ge(c.row_max.sem, c.row_max.at(n0, n + 1))
                dve.tensor_tensor(out, raw, per_head(mx[:, n % 2, :]), ALU.subtract).then_inc(c.shifted.sem, 1)

            def invert(b, n):
                n0 = b + off
                dve.wait_ge(c.exped.sem, c.exped.at(n0, n + 1))
                dve.tensor_reduce(sums[:, n % 4, :], heads4(probs[:, n // 4 % 2 * 4 + n % 4, :]), AX_X, ALU.add).then_inc(c.summed.sem, 1)
                dve.wait_ge(c.summed.sem, c.summed.at(n0, n + 1))
                dve.wait_ge(c.probs.sem, c.probs.at(n0, n - 3))
                dve.reciprocal(inv[:, n % 4, :], sums[:, n % 4, :]).then_inc(c.inverted.sem, 1)

            def attend(b, g, gv):
                n0 = b + off
                if g is not None:
                    if g == 0 and layer == 1:
                        dve.wait_ge(c.masked.sem, c.masked.at(b, 0))
                        dve.tensor_copy(mask[:, :], ctx_mask[:, bass.ds(b * L, L)]).then_inc(mask_done, 1)
                        dve.wait_ge(mask_done, b + 2)
                    for n in range(4 * g, 4 * g + 4):
                        shift(b, n)
                        if n > 4 * g:
                            invert(b, n - 1)
                    invert(b, 4 * g + 3)
                else:
                    dve.wait_ge(c.att_high.sem, c.att_high.at(n0, gv + 1))
                    dve.tensor_tensor(al[:, gv, :], att_ps[:, :], ah[:, gv, :].bitcast(F32), ALU.subtract).then_inc(c.att_low.sem, 1)

            def finish(b):
                n0 = b + off
                if layer == 0:
                    dve.wait_ge(c.gate_in.sem, c.gate_in.at(0, 1))
                else:
                    dve.wait_ge(c.gate_in.sem, c.gate_in.at(b + 1, 1))
                for t in range(TT):
                    dve.wait_ge(c.projected.sem, c.projected.at(n0, t + 1))
                    dve.wait_ge(c.added.sem, c.added.at(n0, t - 1))
                    dve.tensor_tensor(gated[:, t % 2, :], out_ps[:, :], gate[:, :], gate_op).then_inc(c.gated.sem, 1)

            schedule(dve, norm, lambda b, m: None, attend, finish)

        @block.tensor
        def _(pe):
            if layer == 0:
                for q in (c.dense_mm, c.scored, c.turned, c.attended, c.projected):
                    pe.sem_inc(q.sem, q.credit)
            pe.wait_ge(wt.low_done, len(chunks))

            def norm(b):
                n = b + off
                pe.wait_ge(nm.normed.sem, nm.normed.at(n, TT))
                for ch in range(KC):
                    pe.wait_ge(c.dense_out.sem, c.dense_out.at(n, ch - 1))
                    for t in range(TT):
                        last = pe.transpose(dense[ch % 2][:, t * P:(t + 1) * P], bf["x"][:, t, ch * P:(ch + 1) * P], k.ident[:, :])
                    last.then_inc(c.dense_mm.sem, 1)

            def query(b, m):
                n = b + off
                pe.wait_ge(nm.low.sem, nm.low.at(n, KC))
                pe.wait_ge(c.dense_out.sem, c.dense_out.at(n, 4 + m - 1))
                split_matmul(pe, dense[m % 2][:, :], [(wqh[:, ch, m * P:(m + 1) * P], wql[:, ch, m * P:(m + 1) * P]) for ch in range(KC)],
                             [(xh[:, ch, :], xl[:, ch, :]) for ch in range(KC)]).then_inc(c.dense_mm.sem, 1)

            def attend(b, g, gv):
                n0 = b + off
                if g is not None:
                    pe.wait_ge(c.dense_out.sem, c.dense_out.at(n0, 5 + g))
                    pe.wait_ge(c.keys_in.sem, c.keys_in.at(n0, HG))
                    freed, fn = (c.shifted, n0) if layer == 0 else (c.masked, b)
                    for n in range(4 * g, 4 * g + 4):
                        pe.wait_ge(freed.sem, freed.at(fn, n - 1))
                        t = n % 4
                        pe.matmul(score_ps[n % 2][:, 0:GL], queries[:, g, t * P:(t + 1) * P], keys[:, g, :],
                                  start=True, stop=True).then_inc(c.scored.sem, 1)
                else:
                    pe.wait_ge(c.probs.sem, c.probs.at(n0, 4 * gv + 4))
                    for r in range(HG):
                        h = HG * gv + r
                        pe.wait_ge(c.turned_out.sem, c.turned_out.at(n0, h - 1))
                        for t in range(TT):
                            last = pe.transpose(turn_ps[h % 2][0:L, t * P:(t + 1) * P],
                                                probs[:, gv % 2 * 4 + t, r * L:(r + 1) * L], k.ident[:, :])
                        last.then_inc(c.turned.sem, 1)
                    pe.wait_ge(c.turned_out.sem, c.turned_out.at(n0, HG * gv + HG))
                    pe.wait_ge(c.vals_in.sem, c.vals_in.at(n0, 1))
                    pe.wait_ge(c.att_low.sem, c.att_low.at(n0, gv))
                    for r in range(HG):
                        h = HG * gv + r
                        last = pe.matmul(att_ps[HD * r:HD * r + HD, :], vals[:, h * HD:(h + 1) * HD], probs_t[:, r, :],
                                         start=True, stop=True)
                    last.then_inc(c.attended.sem, 1)

            def finish(b):
                n0 = b + off
                pe.wait_ge(c.att_low.sem, c.att_low.at(n0, NG))
                for t in range(TT):
                    pe.wait_ge(c.gated.sem, c.gated.at(n0, t))
                    split_matmul(pe, out_ps[:, :], [(ah[:, ch, t * P:(t + 1) * P], al[:, ch, t * P:(t + 1) * P]) for ch in range(KC)],
                                 [(woh[:, ch, :], wol[:, ch, :]) for ch in range(KC)]).then_inc(c.projected.sem, 1)

            schedule(pe, norm, query, attend, finish)


HS = NG * 2 * HG
ROT = [(d + HD // 2) % HD for d in range(HD)]


def self_phase(nc, k, src, dst):
    with ExitStack() as ctx:
        def sb(name, shape, dt=F32):
            return ctx.enter_context(nc.sbuf_tensor("s_" + name, shape, dt))

        def ps(name):
            return ctx.enter_context(nc.psum_tensor("s_ps_" + name, [P, 512], F32))

        def count(name, per, unit=1, base=None):
            return Count(nc, ctx, "s_" + name, per, unit, base)

        mod = k.mod[1]
        nm = Norm(nc, ctx, "s")
        gate_in, res_in = count("gate_in", 1, 16), count("res_in", 1, 16)
        stored = count("stored", 1, 16, base=0)
        dense_mm = count("dense_mm", 16)
        act_dense = count("act_dense", 8)
        cos_done, shuffled = count("cos_done", 8), count("shuffled", 8)
        sin_done, roped = count("sin_done", 8), count("roped", 8)
        qk_high, qk_low = count("qk_high", 8), count("qk_low", 8)
        stack_in = [count(f"stack_in{w}", 12 * NG, 16) for w in range(2)]
        scored, masked, exped, inverted, probs_done = (count(x, 2 * HS) for x in ("scored", "masked", "exped", "inverted", "probs_done"))
        turned, turned_out = count("turned", 2 * HS), count("turned_out", 2 * HS)
        attended, att_out = count("attended", 2 * NG), count("att_out", 2 * NG)
        projected, gated_done, added = count("projected", TT), count("gated_done", TT), count("added", TT)
        mask_in, mask_done, rope_in, wo_in = (ctx.enter_context(nc.semaphore("s_" + x)) for x in ("mask_in", "mask_done", "rope_in", "wo_in"))

        bf = norm_buffers(sb)
        res = bf["x"]
        wh, wl = sb("wh", [P, KC, 3 * D], F32R), sb("wl", [P, KC, 3 * D], F32R)
        wo = sb("wo", [P, KC, D])
        full = sb("full", [P, 2, S])
        xh, xl = sb("xh", [P, KC, S], F32R), sb("xl", [P, KC, S], F32R)
        rope = sb("rope", [P, 2, S // 2])
        with_cos, swapped = sb("with_cos", [P, 2, S]), sb("swapped", [P, 2, S])
        parts = sb("parts", [P, 2, 2, S], F32R)
        stacks = [sb(f"stack{w}", [3 * HD, 2 * HG, S], F32R) for w in range(2)]
        vals = [sb(f"vals{n}", [P, TT, D]) for n in range(2)]
        mask_add = sb("mask_add", [P, TT, S], BF16)
        scores = sb("scores", [P, 2, S])
        low_score, sums, inv = sb("low_score", [P, PR]), sb("sums", [P, PR]), sb("inv", [P, PR])
        probs = sb("probs", [P, PR, S])
        probs_t = sb("probs_t", [P, HG, KC, S // 2])
        att = sb("att", [P, NG, S])
        gate, gated = sb("gate", [P, D]), sb("gated", [P, 2, D])
        mask_u8 = gated[:, 0, :].bitcast(U8).rearrange("p (t n) -> p t n", t=TT)
        dense, score_ps, turn_ps = [ps(f"dense{n}") for n in range(2)], [ps(f"score{n}") for n in range(2)], [ps(f"turn{n}") for n in range(2)]
        att_ps, out_ps = ps("att"), ps("out")
        wt = Weights(nc, ctx, "s", probs)
        w_qkv = k.ins["L1_xcond_qkv_W"]
        chunks = [(w_qkv[c * P:(c + 1) * P, j * D:(j + 1) * D], wh[:, c, j * D:(j + 1) * D], wl[:, c, j * D:(j + 1) * D],
                   -SCALE if j == 0 else 1.0) for j in range(3) for c in range(KC)]

        def schedule(eng, lag, head, tail, norm_in, norm_out, qk, value, project):
            def entry(b, par, before, after):
                for s in range(HS):
                    head(b, s)
                    if s >= lag:
                        tail(b, s - lag, par)
                    elif before:
                        tail(b - 1, s - lag + HS, 1 - par)
                    if s in (0, 1, 9, 11, 17, 19):
                        qk(b, s // 8 + 1, s // 2 % 2 if s > 1 and s != 9 and s != 17 else 0 if s != 1 else 1)
                    if before and s in (3, 4, 5):
                        for t in {3: (0, 1), 4: (2,), 5: (3,)}[s]:
                            project(b - 1, t)
                    if after and s == 16:
                        norm_in(b + 1)
                    if after and s == 20:
                        norm_out(b + 1)
                    if after and s in (25, 26):
                        qk(b + 1, 0, s - 25)
                    if after and 27 <= s <= 30:
                        value(b + 1, s - 27, 1 - par)
            norm_in(0)
            norm_out(0)
            qk(0, 0, 0)
            qk(0, 0, 1)
            for t in range(TT):
                value(0, t, 0)
            entry(0, 0, False, True)
            with eng.Fori(0, B // 2 - 1) as j:
                entry(j * 2 + 1, 1, True, True)
                entry(j * 2 + 2, 0, True, True)
            entry(B - 1, 1, True, False)
            for s in range(HS - lag, HS):
                tail(B - 1, s, 1)
            for t in range(TT):
                project(B - 1, t)

        def nothing(*_):
            pass

        def dense_slot(kind, i, w=0):
            return {"norm": i, "qk": 4 + w if i == 0 else 8 + 2 * i + w, "value": 6 + i}[kind]

        block = ctx.enter_context(nc.Block())

        @block.sync
        def _(sp):
            for q in (nm.x_in, gate_in, res_in, *stack_in):
                sp.sem_inc(q.sem, q.credit)

            def load_x(b):
                sp.dma_start(bf["x"][:, :, :], row(src, b)).then_inc(nm.x_in.sem, 16)

            def load_res(b):
                wait_apart(sp, gated_done.sem, gated_done.at(b, 0))
                sp.dma_start(gate[:, :], k.gates[0][bass.ds(b, 1), :].rearrange("o n -> (o n)").partition_broadcast(P)).then_inc(gate_in.sem, 16)
                sp.dma_start(res[:, :, :], row(src, b)).then_inc(res_in.sem, 16)

            def stack(b, g):
                for w in range(2):
                    wait_apart(sp, qk_low.sem, qk_low.at(b, 2 * g + w + 1))
                    wait_apart(sp, scored.sem, scored.at(b, 16 * (g - 1)))
                    for r in range(HG):
                        rows = slice(HD * r, HD * r + HD)
                        for n, part in enumerate(((0, 0, 1), (0, 1, 0))[w]):
                            sp.dma_start(stacks[w][HD * n:HD * n + HD, g % 2 * HG + r, :].bitcast(F32),
                                         parts[rows, w, part, :].bitcast(F32)).then_inc(stack_in[w].sem, 16)

            def entry(b, first, last):
                stack(b, 1)
                if first:
                    wait_apart(sp, act_dense.sem, act_dense.at(b, KC))
                else:
                    wait_apart(sp, stored.sem, stored.at(b - 1, 1))
                if last:
                    load_res(b)
                else:
                    load_x(b + 1)
                stack(b, 2)
                stack(b, 3)
                if not last:
                    wait_apart(sp, act_dense.sem, act_dense.at(b + 1, KC))
                    load_res(b)
                    stack(b + 1, 0)

            load_x(0)
            wt.load(sp, chunks)
            sp.dma_start(mask_u8[:, :, :], k.ins["mask_SxS_bk0"].rearrange("(t p) n -> p t n", p=P)).then_inc(mask_in, 16)
            sp.dma_start(rope[:, :, :], k.rope.rearrange("o p n -> p o n")).then_inc(rope_in, 16)
            sp.dma_start(wo[:, :, :], k.ins["L1_xcond_attn_out_W"].rearrange("(k p) n -> p k n", p=P)).then_inc(wo_in, 16)
            stack(0, 0)
            entry(0, True, False)
            with sp.Fori(1, B - 1) as b:
                entry(b, False, False)
            entry(B - 1, False, True)

        @block.gpsimd
        def _(pool):
            for q in (nm.var_eps_done, nm.rstd_done, sin_done, roped, probs_done, added):
                pool.sem_inc(q.sem, q.credit)
            pool.wait_ge(rope_in, 16)
            sin = rope[:, 1, :].unsqueeze(1).broadcast_to([P, 2, S // 2])

            def norm_in(b):
                norm_rstd(pool, nm, bf, b, k.neg_half)

            def qk(b, g, w):
                i = 2 * g + w
                sw = swapped[:, w, :].rearrange("p (a n) -> p a n", a=2)
                pool.wait_ge(shuffled.sem, shuffled.at(b, i + 1))
                pool.tensor_tensor(sw, sw, sin, ALU.mult).then_inc(sin_done.sem, 1)
                pool.wait_ge(sin_done.sem, sin_done.at(b, i + 1))
                pool.wait_ge(cos_done.sem, cos_done.at(b, i + 1))
                pool.tensor_tensor(with_cos[:, w, :], with_cos[:, w, :], swapped[:, w, :], ALU.add).then_inc(roped.sem, 1)

            def tail(b, s, par):
                for n in (2 * s, 2 * s + 1):
                    tile = probs[:, n % PR, :]
                    wait_apart(pool, inverted.sem, inverted.at(b, n + 1))
                    pool.tensor_scalar(tile, tile, inv[:, n % PR:n % PR + 1], 0.0, ALU.mult, ALU.add).then_inc(probs_done.sem, 1)

            def project(b, t):
                if t == 0:
                    pool.wait_ge(res_in.sem, res_in.at(b, 1))
                pool.wait_ge(gated_done.sem, gated_done.at(b, t + 1))
                pool.tensor_tensor(res[:, t, :], res[:, t, :], gated[:, t % 2, :], ALU.add).then_inc(added.sem, 1)
                if t == TT - 1:
                    pool.wait_ge(added.sem, added.at(b, TT))
                    pool.dma_start(row(dst, b), res[:, :, :]).then_inc(stored.sem, 16)

            schedule(pool, 1, nothing, tail, norm_in, nothing, qk, nothing, project)
            pool.wait_ge(stored.sem, stored.at(B - 1, 1))

        @block.scalar
        def _(act):
            for q in (act_dense, exped, turned_out, att_out):
                act.sem_inc(q.sem, q.credit)
            wt.high(act, chunks)

            def norm_out(b):
                act.wait_ge(nm.mod_done.sem, nm.mod_done.at(b, 1))
                for ch in range(KC):
                    act.wait_ge(dense_mm.sem, dense_mm.at(b, dense_slot("norm", ch) + 1))
                    act.wait_ge(nm.low.sem, nm.low.at(b, ch - 1))
                    act.activation(full[:, ch % 2, :], dense[ch % 2][:, :], ACT.Identity, bias=bf["mod"][:, 1, ch, :],
                                   scale=bf["mod"][:, 0, ch, :]).then_inc(act_dense.sem, 1)

            def value(b, t, par):
                u = dense_slot("value", t)
                act.wait_ge(dense_mm.sem, dense_mm.at(b, u + 1))
                act.copy(vals[par][:, t, :], dense[u % 2][:, :]).then_inc(act_dense.sem, 1)

            def head(b, s):
                act.wait_ge(turned.sem, turned.at(b, 2 * s - PR + 2))
                for n in (2 * s, 2 * s + 1):
                    act.wait_ge(masked.sem, masked.at(b, n + 1))
                    act.wait_ge(inverted.sem, inverted.at(b, n + 1 - PR))
                    act.activation(probs[:, n % PR, :], scores[:, n % 2, :], ACT.Exp, bias=low_score[:, n % PR:n % PR + 1], scale=-1.0,
                                   accum_out=sums[:, n % PR:n % PR + 1]).then_inc(exped.sem, 1)

            def tail(b, s, par):
                slot, r = s // HG, s % HG
                act.wait_ge(attended.sem, attended.at(b, slot))
                for i in range(2):
                    act.wait_ge(turned.sem, turned.at(b, 2 * s + i + 1))
                    act.copy(probs_t[:, r, 2 * i:2 * i + 2, :], turn_ps[i][:, :].rearrange("p (c n) -> p c n", c=2)).then_inc(turned_out.sem, 1)
                if r == HG - 1:
                    act.wait_ge(attended.sem, attended.at(b, slot + 1))
                    half = slot % 2 * (S // 2)
                    act.copy(att[:, slot // 2, half:half + S // 2], att_ps[:, 0:S // 2]).then_inc(att_out.sem, 1)

            schedule(act, LAG, head, tail, nothing, norm_out, nothing, value, nothing)

        @block.vector
        def _(dve):
            for q in (nm.stats_done, nm.mean_var, nm.normed, nm.mod_done, nm.high, nm.low, cos_done, shuffled, qk_high, qk_low,
                      masked, inverted, gated_done):
                dve.sem_inc(q.sem, q.credit)
            wt.low(dve, chunks)
            dve.wait_ge(mask_in, 16)
            dve.tensor_scalar(mask_add[:, :, :], mask_u8[:, :, :], -BIG16, BIG16, ALU.mult, ALU.add).then_inc(mask_done, 1)
            dve.wait_ge(mask_done, 1)
            dve.wait_ge(rope_in, 16)
            cos = rope[:, 0, :].unsqueeze(1).broadcast_to([P, 2, S // 2])

            def norm_in(b):
                norm_stats(dve, nm, bf, b)
                mod_copy(dve, nm, bf, mod, b, b, act_dense, act_dense.at(b, KC - 8))
                norm_apply(dve, nm, bf, b)

            def norm_out(b):
                dve.wait_ge(dense_mm.sem, dense_mm.at(b, 0))
                for ch in range(KC):
                    dve.wait_ge(act_dense.sem, act_dense.at(b, ch + 1))
                    split(dve, nm, b, ch, full[:, ch % 2, :], xh[:, ch, :], xl[:, ch, :])

            def qk(b, g, w):
                i, u = 2 * g + w, dense_slot("qk", g, w)
                dve.wait_ge(dense_mm.sem, dense_mm.at(b, u + 1))
                dve.wait_ge(qk_low.sem, qk_low.at(b, i - 1))
                dve.tensor_tensor(with_cos[:, w, :].rearrange("p (a n) -> p a n", a=2),
                                  dense[u % 2][:, :].rearrange("p (a n) -> p a n", a=2), cos, ALU.mult).then_inc(cos_done.sem, 1)
                dve.stream_shuffle(swapped[:, w, :], dense[u % 2][:, :], ROT).then_inc(shuffled.sem, 1)

            def qk_split(b, g, w):
                i = 2 * g + w
                dve.wait_ge(roped.sem, roped.at(b, i + 1))
                dve.wait_ge(stack_in[w].sem, stack_in[w].at(b, 12 * g))
                dve.tensor_copy(parts[:, w, 0, :], with_cos[:, w, :]).then_inc(qk_high.sem, 1)
                dve.wait_ge(qk_high.sem, qk_high.at(b, i + 1))
                dve.tensor_tensor(parts[:, w, 1, :], with_cos[:, w, :], parts[:, w, 0, :].bitcast(F32), ALU.subtract).then_inc(qk_low.sem, 1)

            def qk_both(b, g, w):
                qk(b, g, w)
                if w == 1:
                    qk_split(b, g, 0)
                    qk_split(b, g, 1)

            def head(b, s):
                half = s // HG % 2
                for n in (2 * s, 2 * s + 1):
                    dve.wait_ge(scored.sem, scored.at(b, n + 1))
                    wait_apart(dve, exped.sem, exped.at(b, n - 1))
                    dve.tensor_tensor_reduce(scores[:, n % 2, :], score_ps[n % 2][:, :], mask_add[:, 2 * half + n % 2, :], 1.0, BIG,
                                             ALU.add, ALU.min, low_score[:, n % PR:n % PR + 1]).then_inc(masked.sem, 1)

            def tail(b, s, par):
                for n in (2 * s, 2 * s + 1):
                    dve.wait_ge(exped.sem, exped.at(b, n + 1))
                    dve.wait_ge(probs_done.sem, probs_done.at(b, n + 1 - PR))
                    dve.reciprocal(inv[:, n % PR:n % PR + 1], sums[:, n % PR:n % PR + 1]).then_inc(inverted.sem, 1)

            def project(b, t):
                if t == 0:
                    dve.wait_ge(gate_in.sem, gate_in.at(b, 1))
                dve.wait_ge(projected.sem, projected.at(b, t + 1))
                dve.wait_ge(added.sem, added.at(b, t - 1))
                dve.tensor_tensor(gated[:, t % 2, :], out_ps[:, :], gate[:, :], ALU.mult).then_inc(gated_done.sem, 1)

            schedule(dve, 1, head, tail, norm_in, norm_out, qk_both, nothing, project)

        @block.tensor
        def _(pe):
            for q in (dense_mm, scored, turned, attended, projected):
                pe.sem_inc(q.sem, q.credit)
            pe.wait_ge(wt.low_done, len(chunks))
            pe.wait_ge(wo_in, 16)

            def dense_free(b, u):
                prev = u - 2
                if prev < 4 and prev >= 0:
                    pe.wait_ge(act_dense.sem, act_dense.at(b, prev + 1))
                elif 6 <= prev < 10:
                    pe.wait_ge(act_dense.sem, act_dense.at(b, prev - 1))
                elif prev < 0:
                    pe.wait_ge(shuffled.sem, shuffled.at(b, prev + 1))
                else:
                    pe.wait_ge(shuffled.sem, shuffled.at(b, prev - 3 if prev < 6 else prev - 7))

            def norm_out(b):
                pe.wait_ge(nm.normed.sem, nm.normed.at(b, TT))
                for ch in range(KC):
                    dense_free(b, ch)
                    for t in range(TT):
                        last = pe.transpose(dense[ch % 2][:, t * P:(t + 1) * P], bf["x"][:, t, ch * P:(ch + 1) * P], k.ident[:, :])
                    last.then_inc(dense_mm.sem, 1)

            def qk(b, g, w):
                u, c0 = dense_slot("qk", g, w), w * D + g * P
                pe.wait_ge(nm.low.sem, nm.low.at(b, KC))
                dense_free(b, u)
                split_matmul(pe, dense[u % 2][:, :], [(wh[:, ch, c0:c0 + P], wl[:, ch, c0:c0 + P]) for ch in range(KC)],
                             [(xh[:, ch, :], xl[:, ch, :]) for ch in range(KC)]).then_inc(dense_mm.sem, 1)

            def value(b, t, par):
                u = dense_slot("value", t)
                dense_free(b, u)
                split_matmul(pe, dense[u % 2][:, :], [(xh[:, ch, t * P:(t + 1) * P], xl[:, ch, t * P:(t + 1) * P]) for ch in range(KC)],
                             [(wh[:, ch, 2 * D:3 * D], wl[:, ch, 2 * D:3 * D]) for ch in range(KC)]).then_inc(dense_mm.sem, 1)

            def head(b, s):
                g, half, r = s // (2 * HG), s // HG % 2, s % HG
                if s % (2 * HG) == 0:
                    for w in range(2):
                        pe.wait_ge(stack_in[w].sem, stack_in[w].at(b, 12 * (g + 1)))
                for n in (2 * s, 2 * s + 1):
                    pe.wait_ge(masked.sem, masked.at(b, n - 1))
                    t, slot = 2 * half + n % 2, g % 2 * HG + r
                    pe.matmul(score_ps[n % 2][:, :], stacks[0][:, slot, t * P:(t + 1) * P], stacks[1][:, slot, :],
                              start=True, stop=True).then_inc(scored.sem, 1)

            def tail(b, s, par):
                slot, r = s // HG, s % HG
                pe.wait_ge(probs_done.sem, probs_done.at(b, 2 * s + 2))
                for i in range(2):
                    pe.wait_ge(turned_out.sem, turned_out.at(b, 2 * s + i - 1))
                    for ch in (2 * i, 2 * i + 1):
                        for j in range(2):
                            c0 = ch % 2 * (S // 2) + j * P
                            last = pe.transpose(turn_ps[i][:, c0:c0 + P], probs[:, (2 * s + j) % PR, ch * P:(ch + 1) * P], k.ident[:, :])
                    last.then_inc(turned.sem, 1)
                if r == HG - 1:
                    g = slot // 2
                    pe.wait_ge(turned_out.sem, turned_out.at(b, 2 * HG * (slot + 1)))
                    pe.wait_ge(act_dense.sem, act_dense.at(b, 8))
                    pe.wait_ge(att_out.sem, att_out.at(b, slot))
                    for ch in range(KC):
                        for h in range(HG):
                            last = pe.matmul(att_ps[HD * h:HD * h + HD, 0:S // 2], vals[par][:, ch, (HG * g + h) * HD:(HG * g + h + 1) * HD],
                                             probs_t[:, h, ch, :], start=ch == 0, stop=ch == KC - 1)
                    last.then_inc(attended.sem, 1)

            def project(b, t):
                pe.wait_ge(att_out.sem, att_out.at(b, 2 * NG))
                pe.wait_ge(gated_done.sem, gated_done.at(b, t))
                for ch in range(KC):
                    last = pe.matmul(out_ps[:, :], att[:, ch, t * P:(t + 1) * P], wo[:, ch, :], start=ch == 0, stop=ch == KC - 1)
                last.then_inc(projected.sem, 1)

            schedule(pe, LAG, head, tail, nothing, norm_out, qk, value, project)


def mlp_phase(nc, k, src, dst):
    with ExitStack() as ctx:
        def sb(name, shape, dt=F32):
            return ctx.enter_context(nc.sbuf_tensor("m_" + name, shape, dt))

        def ps(name):
            return ctx.enter_context(nc.psum_tensor("m_ps_" + name, [P, 512], F32))

        def count(name, per, unit=1, base=None):
            return Count(nc, ctx, "m_" + name, per, unit, base)

        mod, mlag, ring = k.mod[3], 3, 4
        nm = Norm(nc, ctx, "m")
        gate_in, res_in, stored = count("gate_in", 1, 16), count("res_in", 1, 16), count("stored", 1, 16, base=0)
        norm_t, full_done = count("norm_t", KC), count("full_done", KC)
        hidden, gelu_done, h_high, h_low, summed = (count(x, NF) for x in ("hidden", "gelu_done", "h_high", "h_low", "summed"))
        bias_done, gated_done, biased, added = count("bias_done", 1), count("gated_done", TT), count("biased", TT), count("added", TT)
        b_in = ctx.enter_context(nc.semaphore("m_b_in"))

        bf = norm_buffers(sb)
        w1h, w1l = sb("w1h", [P, KC, FF], F32R), sb("w1l", [P, KC, FF], F32R)
        w2h, w2l = sb("w2h", [P, NF, D], F32R), sb("w2l", [P, NF, D], F32R)
        full = sb("full", [P, KC, S])
        xh, xl = sb("xh", [P, KC, S], F32R), sb("xl", [P, KC, S], F32R)
        hid = sb("hid", [P, 2, S])
        hh, hl = sb("hh", [P, ring, S], F32R), sb("hl", [P, ring, S], F32R)
        gate, gate_bias, b2 = sb("gate", [P, D]), sb("gate_bias", [P, D]), sb("b2", [P, D])
        gated = sb("gated", [P, 2, D])
        res = sb("res", [P, TT, D])
        b1 = sb("b1", [P, NF])
        hid_ps, norm_ps, out_ps = [ps(f"hid{n}") for n in range(2)], [ps(f"norm{n}") for n in range(2)], [ps(f"out{n}") for n in range(TT)]
        wt = Weights(nc, ctx, "m", res)
        w1, w2 = k.ins["L1_xcond_mlp_W1"], k.ins["L1_xcond_mlp_W2"]
        chunks = [(w1[c * P:(c + 1) * P, j * D:(j + 1) * D], w1h[:, c, j * D:(j + 1) * D], w1l[:, c, j * D:(j + 1) * D], 1.0)
                  for j in range(FF // D) for c in range(KC)]
        chunks += [(w2[f * P:(f + 1) * P, :], w2h[:, f, :], w2l[:, f, :], 1.0) for f in range(NF)]

        def schedule(eng, norm_in, norm_t_, norm_split, up, down, finish):
            def entry(b, after):
                for f in range(NF):
                    up(b, f)
                    if f >= mlag:
                        down(b, f - mlag)
                    if after and f == 6:
                        norm_in(b + 1)
                    if after and f == 10:
                        norm_t_(b + 1)
                if after:
                    norm_split(b + 1)
                for f in range(NF - mlag, NF):
                    down(b, f)
                finish(b)
            norm_in(0)
            norm_t_(0)
            norm_split(0)
            with eng.Fori(0, B - 1) as b:
                entry(b, True)
            entry(B - 1, False)

        def nothing(*_):
            pass

        block = ctx.enter_context(nc.Block())

        @block.sync
        def _(sp):
            for q in (nm.x_in, gate_in, res_in):
                sp.sem_inc(q.sem, q.credit)

            def load_x(b):
                wait_apart(sp, full_done.sem, full_done.at(b, 0))
                sp.dma_start(bf["x"][:, :, :], row(src, b)).then_inc(nm.x_in.sem, 16)

            def load_res(b, first=False):
                wait_apart(sp, gated_done.sem, gated_done.at(b, 0))
                sp.dma_start(gate[:, :], k.gates[2][bass.ds(b, 1), :].rearrange("o n -> (o n)").partition_broadcast(P)).then_inc(gate_in.sem, 16)
                if not first:
                    wait_apart(sp, stored.sem, stored.at(b, 0))
                sp.dma_start(res[:, :, :], row(src, b)).then_inc(res_in.sem, 16)

            load_x(0)
            sp.dma_start(b1[:, :], k.ins["L1_xcond_mlp_b1"].rearrange("(c p) -> p c", p=P), allow_slow_non_contiguous=True).then_inc(b_in, 16)
            sp.dma_start(b2[:, :], k.ins["L1_xcond_mlp_b2"].partition_broadcast(P)).then_inc(b_in, 16)
            wt.load(sp, chunks)
            sp.wait_ge(wt.low_done, len(chunks))
            load_res(0, first=True)
            load_x(1)
            with sp.Fori(1, B - 1) as b:
                load_res(b)
                load_x(b + 1)
            load_res(B - 1)

        @block.gpsimd
        def _(pool):
            for q in (nm.var_eps_done, nm.rstd_done, added):
                pool.sem_inc(q.sem, q.credit)

            def finish(b):
                pool.wait_ge(res_in.sem, res_in.at(b, 1))
                for t in range(TT):
                    pool.wait_ge(biased.sem, biased.at(b, t + 1))
                    pool.tensor_tensor(res[:, t, :], res[:, t, :], gated[:, t % 2, :], ALU.add).then_inc(added.sem, 1)
                pool.wait_ge(added.sem, added.at(b, TT))
                pool.dma_start(row(dst, b), res[:, :, :]).then_inc(stored.sem, 16)

            schedule(pool, lambda b: norm_rstd(pool, nm, bf, b, k.neg_half), nothing, nothing, nothing, nothing, finish)
            pool.wait_ge(stored.sem, stored.at(B - 1, 1))

        @block.scalar
        def _(act):
            for q in (full_done, gelu_done):
                act.sem_inc(q.sem, q.credit)
            wt.high(act, chunks)
            act.wait_ge(b_in, 32)

            def norm_t_(b):
                act.wait_ge(nm.mod_done.sem, nm.mod_done.at(b, 1))
                act.wait_ge(nm.low.sem, nm.low.at(b, 0))
                for ch in range(KC):
                    act.wait_ge(norm_t.sem, norm_t.at(b, ch + 1))
                    act.activation(full[:, ch, :], norm_ps[ch % 2][:, :], ACT.Identity, bias=bf["mod"][:, 1, ch, :],
                                   scale=bf["mod"][:, 0, ch, :]).then_inc(full_done.sem, 1)

            def up(b, f):
                act.wait_ge(hidden.sem, hidden.at(b, f + 1))
                act.wait_ge(h_low.sem, h_low.at(b, f - 1))
                act.activation(hid[:, f % 2, :], hid_ps[f % 2][:, :], ACT.Gelu_apprx_tanh, bias=b1[:, f:f + 1]).then_inc(gelu_done.sem, 1)

            schedule(act, nothing, norm_t_, nothing, up, nothing, nothing)

        @block.vector
        def _(dve):
            for q in (nm.stats_done, nm.mean_var, nm.normed, nm.mod_done, nm.high, nm.low, h_high, h_low, bias_done, gated_done, biased):
                dve.sem_inc(q.sem, q.credit)
            wt.low(dve, chunks)
            dve.wait_ge(b_in, 32)

            def norm_in(b):
                norm_stats(dve, nm, bf, b)
                mod_copy(dve, nm, bf, mod, b, b, full_done, full_done.at(b, 0))
                norm_apply(dve, nm, bf, b)

            def norm_split(b):
                dve.wait_ge(hidden.sem, hidden.at(b, 0))
                for ch in range(KC):
                    dve.wait_ge(full_done.sem, full_done.at(b, ch + 1))
                    split(dve, nm, b, ch, full[:, ch, :], xh[:, ch, :], xl[:, ch, :])

            def up(b, f):
                dve.wait_ge(gelu_done.sem, gelu_done.at(b, f + 1))
                dve.wait_ge(summed.sem, summed.at(b, f + 1 - ring))
                dve.tensor_copy(hh[:, f % ring, :], hid[:, f % 2, :]).then_inc(h_high.sem, 1)
                dve.wait_ge(h_high.sem, h_high.at(b, f + 1))
                dve.tensor_tensor(hl[:, f % ring, :], hid[:, f % 2, :], hh[:, f % ring, :].bitcast(F32), ALU.subtract).then_inc(h_low.sem, 1)

            def finish(b):
                dve.wait_ge(gate_in.sem, gate_in.at(b, 1))
                dve.tensor_tensor(gate_bias[:, :], gate[:, :], b2[:, :], ALU.mult).then_inc(bias_done.sem, 1)
                dve.wait_ge(bias_done.sem, bias_done.at(b, 1))
                dve.wait_ge(summed.sem, summed.at(b, NF))
                for t in range(TT):
                    dve.wait_ge(added.sem, added.at(b, t - 1))
                    dve.tensor_tensor(gated[:, t % 2, :], out_ps[t][:, :], gate[:, :], ALU.mult).then_inc(gated_done.sem, 1)
                    dve.wait_ge(gated_done.sem, gated_done.at(b, t + 1))
                    dve.tensor_tensor(gated[:, t % 2, :], gated[:, t % 2, :], gate_bias[:, :], ALU.add).then_inc(biased.sem, 1)

            schedule(dve, norm_in, nothing, norm_split, up, nothing, finish)

        @block.tensor
        def _(pe):
            for q in (norm_t, hidden, summed):
                pe.sem_inc(q.sem, q.credit)

            def norm_t_(b):
                pe.wait_ge(nm.normed.sem, nm.normed.at(b, TT))
                for ch in range(KC):
                    pe.wait_ge(full_done.sem, full_done.at(b, ch - 1))
                    for t in range(TT):
                        last = pe.transpose(norm_ps[ch % 2][:, t * P:(t + 1) * P], bf["x"][:, t, ch * P:(ch + 1) * P], k.ident[:, :])
                    last.then_inc(norm_t.sem, 1)

            def up(b, f):
                if f == 0:
                    pe.wait_ge(nm.low.sem, nm.low.at(b, KC))
                pe.wait_ge(gelu_done.sem, gelu_done.at(b, f - 1))
                split_matmul(pe, hid_ps[f % 2][:, :], [(w1h[:, ch, f * P:(f + 1) * P], w1l[:, ch, f * P:(f + 1) * P]) for ch in range(KC)],
                             [(xh[:, ch, :], xl[:, ch, :]) for ch in range(KC)]).then_inc(hidden.sem, 1)

            def down(b, f):
                pe.wait_ge(h_low.sem, h_low.at(b, f + 1))
                for t in range(TT):
                    if f == 0:
                        pe.wait_ge(gated_done.sem, gated_done.at(b, t + 1 - TT))
                    for n, (a, c) in enumerate(((hh, w2h), (hh, w2l), (hl, w2h))):
                        last = pe.matmul(out_ps[t][:, :], a[:, f % ring, t * P:(t + 1) * P], c[:, f, :],
                                         start=f == 0 and n == 0, stop=f == NF - 1 and n == 2)
                last.then_inc(summed.sem, 1)

            pe.wait_ge(wt.low_done, len(chunks))
            schedule(pe, nothing, norm_t_, nothing, up, down, nothing)




def rope_tables():
    inv_freq = 1.0 / 10000.0 ** (np.arange(0, HD, 2, dtype=np.float32) / HD)
    freqs = np.outer(np.arange(S // 2, dtype=np.float32), inv_freq)
    emb = np.concatenate([freqs, freqs], axis=-1)
    cos, sin = np.cos(emb).astype(np.float32), np.sin(emb).astype(np.float32)
    sign = np.where(np.arange(HD) < HD // 2, np.float32(-1), np.float32(1))
    return np.ascontiguousarray(np.stack([np.tile(cos.T, (HG, 1)), np.tile((sin * sign).T, (HG, 1))]))


def program(nc, ins, rope, out):
    with ExitStack() as ctx:
        PASSED.clear()
        k = Kernel()
        k.ins, k.rope, k.out = ins, rope, out
        k.gates = nc.dram_tensor("gates", (3, B, D), F32).ap()
        k.keys = nc.dram_tensor("ctx_keys", (2, B, NG, P, L), F32).ap()
        k.vals = nc.dram_tensor("ctx_vals", (2, B * L, D), F32).ap()
        k.x1 = nc.dram_tensor("x_after_cross0", (B, S, D), F32).ap()
        k.x2 = nc.dram_tensor("x_after_self", (B, S, D), F32).ap()
        k.x3 = nc.dram_tensor("x_after_cross1", (B, S, D), F32).ap()
        k.ident = ctx.enter_context(nc.sbuf_tensor("ident", [P, P], F32))
        k.neg_half = ctx.enter_context(nc.sbuf_tensor("neg_half", [P, TT], F32))
        k.mod = [ctx.enter_context(nc.sbuf_tensor(f"mod{n}", [P, 2, KC, B], F32)) for n in range(4)]
        for e in (nc.sync, nc.vector, nc.gpsimd):
            PASSED[e.engine] = ctx.enter_context(nc.semaphore(f"passed_{len(PASSED)}"))
        prologue(nc, k)
        c = CrossCounts(nc, ctx)
        cross_phase(nc, k, c, 0, ins["x"], k.x1)
        self_phase(nc, k, k.x1, k.x2)
        cross_phase(nc, k, c, 1, k.x2, k.x3)
        mlp_phase(nc, k, k.x3, out)


def kernel(**inputs):
    import concourse.bacc as bacc
    from concourse.bass_utils import run_bass_kernel_spmd

    nc = bacc.Bacc("TRN2", target_bir_lowering=False, num_devices=1)
    arrays, ins = {}, {}
    for name, a in inputs.items():
        a = np.ascontiguousarray(a)
        arrays[name] = a
        ins[name] = nc.dram_tensor(name, a.shape, mybir.dt.from_np(a.dtype), kind="ExternalInput").ap()
    arrays["rope"] = rope_tables()
    rope = nc.dram_tensor("rope", arrays["rope"].shape, F32, kind="ExternalInput").ap()
    out = nc.dram_tensor("out", (B, S, D), F32, kind="ExternalOutput").ap()
    program(nc, ins, rope, out)
    r = run_bass_kernel_spmd(nc, [arrays], core_ids=[0])
    return r.results[0]["out"]
```

```python
from contextlib import ExitStack

import numpy as np

import concourse.bass as bass
from concourse import mybir

F32 = mybir.dt.float32
F32R = mybir.dt.float32r
BF16 = mybir.dt.bfloat16
U8 = mybir.dt.uint8
ALU = mybir.AluOpType
ACT = mybir.ActivationFunctionType
AX_X = mybir.AxisListType.X

P = 128
B = 8
S = 512
D = 512
L = 77
NH = 16
HD = D // NH
KC = D // P
TT = S // P
HG = P // HD
NG = NH // HG
GL = HG * L
FF = 4 * D
NF = FF // P
EPS = 1e-5
SCALE = float(HD) ** -0.5
BIG = float(np.finfo(np.float32).max)
BIG16 = 3.3895313892515355e38
LAG = 3
PR = 8
STEPS = NG * TT
TURN_LAG = HG + 1
ATTEND_LAG = TURN_LAG + HG
PROJECT_AT = 7
NORM_STATS = (1, 3)
NORM_APPLY = (5, 6)
NORM_TURN = 8


class Count:

    def __init__(self, nc, ctx, name, per, unit=1, base=None):
        self.sem = ctx.enter_context(nc.semaphore(name))
        self.per, self.unit, self.base = per, unit, per if base is None else base

    @property
    def credit(self):
        return self.base * self.unit

    def at(self, b, k):
        return (b * self.per + (self.base + k)) * self.unit


PASSED = {}


def wait_apart(eng, sem, value):
    eng.wait_ge(sem, value)
    eng.sem_inc(PASSED[eng.engine], 1)


def one(ap3):
    return ap3.rearrange("o p d -> (o p) d")


def row(x, b):
    return one(x[bass.ds(b, 1)]).rearrange("(t p) d -> p t d", p=P)


def split_matmul(pe, out, lhs, rhs, part=0, parts=1):
    terms = [(a, c) for (ah, al), (ch, cl) in zip(lhs, rhs) for a, c in ((ah, ch), (ah, cl), (al, ch))]
    size = len(terms) // parts
    for n in range(part * size, part * size + size):
        a, c = terms[n]
        last = pe.matmul(out, a, c, start=n == 0, stop=n == len(terms) - 1)
    return last


class Kernel:
    pass


def prologue(nc, k):
    with ExitStack() as ctx:
        def sb(name, shape, dt=F32):
            return ctx.enter_context(nc.sbuf_tensor("p_" + name, shape, dt))

        def ps(name):
            return ctx.enter_context(nc.psum_tensor("p_ps_" + name, [P, 512], F32))

        used = []

        def sem(name):
            used.append(ctx.enter_context(nc.semaphore("p_" + name)))
            return used[-1]

        cond = sb("cond", [B, 2, D])
        cond_t = sb("cond_t", [P, 2, KC, 32])
        bias_rows = sb("bias_rows", [P, 4, D])
        mod_rows = sb("mod_rows", [P, 4, D])
        mod_cols = sb("mod_cols", [P, 4, KC, P])
        norm_w = sb("norm_w", [P, 3, KC])
        kv_mod = sb("kv_mod", [P, 2, KC, B])
        ring = [sb(f"w{n}", [P, KC, D]) for n in range(8)]
        wkv = sb("wkv", [P, KC, 2 * D])
        ck = ring[0]
        cv = ring[1]
        ctx_raw = sb("ctx_raw", [L, B, D])
        ctx_n = ring[4]
        ctx_nn = sb("ctx_nn", [L, B, D])
        ctx_t = sb("ctx_t", [P, 2, KC, B * L])
        stats = sb("stats", [L, B, 6])
        mv = sb("mv", [L, B, 2])
        rstd = sb("rstd", [L, B])
        var_eps = sb("var_eps", [L, B])
        half_l = sb("half_l", [L, B])
        bk = sb("bk", [P, KC])
        bv_rows = sb("bv_rows", [P, D])
        keys = [sb(f"keys{n}", [P, 4 * L]) for n in range(2)]
        vals = [sb(f"vals{n}", [P, D]) for n in range(2)]
        acc = [ps(f"acc{n}") for n in range(4)]
        tp = [ps(f"tp{n}") for n in range(4)]

        NB = 13
        cond_in, cond_silu, small_in, zeroed, ident_z = (sem(x) for x in ("cond_in", "cond_silu", "small_in", "zeroed", "ident_z"))
        bias_in, ctx_in, wkv_in, ck_in, cv_in = (sem(x) for x in ("bias_in", "ctx_in", "wkv_in", "ck_in", "cv_in"))
        w_in = [sem(f"w_in{n}") for n in range(8)]
        cond_tp, cond_td, rows_mm, rows_done, cols_tp, cols_done = (
            sem(x) for x in ("cond_tp", "cond_td", "rows_mm", "rows_done", "cols_tp", "cols_done"))
        mods, st_done, mv_done, ve_done, rstd_done, ctx_normed = (
            sem(x) for x in ("mods", "st_done", "mv_done", "ve_done", "rstd_done", "ctx_normed"))
        ctx_tp, ctx_raw_done, ctx_a, ctx_td = (sem(x) for x in ("ctx_tp", "ctx_raw_done", "ctx_a", "ctx_td"))
        k_mm, k_evac, v_mm, v_evac, gates_out = (sem(x) for x in ("k_mm", "k_evac", "v_mm", "v_evac", "gates_out"))
        k_out = [sem(f"k_out{n}") for n in range(2)]
        v_out = [sem(f"v_out{n}") for n in range(2)]

        blocks = []
        for w, bias, n, src in (("L0_xcond_Wss_q", "L0_xcond_bss_q", 2, 0), ("L0_xcond_Wss_kv", "L0_xcond_bss_kv", 2, 0),
                                ("L1_xcond_adaLN_W", "L1_xcond_adaLN_b", 9, 1)):
            blocks += [(k.ins[w], k.ins[bias], j * D, src) for j in range(n)]
        vtiles = [(t * P, min(P, B * L - t * P)) for t in range(-(-B * L // P))]
        engines = ExitStack()
        block = engines.enter_context(nc.Block())

        @block.sync
        def _(sp):
            sp.dma_start(cond[:, 1, :], k.ins["cond_1024"]).then_inc(cond_in, 16)
            for n in range(8):
                w, _, c0, _ = blocks[n]
                sp.dma_start(ring[n][:, :, :], w[:, c0:c0 + D].rearrange("(k p) n -> p k n", p=P)).then_inc(w_in[n], 16)
                if n == 3:
                    sp.dma_start(ctx_raw[:, :, :], k.ins["ctx_1024"].rearrange("b s d -> s b d")).then_inc(ctx_in, 16)
            sp.wait_ge(zeroed, 1)
            for n, (_, bias, c0, _) in enumerate(blocks):
                src = bias[c0:c0 + D].partition_broadcast(B)
                sp.dma_start(bias_rows[32 * (n % 4):32 * (n % 4) + B, n // 4, :], src).then_inc(bias_in, 16)
            for n, w in enumerate(("L1_xcond_norm1_w", "L1_xcond_normc_w", "L1_xcond_norm2_w")):
                sp.dma_start(norm_w[:, n, :], k.ins[w].rearrange("(c p) -> p c", p=P), allow_slow_non_contiguous=True).then_inc(small_in, 16)
            sp.dma_start(bk[:, :], k.ins["L0_xcond_bkv"][0:D].rearrange("(c p) -> p c", p=P), allow_slow_non_contiguous=True).then_inc(small_in, 16)
            sp.dma_start(bv_rows[:, :], k.ins["L0_xcond_bkv"][D:2 * D].partition_broadcast(P)).then_inc(small_in, 16)
            sp.dma_start(wkv[:, :, :], k.ins["L0_xcond_Wkv"].rearrange("(k p) n -> p k n", p=P)).then_inc(wkv_in, 16)
            for n in range(8, NB):
                sp.wait_ge(rows_mm, n // 4 - 1)
                w, _, c0, _ = blocks[n]
                sp.dma_start(ring[n % 8][:, :, :], w[:, c0:c0 + D].rearrange("(k p) n -> p k n", p=P)).then_inc(w_in[n % 8], 16)
            for n, g in enumerate((6, 9, 12)):
                sp.wait_ge(rows_done, g // 4 + 1)
                sp.dma_start(k.gates[n], mod_rows[32 * (g % 4):32 * (g % 4) + B, g // 4, :]).then_inc(gates_out, 16)
            sp.wait_ge(rows_mm, 4)
            sp.dma_start(ck[:, :, :], k.ins["L1_xcond_ck_W"].rearrange("(k p) n -> p k n", p=P)).then_inc(ck_in, 16)
            sp.dma_start(cv[:, :, :], k.ins["L1_xcond_cv_W"].rearrange("(k p) n -> p k n", p=P)).then_inc(cv_in, 16)
            n = 0
            for layer in range(2):
                for m in range(KC):
                    for half in range(2):
                        sp.wait_ge(k_evac, n + 1)
                        sp.dma_start(k.keys[layer][4 * half:4 * half + 4, m].rearrange("b p t -> p b t"),
                                     keys[n % 2][:, :].rearrange("p (b t) -> p b t", b=4)).then_inc(k_out[n % 2], 16)
                        n += 1
                for t, (t0, tn) in enumerate(vtiles):
                    n2 = layer * len(vtiles) + t
                    sp.wait_ge(v_evac, n2 + 1)
                    sp.dma_start(k.vals[layer][t0:t0 + tn, :], vals[n2 % 2][0:tn, :]).then_inc(v_out[n2 % 2], 16)
            sp.wait_ge(gates_out, 48)
            for s in k_out:
                sp.wait_ge(s, 16 * 8)
            for s in v_out:
                sp.wait_ge(s, 16 * len(vtiles))

        @block.gpsimd
        def _(pool):
            pool.memset(k.ident[:, :], 0.0).then_inc(ident_z, 1)
            pool.memset(bias_rows[:, :, :], 0.0).then_inc(zeroed, 1)
            pool.wait_ge(ident_z, 1)
            pool.affine_select(out=k.ident[:, :], in_=k.ident[:, :], compare_op=ALU.not_equal, fill=1.0, base=0,
                               pattern=[[-1, P]], channel_multiplier=1).then_inc(ident_z, 1)
            pool.memset(cond_t[:, :, :, :], 0.0).then_inc(zeroed, 1)
            pool.memset(mod_rows[:, 3, :], 0.0).then_inc(zeroed, 1)
            pool.memset(k.neg_half[:, :], -0.5)
            pool.memset(half_l[:, :], -0.5).then_inc(zeroed, 1)
            pool.wait_ge(zeroed, 4)
            pool.wait_ge(mv_done, B)
            pool.tensor_scalar(var_eps[:, :], mv[:, :, 1], EPS, None, ALU.add).then_inc(ve_done, 1)
            pool.wait_ge(ve_done, 1)
            pool.tensor_tensor(rstd[:, :], var_eps[:, :], half_l[:, :], ALU.pow).then_inc(rstd_done, 1)

        @block.scalar
        def _(act):
            act.wait_ge(cond_in, 16)
            act.activation(cond[:, 0, :], cond[:, 1, :], ACT.Silu).then_inc(cond_silu, 1)
            for n in range(8):
                act.wait_ge(ctx_tp, n + 1)
                act.copy(ctx_t[:, 0, n // 2, 4 * L * (n % 2):4 * L * (n % 2) + 4 * L], tp[n % 4][:, 0:4 * L]).then_inc(ctx_raw_done, 1)
            act.wait_ge(small_in, 16 * 5)
            for n in range(16):
                layer, m = n // 8, n % 8 // 2
                act.wait_ge(k_mm, n + 1)
                if n >= 2:
                    act.wait_ge(k_out[n % 2], 16 * (n // 2))
                if layer == 0:
                    act.activation(keys[n % 2][:, :], acc[n % 2][:, 0:4 * L], ACT.Identity, bias=bk[:, m:m + 1]).then_inc(k_evac, 1)
                else:
                    act.copy(keys[n % 2][:, :], acc[n % 2][:, 0:4 * L]).then_inc(k_evac, 1)

        @block.vector
        def _(dve):
            dve.wait_ge(cond_tp, 1)
            dve.wait_ge(zeroed, 2)
            dve.tensor_copy(cond_t[:, :, :, 0:B], tp[0][:, 0:2 * KC * B].rearrange("p (s c b) -> p s c b", s=2, c=KC)).then_inc(cond_td, 1)
            dve.wait_ge(ctx_in, 16)
            for b in range(B):
                dve.bn_stats(stats[:, b, :], ctx_raw[:, b, :]).then_inc(st_done, 1)
            for b in range(B):
                dve.wait_ge(st_done, b + 1)
                dve.bn_aggr(mv[:, b, :], stats[:, b, :]).then_inc(mv_done, 1)
            dve.wait_ge(rstd_done, 1)
            for b in range(B):
                dve.tensor_scalar(ctx_nn[:, b, :], ctx_raw[:, b, :], mv[:, b, 0:1], rstd[:, b:b + 1],
                                  ALU.subtract, ALU.mult).then_inc(ctx_normed, 1)
            dve.wait_ge(bias_in, 16 * NB)
            dve.wait_ge(zeroed, 3)
            for q in range(4):
                np_ = P if q < 3 else 32
                dve.wait_ge(rows_mm, q + 1)
                dve.tensor_tensor(mod_rows[0:np_, q, :], acc[q][0:np_, :], bias_rows[0:np_, q, :], ALU.add).then_inc(rows_done, 1)
            for q in range(4):
                dve.wait_ge(cols_tp, q + 1)
                dve.tensor_copy(mod_cols[:, q, :, 0:P if q < 3 else 32],
                                tp[q][:, :].rearrange("p (c n) -> p c n", c=KC)[:, :, 0:P if q < 3 else 32]).then_inc(cols_done, 1)
            dve.wait_ge(cols_done, 4)
            dve.wait_ge(small_in, 16 * 5)

            def vec(n):
                return mod_cols[:, n // 4, :, 32 * (n % 4):32 * (n % 4) + B]

            for dst, sc, sh in ((k.mod[0], 0, 1), (kv_mod, 2, 3)):
                dve.tensor_scalar(dst[:, 0, :, :], vec(sc), 1.0, None, ALU.add).then_inc(mods, 1)
                dve.tensor_copy(dst[:, 1, :, :], vec(sh)).then_inc(mods, 1)
            for n, (sc, sh) in enumerate(((5, 4), (8, 7), (11, 10))):
                dve.scalar_tensor_tensor(k.mod[1 + n][:, 0, :, :], vec(sc), 1.0, norm_w[:, n, :].unsqueeze(2).broadcast_to([P, KC, B]),
                                         ALU.add, ALU.mult).then_inc(mods, 1)
                dve.tensor_copy(k.mod[1 + n][:, 1, :, :], vec(sh)).then_inc(mods, 1)
            dve.wait_ge(mods, 4)
            for n in range(8, 16):
                c, half = (n - 8) // 2, n % 2
                out = ctx_t[:, 1, c, 4 * L * half:4 * L * half + 4 * L].rearrange("p (b t) -> p b t", b=4)
                bs = slice(4 * half, 4 * half + 4)
                dve.wait_ge(ctx_tp, n + 1)
                dve.tensor_tensor(out, tp[n % 4][:, 0:4 * L].rearrange("p (b t) -> p b t", b=4),
                                  kv_mod[:, 0, c, bs].unsqueeze(2).broadcast_to([P, 4, L]), ALU.mult).then_inc(ctx_a, 1)
                dve.wait_ge(ctx_a, n - 7)
                dve.tensor_tensor(out, out, kv_mod[:, 1, c, bs].unsqueeze(2).broadcast_to([P, 4, L]), ALU.add).then_inc(ctx_td, 1)
            for n in range(2 * len(vtiles)):
                tn = vtiles[n % len(vtiles)][1]
                dve.wait_ge(v_mm, n + 1)
                if n >= 2:
                    dve.wait_ge(v_out[n % 2], 16 * (n // 2))
                if n < len(vtiles):
                    dve.tensor_tensor(vals[n % 2][0:tn, :], acc[2 + n % 2][0:tn, :], bv_rows[0:tn, :], ALU.add).then_inc(v_evac, 1)
                else:
                    dve.tensor_copy(vals[n % 2][0:tn, :], acc[2 + n % 2][0:tn, :]).then_inc(v_evac, 1)

        @block.tensor
        def _(pe):
            pe.wait_ge(ident_z, 2)
            pe.wait_ge(cond_silu, 1)
            for s in range(2):
                for c in range(KC):
                    last = pe.transpose(tp[0][:, (s * KC + c) * B:(s * KC + c + 1) * B], cond[:, s, c * P:(c + 1) * P], k.ident[0:B, 0:B])
            last.then_inc(cond_tp, 1)
            pe.wait_ge(cond_td, 1)
            for q in range(4):
                mine = [n for n in range(4 * q, min(4 * q + 4, NB))]
                for n in mine:
                    pe.wait_ge(w_in[n % 8], 16 * (n // 8 + 1))
                for c in range(KC):
                    for n in mine:
                        r = 32 * (n % 4)
                        last = pe.matmul(acc[q][r:r + 32, :], cond_t[:, blocks[n][3], c, :], ring[n % 8][:, c, :],
                                         start=c == 0, stop=c == KC - 1)
                last.then_inc(rows_mm, 1)
            for q in range(4):
                n = P if q < 3 else 32
                pe.wait_ge(rows_done, q + 1)
                for c in range(KC):
                    last = pe.transpose(tp[q][:, c * P:c * P + n], mod_rows[0:n, q, c * P:(c + 1) * P], k.ident[0:n, 0:n])
                last.then_inc(cols_tp, 1)
            for n in range(16):
                src = ctx_raw if n < 8 else ctx_nn
                c, half = n % 8 // 2, n % 2
                if n == 0:
                    pe.wait_ge(ctx_in, 16)
                    pe.wait_ge(cols_done, 4)
                if n == 8:
                    pe.wait_ge(ctx_normed, B)
                if 4 <= n < 12:
                    pe.wait_ge(ctx_raw_done, n - 3)
                if n >= 12:
                    pe.wait_ge(ctx_a, n - 11)
                for j in range(4):
                    last = pe.transpose(tp[n % 4][:, j * L:(j + 1) * L], src[:, 4 * half + j, c * P:(c + 1) * P], k.ident[0:L, 0:L])
                last.then_inc(ctx_tp, 1)
            pe.wait_ge(wkv_in, 16)
            pe.wait_ge(ctx_td, 8)
            pe.wait_ge(rows_done, 4)
            for layer in range(2):
                if layer:
                    pe.wait_ge(ck_in, 16)
                    pe.wait_ge(cv_in, 16)
                wk = wkv if layer == 0 else ck
                for i in range(8):
                    n, m, half = layer * 8 + i, i // 2, i % 2
                    if n >= 2:
                        pe.wait_ge(k_evac, n - 1)
                    for c in range(KC):
                        last = pe.matmul(acc[n % 2][:, 0:4 * L], wk[:, c, m * P:(m + 1) * P],
                                         ctx_t[:, 1 - layer, c, 4 * L * half:4 * L * half + 4 * L], start=c == 0, stop=c == KC - 1)
                    last.then_inc(k_mm, 1)
                for t, (t0, tn) in enumerate(vtiles):
                    n = layer * len(vtiles) + t
                    if n >= 2:
                        pe.wait_ge(v_evac, n - 1)
                    for c in range(KC):
                        w = wkv[:, c, D:2 * D] if layer == 0 else cv[:, c, :]
                        last = pe.matmul(acc[2 + n % 2][0:tn, :], ctx_t[:, 1 - layer, c, t0:t0 + tn], w, start=c == 0, stop=c == KC - 1)
                    last.then_inc(v_mm, 1)

        engines.close()
        with nc.Block() as tidy:
            @tidy.sync
            def _(sp):
                for s in used:
                    sp.sem_clear(s)


class Norm:

    def __init__(self, nc, ctx, tag):
        def count(name, per, unit=1):
            return Count(nc, ctx, f"{tag}_{name}", per, unit)
        self.x_in = count("x_in", 1, 16)
        self.stats_done = count("stats_done", TT)
        self.mean_var = count("mean_var", TT)
        self.var_eps_done = count("var_eps_done", 1)
        self.rstd_done = count("rstd_done", 1)
        self.normed = count("normed", TT)
        self.mod_done = count("mod_done", 1)
        self.high = count("high", KC)
        self.low = count("low", KC)


def norm_stats(dve, nm, bf, n, tiles=range(TT)):
    dve.wait_ge(nm.x_in.sem, nm.x_in.at(n, 1))
    for t in tiles:
        dve.bn_stats(bf["stats"][:, t, :], bf["x"][:, t, :]).then_inc(nm.stats_done.sem, 1)
    for t in tiles:
        wait_apart(dve, nm.stats_done.sem, nm.stats_done.at(n, t + 1))
        dve.bn_aggr(bf["mv"][:, t, :], bf["stats"][:, t, :]).then_inc(nm.mean_var.sem, 1)


def norm_rstd(pool, nm, bf, n, neg_half):
    wait_apart(pool, nm.mean_var.sem, nm.mean_var.at(n, TT))
    pool.tensor_scalar(bf["var_eps"][:, :], bf["mv"][:, :, 1], EPS, None, ALU.add).then_inc(nm.var_eps_done.sem, 1)
    pool.wait_ge(nm.var_eps_done.sem, nm.var_eps_done.at(n, 1))
    pool.tensor_tensor(bf["rstd"][:, :], bf["var_eps"][:, :], neg_half[:, :], ALU.pow).then_inc(nm.rstd_done.sem, 1)


def norm_apply(dve, nm, bf, n, tiles=range(TT)):
    dve.wait_ge(nm.rstd_done.sem, nm.rstd_done.at(n, 1))
    for t in tiles:
        dve.tensor_scalar(bf["x"][:, t, :], bf["x"][:, t, :], bf["mv"][:, t, 0:1], bf["rstd"][:, t:t + 1],
                          ALU.subtract, ALU.mult).then_inc(nm.normed.sem, 1)


def norm_buffers(sb):
    return {"x": sb("x", [P, TT, D]), "stats": sb("stats", [P, TT, 6]), "mv": sb("mv", [P, TT, 2]),
            "rstd": sb("rstd", [P, TT]), "var_eps": sb("var_eps", [P, TT]), "mod": sb("mod", [P, 2, KC, 1])}


def mod_copy(dve, nm, bf, mod, b, n, used, used_at):
    dve.wait_ge(used.sem, used_at)
    dve.tensor_copy(bf["mod"][:, :, :, :], mod[:, :, :, bass.ds(b, 1)]).then_inc(nm.mod_done.sem, 1)


def split(dve, nm, n, c, full, high, low):
    dve.tensor_copy(high, full).then_inc(nm.high.sem, 1)
    dve.wait_ge(nm.high.sem, nm.high.at(n, c + 1))
    dve.tensor_tensor(low, full, high.bitcast(F32), ALU.subtract).then_inc(nm.low.sem, 1)


class Weights:

    def __init__(self, nc, ctx, tag, stage):
        self.stage = stage
        self.chunk_in = [ctx.enter_context(nc.semaphore(f"{tag}_w_in{n}")) for n in range(4)]
        self.scaled = ctx.enter_context(nc.semaphore(f"{tag}_w_scaled"))
        self.high_done = ctx.enter_context(nc.semaphore(f"{tag}_w_high"))
        self.low_done = ctx.enter_context(nc.semaphore(f"{tag}_w_low"))

    def load(self, sp, chunks):
        for n, (src, _, _, _) in enumerate(chunks):
            if n >= 4:
                sp.wait_ge(self.low_done, n - 3)
            sp.dma_start(self.stage[:, n % 4, :], src).then_inc(self.chunk_in[n % 4], 16)

    def high(self, act, chunks):
        for n, (_, high, _, scale) in enumerate(chunks):
            act.wait_ge(self.chunk_in[n % 4], 16 * (n // 4 + 1))
            if scale != 1.0:
                act.mul(self.stage[:, n % 4, :], self.stage[:, n % 4, :], scale).then_inc(self.scaled, 1)
                act.wait_ge(self.scaled, 1 + sum(c[3] != 1.0 for c in chunks[:n]))
            act.copy(high, self.stage[:, n % 4, :]).then_inc(self.high_done, 1)

    def low(self, dve, chunks):
        for n, (_, high, low, _) in enumerate(chunks):
            dve.wait_ge(self.high_done, n + 1)
            dve.tensor_tensor(low, self.stage[:, n % 4, :], high.bitcast(F32), ALU.subtract).then_inc(self.low_done, 1)


def weight_chunks(w, cols, high, low, scale=1.0):
    return [(w[c * P:(c + 1) * P, cols], high[:, c, :], low[:, c, :], scale) for c in range(KC)]


class CrossCounts:
    def __init__(self, nc, ctx):
        def count(name, per, unit=1):
            return Count(nc, ctx, f"x_{name}", per, unit)
        self.norm = Norm(nc, ctx, "x")
        self.keys_in = count("keys_in", HG, 16)
        self.vals_in = count("vals_in", 1, 16)
        self.gate_in = count("gate_in", 1, 16)
        self.res_in = count("res_in", 1, 16)
        self.dense_mm = count("dense_mm", 8)
        self.dense_out = count("dense_out", 8)
        self.scored = count("scored", 16)
        self.masked = count("masked", 16)
        self.row_max = count("row_max", 16)
        self.shifted = count("shifted", 16)
        self.exped = count("exped", 16)
        self.summed = count("summed", 16)
        self.inverted = count("inverted", 16)
        self.probs = count("probs", 16)
        self.turned = count("turned", 16)
        self.turned_out = count("turned_out", 16)
        self.attended = count("attended", NG)
        self.att_high = count("att_high", NG)
        self.att_low = count("att_low", NG)
        self.projected = count("projected", TT)
        self.gated = count("gated", TT)
        self.added = count("added", TT)
        self.stored = Count(nc, ctx, "x_stored", 1, 16, base=0)


def cross_phase(nc, k, c, layer, src, dst):
    with ExitStack() as ctx:
        def sb(name, shape, dt=F32):
            return ctx.enter_context(nc.sbuf_tensor(f"x{layer}_" + name, shape, dt))

        def ps(name):
            return ctx.enter_context(nc.psum_tensor(f"x{layer}_ps_" + name, [P, 512], F32))

        off = layer * B
        nm = c.norm
        if layer == 0:
            wq, wo, mod, gate_op = "L0_xcond_Wq", "L0_xcond_Wp", k.mod[0], ALU.add
        else:
            wq, wo, mod, gate_op = "L1_xcond_cq_W", "L1_xcond_co_W", k.mod[2], ALU.mult
        bf = norm_buffers(sb)
        wqh, wql = sb("wqh", [P, KC, D], F32R), sb("wql", [P, KC, D], F32R)
        woh, wol = sb("woh", [P, KC, D], F32R), sb("wol", [P, KC, D], F32R)
        full = sb("full", [P, KC, S])
        xh, xl = sb("xh", [P, KC, S], F32R), sb("xl", [P, KC, S], F32R)
        queries = [sb(f"queries{n}", [P, NG, S]) for n in range(2)]
        keys = [sb(f"keys{n}", [P, NG, GL]) for n in range(2)]
        vals = sb("vals", [L, D])
        scores = sb("scores", [P, 4, GL])
        mx, sums, inv = sb("mx", [P, 2, HG]), sb("sums", [P, STEPS, HG]), sb("inv", [P, STEPS, HG])
        probs = sb("probs", [P, STEPS, GL])
        probs_t = [sb(f"probs_t{n}", [L, HG, S]) for n in range(2)]
        ah, al = [sb(f"ah{n}", [P, NG, S], F32R) for n in range(2)], [sb(f"al{n}", [P, NG, S], F32R) for n in range(2)]
        gate = sb("gate", [P, D])
        gated = sb("gated", [P, 2, D])
        res = sb("res", [P, TT, D])
        bq = sb("bq", [P, KC])
        mask = sb("mask", [P, L])
        if layer == 1:
            mask_u8, ctx_mask = sb("mask_u8", [P, B * L], U8), sb("ctx_mask", [P, B * L])
        dense, score_ps, turn_ps = [ps(f"dense{n}") for n in range(2)], [ps(f"score{n}") for n in range(2)], [ps(f"turn{n}") for n in range(2)]
        att_ps, out_ps = ps("att"), ps("out")
        wt = Weights(nc, ctx, f"x{layer}", res)
        bq_in, keys_zeroed, mask_done = (ctx.enter_context(nc.semaphore(f"x{layer}_{x}")) for x in ("bq_in", "keys_zeroed", "mask_done"))
        mask_in = bq_in
        chunks = weight_chunks(k.ins[wq], slice(0, D), wqh, wql) + weight_chunks(k.ins[wo], slice(0, D), woh, wol)

        def heads4(ap):
            return ap.rearrange("p (h t) -> p h t", h=HG)

        def per_head(ap):
            return ap.unsqueeze(2).broadcast_to([P, HG, L])

        block = ctx.enter_context(nc.Block())

        def schedule(eng, score, turn, query, query_out, attend, attend_out, norm, project, project_out):
            def entry(b, par, before, after, after2):
                for n in range(STEPS):
                    u, (g, rest) = n - PROJECT_AT, divmod(n - ATTEND_LAG, HG)
                    if before and u % 2 == 0 and 2 <= u <= 2 * TT:
                        project_out(b - 1, u // 2 - 1)
                    if after and n % 2 == 0 and 2 <= n <= 2 * NG:
                        query_out(b + 1, n // 2 - 1, 1 - par)
                    if rest == 1 and g >= 0:
                        attend_out(b, g, par)
                    elif rest == 1 and before:
                        attend_out(b - 1, g + NG, 1 - par)
                    score(b, n, par)
                    if n >= TURN_LAG:
                        turn(b, n - TURN_LAG)
                    elif before:
                        turn(b - 1, n - TURN_LAG + STEPS)
                    if after and n < 2 * NG:
                        query(b + 1, n // 2, n % 2)
                    if rest == 0 and g >= 0:
                        attend(b, g, par)
                    elif rest == 0 and before:
                        attend(b - 1, g + NG, 1 - par)
                    if after2:
                        norm(b + 2, n)
                    if before and 0 <= u < 2 * TT:
                        project(b - 1, u // 2, u % 2, 1 - par)
            for n in range(STEPS):
                norm(0, n)
            for m in range(NG):
                query(0, m, 0)
                query(0, m, 1)
                query_out(0, m, 0)
            for n in range(STEPS):
                norm(1, n)
            entry(0, 0, False, True, True)
            with eng.Fori(0, (B - 4) // 2) as j:
                entry(j * 2 + 1, 1, True, True, True)
                entry(j * 2 + 2, 0, True, True, True)
            for b in range(B - 3, B):
                entry(b, b % 2, True, b + 1 < B, b + 2 < B)
            for h in range(NH - TURN_LAG, NH):
                turn(B - 1, h)
                if h % HG == ATTEND_LAG % HG:
                    attend(B - 1, h // HG - 1, 1)
                    attend_out(B - 1, h // HG - 1, 1)
            attend(B - 1, NG - 1, 1)
            attend_out(B - 1, NG - 1, 1)
            for t in range(TT):
                project(B - 1, t, 0, 1)
                project(B - 1, t, 1, 1)
                project_out(B - 1, t)

        def nothing(*_):
            pass

        @block.sync
        def _(sp):
            if layer == 0:
                sp.sem_inc(nm.x_in.sem, nm.x_in.credit)
                for q in (c.keys_in, c.vals_in, c.gate_in, c.res_in):
                    sp.sem_inc(q.sem, q.credit)

            def load_x(b):
                wait_apart(sp, c.dense_out.sem, c.dense_out.at(b + off, KC - 8))
                sp.dma_start(bf["x"][:, :, :], row(src, b)).then_inc(nm.x_in.sem, 16)

            def load_keys(b, par):
                wait_apart(sp, c.scored.sem, c.scored.at(b + off, HG - STEPS))
                for r in range(HG):
                    rows = slice(HD * r, HD * r + HD)
                    sp.dma_start(keys[par][rows, :, r * L:(r + 1) * L],
                                 k.keys[layer][bass.ds(b, 1)].rearrange("o g p t -> (o p) g t")[rows]
                                 ).then_inc(c.keys_in.sem, 16)

            def load_vals(b):
                wait_apart(sp, c.attended.sem, c.attended.at(b + off, 0))
                sp.dma_start(vals[:, :], k.vals[layer][bass.ds(b * L, L), :]).then_inc(c.vals_in.sem, 16)

            def load_res(b, first=False):
                if layer == 1:
                    wait_apart(sp, c.gated.sem, c.gated.at(b + off, 0))
                    sp.dma_start(gate[:, :], k.gates[1][bass.ds(b, 1), :].rearrange("o n -> (o n)").partition_broadcast(P)).then_inc(c.gate_in.sem, 16)
                if not (layer == 0 and first):
                    wait_apart(sp, c.stored.sem, c.stored.at(b + off, 0))
                sp.dma_start(res[:, :, :], row(src, b)).then_inc(c.res_in.sem, 16)

            load_x(0)
            wt.load(sp, chunks)
            if layer == 0:
                sp.dma_start(bq[:, :], k.ins["L0_xcond_bq"].rearrange("(c p) -> p c", p=P), allow_slow_non_contiguous=True).then_inc(bq_in, 16)
                sp.dma_start(gate[:, :], k.ins["L0_xcond_bp"].partition_broadcast(P)).then_inc(c.gate_in.sem, 16)
            else:
                sp.dma_start(mask_u8[:, :], k.ins["mask_BxS2_bf1"].rearrange("b s -> (b s)").partition_broadcast(P)).then_inc(mask_in, 16)
            sp.wait_ge(keys_zeroed, 2)
            load_keys(0, 0)
            load_vals(0)
            load_x(1)
            load_x(2)
            load_keys(1, 1)
            sp.wait_ge(wt.low_done, len(chunks))
            load_res(0, first=True)
            load_x(3)
            with sp.Fori(0, (B - 4) // 2) as j:
                for i in range(2):
                    b = j * 2 + 1 + i
                    load_keys(b + 1, i)
                    load_vals(b)
                    load_x(b + 3)
                    load_res(b)
            for b in range(B - 3, B):
                if b + 1 < B:
                    load_keys(b + 1, (b + 1) % 2)
                load_vals(b)
                load_res(b)

        @block.gpsimd
        def _(pool):
            for n in range(2):
                pool.memset(keys[n][:, :, :], 0.0).then_inc(keys_zeroed, 1)
            if layer == 0:
                for q in (nm.var_eps_done, nm.rstd_done, c.probs, c.added):
                    pool.sem_inc(q.sem, q.credit)

            def norm(b, n):
                if n == NORM_STATS[-1]:
                    norm_rstd(pool, nm, bf, b + off, k.neg_half)

            def normalise(b, n):
                pool.wait_ge(c.inverted.sem, c.inverted.at(b + off, n + 1))
                pool.tensor_tensor(heads4(probs[:, n, :]), heads4(probs[:, n, :]), per_head(inv[:, n, :]), ALU.mult).then_inc(c.probs.sem, 1)

            def score(b, n, par):
                if n:
                    normalise(b, n - 1)
                if n == STEPS - 1:
                    normalise(b, n)

            def project_out(b, t):
                if t == 0:
                    pool.wait_ge(c.res_in.sem, c.res_in.at(b + off, 1))
                pool.wait_ge(c.gated.sem, c.gated.at(b + off, t + 1))
                pool.tensor_tensor(res[:, t, :], res[:, t, :], gated[:, t % 2, :], ALU.add).then_inc(c.added.sem, 1)
                if t == TT - 1:
                    pool.wait_ge(c.added.sem, c.added.at(b + off, TT))
                    pool.dma_start(row(dst, b), res[:, :, :]).then_inc(c.stored.sem, 16)

            schedule(pool, score, nothing, nothing, nothing, nothing, nothing, norm, nothing, project_out)
            pool.wait_ge(c.stored.sem, c.stored.at(B - 1 + off, 1))

        @block.scalar
        def _(act):
            if layer == 0:
                for q in (c.dense_out, nm.high, c.exped, c.turned_out, c.att_high):
                    act.sem_inc(q.sem, q.credit)
            wt.high(act, chunks)
            if layer == 0:
                act.wait_ge(bq_in, 16)

            def norm(b, step):
                n, ch = b + off, step - NORM_TURN - 1
                if 0 <= ch < KC:
                    if ch == 0:
                        act.wait_ge(nm.mod_done.sem, nm.mod_done.at(n, 1))
                    act.wait_ge(c.dense_mm.sem, c.dense_mm.at(n, ch + 1))
                    act.wait_ge(nm.low.sem, nm.low.at(n, ch + 1 - KC))
                    act.activation(full[:, ch, :], dense[ch % 2][:, :], ACT.Identity, bias=bf["mod"][:, 1, ch, :],
                                   scale=bf["mod"][:, 0, ch, :]).then_inc(c.dense_out.sem, 1)
                    act.wait_ge(c.dense_out.sem, c.dense_out.at(n, ch + 1))
                    act.copy(xh[:, ch, :], full[:, ch, :]).then_inc(nm.high.sem, 1)

            def query_out(b, m, par):
                act.wait_ge(c.dense_mm.sem, c.dense_mm.at(b + off, 5 + m))
                if layer == 0:
                    act.activation(queries[par][:, m, :], dense[m % 2][:, :], ACT.Identity, bias=bq[:, m:m + 1]).then_inc(c.dense_out.sem, 1)
                else:
                    act.copy(queries[par][:, m, :], dense[m % 2][:, :]).then_inc(c.dense_out.sem, 1)

            def score(b, n, par):
                n0 = b + off
                if n % HG == 0:
                    act.wait_ge(c.turned.sem, c.turned.at(n0, n + HG - STEPS))
                act.wait_ge(c.shifted.sem, c.shifted.at(n0, n + 1))
                act.activation(probs[:, n, :], scores[:, n % 4, :], ACT.Exp, scale=SCALE).then_inc(c.exped.sem, 1)

            def turn(b, h):
                n0 = b + off
                if h % HG == 0:
                    act.wait_ge(c.attended.sem, c.attended.at(n0, h // HG - 1))
                act.wait_ge(c.turned.sem, c.turned.at(n0, h + 1))
                act.copy(probs_t[h // HG % 2][:, h % HG, :], turn_ps[h % 2][0:L, :]).then_inc(c.turned_out.sem, 1)

            def attend_out(b, g, par):
                act.wait_ge(c.attended.sem, c.attended.at(b + off, g + 1))
                act.copy(ah[par][:, g, :], att_ps[:, :]).then_inc(c.att_high.sem, 1)

            schedule(act, score, turn, nothing, query_out, nothing, attend_out, norm, nothing, nothing)

        @block.vector
        def _(dve):
            if layer == 0:
                for q in (nm.stats_done, nm.mean_var, nm.normed, nm.mod_done, nm.low, c.row_max, c.shifted, c.summed,
                          c.inverted, c.att_low, c.gated):
                    dve.sem_inc(q.sem, q.credit)
            else:
                dve.sem_inc(c.masked.sem, c.masked.credit)
            wt.low(dve, chunks)
            if layer == 1:
                dve.wait_ge(mask_in, 16)
                dve.tensor_scalar(ctx_mask[:, :], mask_u8[:, :], BIG, -BIG, ALU.mult, ALU.add).then_inc(mask_done, 1)
                dve.wait_ge(mask_done, 1)

            def norm(b, step):
                n, ch = b + off, step - NORM_TURN - 2
                if step in NORM_STATS:
                    i = NORM_STATS.index(step)
                    norm_stats(dve, nm, bf, n, (2 * i, 2 * i + 1))
                if step == NORM_STATS[-1]:
                    mod_copy(dve, nm, bf, mod, b, n, c.dense_out, c.dense_out.at(n, KC - 8))
                if step in NORM_APPLY:
                    i = NORM_APPLY.index(step)
                    norm_apply(dve, nm, bf, n, (2 * i, 2 * i + 1))
                if 0 <= ch < KC:
                    dve.wait_ge(nm.high.sem, nm.high.at(n, ch + 1))
                    dve.tensor_tensor(xl[:, ch, :], full[:, ch, :], xh[:, ch, :].bitcast(F32), ALU.subtract).then_inc(nm.low.sem, 1)

            def invert(b, n):
                n0 = b + off
                dve.wait_ge(c.exped.sem, c.exped.at(n0, n + 1))
                dve.tensor_reduce(sums[:, n, :], heads4(probs[:, n, :]), AX_X, ALU.add).then_inc(c.summed.sem, 1)
                dve.wait_ge(c.summed.sem, c.summed.at(n0, n + 1))
                dve.wait_ge(c.probs.sem, c.probs.at(n0, n + 1 - STEPS))
                dve.reciprocal(inv[:, n, :], sums[:, n, :]).then_inc(c.inverted.sem, 1)

            def score(b, n, par):
                n0 = b + off
                if n == 0 and layer == 1:
                    dve.wait_ge(c.masked.sem, c.masked.at(b, 0))
                    dve.tensor_copy(mask[:, :], ctx_mask[:, bass.ds(b * L, L)]).then_inc(mask_done, 1)
                    dve.wait_ge(mask_done, b + 2)
                raw, out = heads4(score_ps[n % 2][:, 0:GL]), heads4(scores[:, n % 4, :])
                dve.wait_ge(c.scored.sem, c.scored.at(n0, n + 1))
                dve.wait_ge(c.exped.sem, c.exped.at(n0, n - 3))
                if layer == 1:
                    dve.tensor_tensor(out, raw, mask[:, :].unsqueeze(1).broadcast_to([P, HG, L]), ALU.add).then_inc(c.masked.sem, 1)
                    dve.wait_ge(c.masked.sem, c.masked.at(b, n + 1))
                    raw = out
                dve.tensor_reduce(mx[:, n % 2, :], raw, AX_X, ALU.max).then_inc(c.row_max.sem, 1)
                dve.wait_ge(c.row_max.sem, c.row_max.at(n0, n + 1))
                dve.tensor_tensor(out, raw, per_head(mx[:, n % 2, :]), ALU.subtract).then_inc(c.shifted.sem, 1)
                if n:
                    invert(b, n - 1)
                if n == STEPS - 1:
                    invert(b, n)

            def attend_out(b, g, par):
                dve.wait_ge(c.att_high.sem, c.att_high.at(b + off, g + 1))
                dve.tensor_tensor(al[par][:, g, :], att_ps[:, :], ah[par][:, g, :].bitcast(F32), ALU.subtract).then_inc(c.att_low.sem, 1)

            def project_out(b, t):
                n0 = b + off
                if t == 0:
                    dve.wait_ge(c.gate_in.sem, c.gate_in.at(0, 1) if layer == 0 else c.gate_in.at(b + 1, 1))
                dve.wait_ge(c.projected.sem, c.projected.at(n0, t + 1))
                dve.wait_ge(c.added.sem, c.added.at(n0, t - 1))
                dve.tensor_tensor(gated[:, t % 2, :], out_ps[:, :], gate[:, :], gate_op).then_inc(c.gated.sem, 1)

            schedule(dve, score, nothing, nothing, nothing, nothing, attend_out, norm, nothing, project_out)

        @block.tensor
        def _(pe):
            if layer == 0:
                for q in (c.dense_mm, c.scored, c.turned, c.attended, c.projected):
                    pe.sem_inc(q.sem, q.credit)
            pe.wait_ge(wt.low_done, len(chunks))

            def norm(b, step):
                n, ch = b + off, step - NORM_TURN
                if 0 <= ch < KC:
                    if ch == 0:
                        pe.wait_ge(nm.normed.sem, nm.normed.at(n, TT))
                    pe.wait_ge(c.dense_out.sem, c.dense_out.at(n, ch - 1))
                    for t in range(TT):
                        last = pe.transpose(dense[ch % 2][:, t * P:(t + 1) * P], bf["x"][:, t, ch * P:(ch + 1) * P], k.ident[:, :])
                    last.then_inc(c.dense_mm.sem, 1)

            def query(b, m, half):
                n = b + off
                if m == 0 and half == 0:
                    pe.wait_ge(nm.low.sem, nm.low.at(n, KC))
                if half == 0:
                    pe.wait_ge(c.dense_out.sem, c.dense_out.at(n, 4 + m - 1))
                last = split_matmul(pe, dense[m % 2][:, :], [(wqh[:, ch, m * P:(m + 1) * P], wql[:, ch, m * P:(m + 1) * P]) for ch in range(KC)],
                                    [(xh[:, ch, :], xl[:, ch, :]) for ch in range(KC)], half, 2)
                if half:
                    last.then_inc(c.dense_mm.sem, 1)

            def score(b, n, par):
                n0, g, t = b + off, n // HG, n % HG
                if n == 0:
                    pe.wait_ge(c.keys_in.sem, c.keys_in.at(n0, HG))
                if t == 0:
                    pe.wait_ge(c.dense_out.sem, c.dense_out.at(n0, 5 + g))
                freed, fn = (c.shifted, n0) if layer == 0 else (c.masked, b)
                pe.wait_ge(freed.sem, freed.at(fn, n - 1))
                pe.matmul(score_ps[n % 2][:, 0:GL], queries[par][:, g, t * P:(t + 1) * P], keys[par][:, g, :],
                          start=True, stop=True).then_inc(c.scored.sem, 1)

            def turn(b, h):
                n0, g, r = b + off, h // HG, h % HG
                if r == 0:
                    pe.wait_ge(c.probs.sem, c.probs.at(n0, 4 * g + 4))
                pe.wait_ge(c.turned_out.sem, c.turned_out.at(n0, h - 1))
                for t in range(TT):
                    last = pe.transpose(turn_ps[h % 2][0:L, t * P:(t + 1) * P], probs[:, 4 * g + t, r * L:(r + 1) * L], k.ident[:, :])
                last.then_inc(c.turned.sem, 1)

            def attend(b, g, par):
                n0 = b + off
                if g == 0:
                    pe.wait_ge(c.vals_in.sem, c.vals_in.at(n0, 1))
                pe.wait_ge(c.turned_out.sem, c.turned_out.at(n0, HG * g + HG))
                pe.wait_ge(c.att_low.sem, c.att_low.at(n0, g))
                for r in range(HG):
                    h = HG * g + r
                    last = pe.matmul(att_ps[HD * r:HD * r + HD, :], vals[:, h * HD:(h + 1) * HD], probs_t[g % 2][:, r, :],
                                     start=True, stop=True)
                last.then_inc(c.attended.sem, 1)

            def project(b, t, half, par):
                n0 = b + off
                if t == 0 and half == 0:
                    pe.wait_ge(c.att_low.sem, c.att_low.at(n0, NG))
                if half == 0:
                    pe.wait_ge(c.gated.sem, c.gated.at(n0, t))
                last = split_matmul(pe, out_ps[:, :], [(ah[par][:, ch, t * P:(t + 1) * P], al[par][:, ch, t * P:(t + 1) * P]) for ch in range(KC)],
                                    [(woh[:, ch, :], wol[:, ch, :]) for ch in range(KC)], half, 2)
                if half:
                    last.then_inc(c.projected.sem, 1)

            schedule(pe, score, turn, query, nothing, attend, nothing, norm, project, nothing)


HS = NG * 2 * HG
ROT = [(d + HD // 2) % HD for d in range(HD)]


def self_phase(nc, k, src, dst):
    with ExitStack() as ctx:
        def sb(name, shape, dt=F32):
            return ctx.enter_context(nc.sbuf_tensor("s_" + name, shape, dt))

        def ps(name):
            return ctx.enter_context(nc.psum_tensor("s_ps_" + name, [P, 512], F32))

        def count(name, per, unit=1, base=None):
            return Count(nc, ctx, "s_" + name, per, unit, base)

        mod = k.mod[1]
        nm = Norm(nc, ctx, "s")
        gate_in, res_in = count("gate_in", 1, 16), count("res_in", 1, 16)
        stored = count("stored", 1, 16, base=0)
        dense_mm = count("dense_mm", 16)
        act_dense = count("act_dense", 8)
        cos_done, shuffled = count("cos_done", 8), count("shuffled", 8)
        sin_done, roped = count("sin_done", 8), count("roped", 8)
        qk_high, qk_low = count("qk_high", 8), count("qk_low", 8)
        stack_in = [count(f"stack_in{w}", 12 * NG, 16) for w in range(2)]
        scored, masked, exped, inverted, probs_done = (count(x, 2 * HS) for x in ("scored", "masked", "exped", "inverted", "probs_done"))
        turned, turned_out = count("turned", 2 * HS), count("turned_out", 2 * HS)
        attended, att_out = count("attended", 2 * NG), count("att_out", 2 * NG)
        projected, gated_done, added = count("projected", TT), count("gated_done", TT), count("added", TT)
        mask_in, mask_done, rope_in, wo_in = (ctx.enter_context(nc.semaphore("s_" + x)) for x in ("mask_in", "mask_done", "rope_in", "wo_in"))

        bf = norm_buffers(sb)
        res = bf["x"]
        wh, wl = sb("wh", [P, KC, 3 * D], F32R), sb("wl", [P, KC, 3 * D], F32R)
        wo = sb("wo", [P, KC, D])
        full = sb("full", [P, 2, S])
        xh, xl = sb("xh", [P, KC, S], F32R), sb("xl", [P, KC, S], F32R)
        rope = sb("rope", [P, 2, S // 2])
        with_cos, swapped = sb("with_cos", [P, 2, S]), sb("swapped", [P, 2, S])
        parts = sb("parts", [P, 2, 2, S], F32R)
        stacks = [sb(f"stack{w}", [3 * HD, 2 * HG, S], F32R) for w in range(2)]
        vals = [sb(f"vals{n}", [P, TT, D]) for n in range(2)]
        mask_add = sb("mask_add", [P, TT, S], BF16)
        scores = sb("scores", [P, 2, S])
        low_score, sums, inv = sb("low_score", [P, PR]), sb("sums", [P, PR]), sb("inv", [P, PR])
        probs = sb("probs", [P, PR, S])
        probs_t = sb("probs_t", [P, HG, KC, S // 2])
        att = sb("att", [P, NG, S])
        gate, gated = sb("gate", [P, D]), sb("gated", [P, 2, D])
        mask_u8 = gated[:, 0, :].bitcast(U8).rearrange("p (t n) -> p t n", t=TT)
        dense, score_ps, turn_ps = [ps(f"dense{n}") for n in range(2)], [ps(f"score{n}") for n in range(2)], [ps(f"turn{n}") for n in range(2)]
        att_ps, out_ps = ps("att"), ps("out")
        wt = Weights(nc, ctx, "s", probs)
        w_qkv = k.ins["L1_xcond_qkv_W"]
        chunks = [(w_qkv[c * P:(c + 1) * P, j * D:(j + 1) * D], wh[:, c, j * D:(j + 1) * D], wl[:, c, j * D:(j + 1) * D],
                   -SCALE if j == 0 else 1.0) for j in range(3) for c in range(KC)]

        def schedule(eng, lag, head, tail, norm_in, norm_out, qk, value, project):
            def entry(b, par, before, after):
                for s in range(HS):
                    head(b, s)
                    if s >= lag:
                        tail(b, s - lag, par)
                    elif before:
                        tail(b - 1, s - lag + HS, 1 - par)
                    if s in (0, 1, 9, 11, 17, 19):
                        qk(b, s // 8 + 1, s // 2 % 2 if s > 1 and s != 9 and s != 17 else 0 if s != 1 else 1)
                    if before and s in (3, 4, 5):
                        for t in {3: (0, 1), 4: (2,), 5: (3,)}[s]:
                            project(b - 1, t)
                    if after and s == 16:
                        norm_in(b + 1)
                    if after and s == 20:
                        norm_out(b + 1)
                    if after and s in (25, 26):
                        qk(b + 1, 0, s - 25)
                    if after and 27 <= s <= 30:
                        value(b + 1, s - 27, 1 - par)
            norm_in(0)
            norm_out(0)
            qk(0, 0, 0)
            qk(0, 0, 1)
            for t in range(TT):
                value(0, t, 0)
            entry(0, 0, False, True)
            with eng.Fori(0, B // 2 - 1) as j:
                entry(j * 2 + 1, 1, True, True)
                entry(j * 2 + 2, 0, True, True)
            entry(B - 1, 1, True, False)
            for s in range(HS - lag, HS):
                tail(B - 1, s, 1)
            for t in range(TT):
                project(B - 1, t)

        def nothing(*_):
            pass

        def dense_slot(kind, i, w=0):
            return {"norm": i, "qk": 4 + w if i == 0 else 8 + 2 * i + w, "value": 6 + i}[kind]

        block = ctx.enter_context(nc.Block())

        @block.sync
        def _(sp):
            for q in (nm.x_in, gate_in, res_in, *stack_in):
                sp.sem_inc(q.sem, q.credit)

            def load_x(b):
                sp.dma_start(bf["x"][:, :, :], row(src, b)).then_inc(nm.x_in.sem, 16)

            def load_res(b):
                wait_apart(sp, gated_done.sem, gated_done.at(b, 0))
                sp.dma_start(gate[:, :], k.gates[0][bass.ds(b, 1), :].rearrange("o n -> (o n)").partition_broadcast(P)).then_inc(gate_in.sem, 16)
                sp.dma_start(res[:, :, :], row(src, b)).then_inc(res_in.sem, 16)

            def stack(b, g):
                for w in range(2):
                    wait_apart(sp, qk_low.sem, qk_low.at(b, 2 * g + w + 1))
                    wait_apart(sp, scored.sem, scored.at(b, 16 * (g - 1)))
                    for r in range(HG):
                        rows = slice(HD * r, HD * r + HD)
                        for n, part in enumerate(((0, 0, 1), (0, 1, 0))[w]):
                            sp.dma_start(stacks[w][HD * n:HD * n + HD, g % 2 * HG + r, :].bitcast(F32),
                                         parts[rows, w, part, :].bitcast(F32)).then_inc(stack_in[w].sem, 16)

            def entry(b, first, last):
                stack(b, 1)
                if first:
                    wait_apart(sp, act_dense.sem, act_dense.at(b, KC))
                else:
                    wait_apart(sp, stored.sem, stored.at(b - 1, 1))
                if last:
                    load_res(b)
                else:
                    load_x(b + 1)
                stack(b, 2)
                stack(b, 3)
                if not last:
                    wait_apart(sp, act_dense.sem, act_dense.at(b + 1, KC))
                    load_res(b)
                    stack(b + 1, 0)

            load_x(0)
            wt.load(sp, chunks)
            sp.dma_start(mask_u8[:, :, :], k.ins["mask_SxS_bk0"].rearrange("(t p) n -> p t n", p=P)).then_inc(mask_in, 16)
            sp.dma_start(rope[:, :, :], k.rope.rearrange("o p n -> p o n")).then_inc(rope_in, 16)
            sp.dma_start(wo[:, :, :], k.ins["L1_xcond_attn_out_W"].rearrange("(k p) n -> p k n", p=P)).then_inc(wo_in, 16)
            stack(0, 0)
            entry(0, True, False)
            with sp.Fori(1, B - 1) as b:
                entry(b, False, False)
            entry(B - 1, False, True)

        @block.gpsimd
        def _(pool):
            for q in (nm.var_eps_done, nm.rstd_done, sin_done, roped, probs_done, added):
                pool.sem_inc(q.sem, q.credit)
            pool.wait_ge(rope_in, 16)
            sin = rope[:, 1, :].unsqueeze(1).broadcast_to([P, 2, S // 2])

            def norm_in(b):
                norm_rstd(pool, nm, bf, b, k.neg_half)

            def qk(b, g, w):
                i = 2 * g + w
                sw = swapped[:, w, :].rearrange("p (a n) -> p a n", a=2)
                pool.wait_ge(shuffled.sem, shuffled.at(b, i + 1))
                pool.tensor_tensor(sw, sw, sin, ALU.mult).then_inc(sin_done.sem, 1)
                pool.wait_ge(sin_done.sem, sin_done.at(b, i + 1))
                pool.wait_ge(cos_done.sem, cos_done.at(b, i + 1))
                pool.tensor_tensor(with_cos[:, w, :], with_cos[:, w, :], swapped[:, w, :], ALU.add).then_inc(roped.sem, 1)

            def tail(b, s, par):
                for n in (2 * s, 2 * s + 1):
                    tile = probs[:, n % PR, :]
                    wait_apart(pool, inverted.sem, inverted.at(b, n + 1))
                    pool.tensor_scalar(tile, tile, inv[:, n % PR:n % PR + 1], 0.0, ALU.mult, ALU.add).then_inc(probs_done.sem, 1)

            def project(b, t):
                if t == 0:
                    pool.wait_ge(res_in.sem, res_in.at(b, 1))
                pool.wait_ge(gated_done.sem, gated_done.at(b, t + 1))
                pool.tensor_tensor(res[:, t, :], res[:, t, :], gated[:, t % 2, :], ALU.add).then_inc(added.sem, 1)
                if t == TT - 1:
                    pool.wait_ge(added.sem, added.at(b, TT))
                    pool.dma_start(row(dst, b), res[:, :, :]).then_inc(stored.sem, 16)

            schedule(pool, 1, nothing, tail, norm_in, nothing, qk, nothing, project)
            pool.wait_ge(stored.sem, stored.at(B - 1, 1))

        @block.scalar
        def _(act):
            for q in (act_dense, exped, turned_out, att_out):
                act.sem_inc(q.sem, q.credit)
            wt.high(act, chunks)

            def norm_out(b):
                act.wait_ge(nm.mod_done.sem, nm.mod_done.at(b, 1))
                for ch in range(KC):
                    act.wait_ge(dense_mm.sem, dense_mm.at(b, dense_slot("norm", ch) + 1))
                    act.wait_ge(nm.low.sem, nm.low.at(b, ch - 1))
                    act.activation(full[:, ch % 2, :], dense[ch % 2][:, :], ACT.Identity, bias=bf["mod"][:, 1, ch, :],
                                   scale=bf["mod"][:, 0, ch, :]).then_inc(act_dense.sem, 1)

            def value(b, t, par):
                u = dense_slot("value", t)
                act.wait_ge(dense_mm.sem, dense_mm.at(b, u + 1))
                act.copy(vals[par][:, t, :], dense[u % 2][:, :]).then_inc(act_dense.sem, 1)

            def head(b, s):
                act.wait_ge(turned.sem, turned.at(b, 2 * s - PR + 2))
                for n in (2 * s, 2 * s + 1):
                    act.wait_ge(masked.sem, masked.at(b, n + 1))
                    act.wait_ge(inverted.sem, inverted.at(b, n + 1 - PR))
                    act.activation(probs[:, n % PR, :], scores[:, n % 2, :], ACT.Exp, bias=low_score[:, n % PR:n % PR + 1], scale=-1.0,
                                   accum_out=sums[:, n % PR:n % PR + 1]).then_inc(exped.sem, 1)

            def tail(b, s, par):
                slot, r = s // HG, s % HG
                act.wait_ge(attended.sem, attended.at(b, slot))
                for i in range(2):
                    act.wait_ge(turned.sem, turned.at(b, 2 * s + i + 1))
                    act.copy(probs_t[:, r, 2 * i:2 * i + 2, :], turn_ps[i][:, :].rearrange("p (c n) -> p c n", c=2)).then_inc(turned_out.sem, 1)
                if r == HG - 1:
                    act.wait_ge(attended.sem, attended.at(b, slot + 1))
                    half = slot % 2 * (S // 2)
                    act.copy(att[:, slot // 2, half:half + S // 2], att_ps[:, 0:S // 2]).then_inc(att_out.sem, 1)

            schedule(act, LAG, head, tail, nothing, norm_out, nothing, value, nothing)

        @block.vector
        def _(dve):
            for q in (nm.stats_done, nm.mean_var, nm.normed, nm.mod_done, nm.high, nm.low, cos_done, shuffled, qk_high, qk_low,
                      masked, inverted, gated_done):
                dve.sem_inc(q.sem, q.credit)
            wt.low(dve, chunks)
            dve.wait_ge(mask_in, 16)
            dve.tensor_scalar(mask_add[:, :, :], mask_u8[:, :, :], -BIG16, BIG16, ALU.mult, ALU.add).then_inc(mask_done, 1)
            dve.wait_ge(mask_done, 1)
            dve.wait_ge(rope_in, 16)
            cos = rope[:, 0, :].unsqueeze(1).broadcast_to([P, 2, S // 2])

            def norm_in(b):
                norm_stats(dve, nm, bf, b)
                mod_copy(dve, nm, bf, mod, b, b, act_dense, act_dense.at(b, KC - 8))
                norm_apply(dve, nm, bf, b)

            def norm_out(b):
                dve.wait_ge(dense_mm.sem, dense_mm.at(b, 0))
                for ch in range(KC):
                    dve.wait_ge(act_dense.sem, act_dense.at(b, ch + 1))
                    split(dve, nm, b, ch, full[:, ch % 2, :], xh[:, ch, :], xl[:, ch, :])

            def qk(b, g, w):
                i, u = 2 * g + w, dense_slot("qk", g, w)
                dve.wait_ge(dense_mm.sem, dense_mm.at(b, u + 1))
                dve.wait_ge(qk_low.sem, qk_low.at(b, i - 1))
                dve.tensor_tensor(with_cos[:, w, :].rearrange("p (a n) -> p a n", a=2),
                                  dense[u % 2][:, :].rearrange("p (a n) -> p a n", a=2), cos, ALU.mult).then_inc(cos_done.sem, 1)
                dve.stream_shuffle(swapped[:, w, :], dense[u % 2][:, :], ROT).then_inc(shuffled.sem, 1)

            def qk_split(b, g, w):
                i = 2 * g + w
                dve.wait_ge(roped.sem, roped.at(b, i + 1))
                dve.wait_ge(stack_in[w].sem, stack_in[w].at(b, 12 * g))
                dve.tensor_copy(parts[:, w, 0, :], with_cos[:, w, :]).then_inc(qk_high.sem, 1)
                dve.wait_ge(qk_high.sem, qk_high.at(b, i + 1))
                dve.tensor_tensor(parts[:, w, 1, :], with_cos[:, w, :], parts[:, w, 0, :].bitcast(F32), ALU.subtract).then_inc(qk_low.sem, 1)

            def qk_both(b, g, w):
                qk(b, g, w)
                if w == 1:
                    qk_split(b, g, 0)
                    qk_split(b, g, 1)

            def head(b, s):
                half = s // HG % 2
                for n in (2 * s, 2 * s + 1):
                    dve.wait_ge(scored.sem, scored.at(b, n + 1))
                    wait_apart(dve, exped.sem, exped.at(b, n - 1))
                    dve.tensor_tensor_reduce(scores[:, n % 2, :], score_ps[n % 2][:, :], mask_add[:, 2 * half + n % 2, :], 1.0, BIG,
                                             ALU.add, ALU.min, low_score[:, n % PR:n % PR + 1]).then_inc(masked.sem, 1)

            def tail(b, s, par):
                for n in (2 * s, 2 * s + 1):
                    dve.wait_ge(exped.sem, exped.at(b, n + 1))
                    dve.wait_ge(probs_done.sem, probs_done.at(b, n + 1 - PR))
                    dve.reciprocal(inv[:, n % PR:n % PR + 1], sums[:, n % PR:n % PR + 1]).then_inc(inverted.sem, 1)

            def project(b, t):
                if t == 0:
                    dve.wait_ge(gate_in.sem, gate_in.at(b, 1))
                dve.wait_ge(projected.sem, projected.at(b, t + 1))
                dve.wait_ge(added.sem, added.at(b, t - 1))
                dve.tensor_tensor(gated[:, t % 2, :], out_ps[:, :], gate[:, :], ALU.mult).then_inc(gated_done.sem, 1)

            schedule(dve, 1, head, tail, norm_in, norm_out, qk_both, nothing, project)

        @block.tensor
        def _(pe):
            for q in (dense_mm, scored, turned, attended, projected):
                pe.sem_inc(q.sem, q.credit)
            pe.wait_ge(wt.low_done, len(chunks))
            pe.wait_ge(wo_in, 16)

            def dense_free(b, u):
                prev = u - 2
                if prev < 4 and prev >= 0:
                    pe.wait_ge(act_dense.sem, act_dense.at(b, prev + 1))
                elif 6 <= prev < 10:
                    pe.wait_ge(act_dense.sem, act_dense.at(b, prev - 1))
                elif prev < 0:
                    pe.wait_ge(shuffled.sem, shuffled.at(b, prev + 1))
                else:
                    pe.wait_ge(shuffled.sem, shuffled.at(b, prev - 3 if prev < 6 else prev - 7))

            def norm_out(b):
                pe.wait_ge(nm.normed.sem, nm.normed.at(b, TT))
                for ch in range(KC):
                    dense_free(b, ch)
                    for t in range(TT):
                        last = pe.transpose(dense[ch % 2][:, t * P:(t + 1) * P], bf["x"][:, t, ch * P:(ch + 1) * P], k.ident[:, :])
                    last.then_inc(dense_mm.sem, 1)

            def qk(b, g, w):
                u, c0 = dense_slot("qk", g, w), w * D + g * P
                pe.wait_ge(nm.low.sem, nm.low.at(b, KC))
                dense_free(b, u)
                split_matmul(pe, dense[u % 2][:, :], [(wh[:, ch, c0:c0 + P], wl[:, ch, c0:c0 + P]) for ch in range(KC)],
                             [(xh[:, ch, :], xl[:, ch, :]) for ch in range(KC)]).then_inc(dense_mm.sem, 1)

            def value(b, t, par):
                u = dense_slot("value", t)
                dense_free(b, u)
                split_matmul(pe, dense[u % 2][:, :], [(xh[:, ch, t * P:(t + 1) * P], xl[:, ch, t * P:(t + 1) * P]) for ch in range(KC)],
                             [(wh[:, ch, 2 * D:3 * D], wl[:, ch, 2 * D:3 * D]) for ch in range(KC)]).then_inc(dense_mm.sem, 1)

            def head(b, s):
                g, half, r = s // (2 * HG), s // HG % 2, s % HG
                if s % (2 * HG) == 0:
                    for w in range(2):
                        pe.wait_ge(stack_in[w].sem, stack_in[w].at(b, 12 * (g + 1)))
                for n in (2 * s, 2 * s + 1):
                    pe.wait_ge(masked.sem, masked.at(b, n - 1))
                    t, slot = 2 * half + n % 2, g % 2 * HG + r
                    pe.matmul(score_ps[n % 2][:, :], stacks[0][:, slot, t * P:(t + 1) * P], stacks[1][:, slot, :],
                              start=True, stop=True).then_inc(scored.sem, 1)

            def tail(b, s, par):
                slot, r = s // HG, s % HG
                pe.wait_ge(probs_done.sem, probs_done.at(b, 2 * s + 2))
                for i in range(2):
                    pe.wait_ge(turned_out.sem, turned_out.at(b, 2 * s + i - 1))
                    for ch in (2 * i, 2 * i + 1):
                        for j in range(2):
                            c0 = ch % 2 * (S // 2) + j * P
                            last = pe.transpose(turn_ps[i][:, c0:c0 + P], probs[:, (2 * s + j) % PR, ch * P:(ch + 1) * P], k.ident[:, :])
                    last.then_inc(turned.sem, 1)
                if r == HG - 1:
                    g = slot // 2
                    pe.wait_ge(turned_out.sem, turned_out.at(b, 2 * HG * (slot + 1)))
                    pe.wait_ge(act_dense.sem, act_dense.at(b, 8))
                    pe.wait_ge(att_out.sem, att_out.at(b, slot))
                    for ch in range(KC):
                        for h in range(HG):
                            last = pe.matmul(att_ps[HD * h:HD * h + HD, 0:S // 2], vals[par][:, ch, (HG * g + h) * HD:(HG * g + h + 1) * HD],
                                             probs_t[:, h, ch, :], start=ch == 0, stop=ch == KC - 1)
                    last.then_inc(attended.sem, 1)

            def project(b, t):
                pe.wait_ge(att_out.sem, att_out.at(b, 2 * NG))
                pe.wait_ge(gated_done.sem, gated_done.at(b, t))
                for ch in range(KC):
                    last = pe.matmul(out_ps[:, :], att[:, ch, t * P:(t + 1) * P], wo[:, ch, :], start=ch == 0, stop=ch == KC - 1)
                last.then_inc(projected.sem, 1)

            schedule(pe, LAG, head, tail, nothing, norm_out, qk, value, project)


def mlp_phase(nc, k, src, dst):
    with ExitStack() as ctx:
        def sb(name, shape, dt=F32):
            return ctx.enter_context(nc.sbuf_tensor("m_" + name, shape, dt))

        def ps(name):
            return ctx.enter_context(nc.psum_tensor("m_ps_" + name, [P, 512], F32))

        def count(name, per, unit=1, base=None):
            return Count(nc, ctx, "m_" + name, per, unit, base)

        mod, mlag, ring = k.mod[3], 3, 4
        nm = Norm(nc, ctx, "m")
        gate_in, res_in, stored = count("gate_in", 1, 16), count("res_in", 1, 16), count("stored", 1, 16, base=0)
        norm_t, full_done = count("norm_t", KC), count("full_done", KC)
        hidden, gelu_done, h_high, h_low, summed = (count(x, NF) for x in ("hidden", "gelu_done", "h_high", "h_low", "summed"))
        bias_done, gated_done, biased, added = count("bias_done", 1), count("gated_done", TT), count("biased", TT), count("added", TT)
        b_in = ctx.enter_context(nc.semaphore("m_b_in"))

        bf = norm_buffers(sb)
        w1h, w1l = sb("w1h", [P, KC, FF], F32R), sb("w1l", [P, KC, FF], F32R)
        w2h, w2l = sb("w2h", [P, NF, D], F32R), sb("w2l", [P, NF, D], F32R)
        full = sb("full", [P, KC, S])
        xh, xl = sb("xh", [P, KC, S], F32R), sb("xl", [P, KC, S], F32R)
        hid = sb("hid", [P, 2, S])
        hh, hl = sb("hh", [P, ring, S], F32R), sb("hl", [P, ring, S], F32R)
        gate, gate_bias, b2 = sb("gate", [P, D]), sb("gate_bias", [P, D]), sb("b2", [P, D])
        gated = sb("gated", [P, 2, D])
        res = sb("res", [P, TT, D])
        b1 = sb("b1", [P, NF])
        hid_ps, norm_ps, out_ps = [ps(f"hid{n}") for n in range(2)], [ps(f"norm{n}") for n in range(2)], [ps(f"out{n}") for n in range(TT)]
        wt = Weights(nc, ctx, "m", res)
        w1, w2 = k.ins["L1_xcond_mlp_W1"], k.ins["L1_xcond_mlp_W2"]
        chunks = [(w1[c * P:(c + 1) * P, j * D:(j + 1) * D], w1h[:, c, j * D:(j + 1) * D], w1l[:, c, j * D:(j + 1) * D], 1.0)
                  for j in range(FF // D) for c in range(KC)]
        chunks += [(w2[f * P:(f + 1) * P, :], w2h[:, f, :], w2l[:, f, :], 1.0) for f in range(NF)]

        def schedule(eng, norm_in, norm_t_, norm_split, up, down, finish):
            def entry(b, after):
                for f in range(NF):
                    up(b, f)
                    if f >= mlag:
                        down(b, f - mlag)
                    if after and f == 6:
                        norm_in(b + 1)
                    if after and f == 10:
                        norm_t_(b + 1)
                if after:
                    norm_split(b + 1)
                for f in range(NF - mlag, NF):
                    down(b, f)
                finish(b)
            norm_in(0)
            norm_t_(0)
            norm_split(0)
            with eng.Fori(0, B - 1) as b:
                entry(b, True)
            entry(B - 1, False)

        def nothing(*_):
            pass

        block = ctx.enter_context(nc.Block())

        @block.sync
        def _(sp):
            for q in (nm.x_in, gate_in, res_in):
                sp.sem_inc(q.sem, q.credit)

            def load_x(b):
                wait_apart(sp, full_done.sem, full_done.at(b, 0))
                sp.dma_start(bf["x"][:, :, :], row(src, b)).then_inc(nm.x_in.sem, 16)

            def load_res(b, first=False):
                wait_apart(sp, gated_done.sem, gated_done.at(b, 0))
                sp.dma_start(gate[:, :], k.gates[2][bass.ds(b, 1), :].rearrange("o n -> (o n)").partition_broadcast(P)).then_inc(gate_in.sem, 16)
                if not first:
                    wait_apart(sp, stored.sem, stored.at(b, 0))
                sp.dma_start(res[:, :, :], row(src, b)).then_inc(res_in.sem, 16)

            load_x(0)
            sp.dma_start(b1[:, :], k.ins["L1_xcond_mlp_b1"].rearrange("(c p) -> p c", p=P), allow_slow_non_contiguous=True).then_inc(b_in, 16)
            sp.dma_start(b2[:, :], k.ins["L1_xcond_mlp_b2"].partition_broadcast(P)).then_inc(b_in, 16)
            wt.load(sp, chunks)
            sp.wait_ge(wt.low_done, len(chunks))
            load_res(0, first=True)
            load_x(1)
            with sp.Fori(1, B - 1) as b:
                load_res(b)
                load_x(b + 1)
            load_res(B - 1)

        @block.gpsimd
        def _(pool):
            for q in (nm.var_eps_done, nm.rstd_done, added):
                pool.sem_inc(q.sem, q.credit)

            def finish(b):
                pool.wait_ge(res_in.sem, res_in.at(b, 1))
                for t in range(TT):
                    pool.wait_ge(biased.sem, biased.at(b, t + 1))
                    pool.tensor_tensor(res[:, t, :], res[:, t, :], gated[:, t % 2, :], ALU.add).then_inc(added.sem, 1)
                pool.wait_ge(added.sem, added.at(b, TT))
                pool.dma_start(row(dst, b), res[:, :, :]).then_inc(stored.sem, 16)

            schedule(pool, lambda b: norm_rstd(pool, nm, bf, b, k.neg_half), nothing, nothing, nothing, nothing, finish)
            pool.wait_ge(stored.sem, stored.at(B - 1, 1))

        @block.scalar
        def _(act):
            for q in (full_done, gelu_done):
                act.sem_inc(q.sem, q.credit)
            wt.high(act, chunks)
            act.wait_ge(b_in, 32)

            def norm_t_(b):
                act.wait_ge(nm.mod_done.sem, nm.mod_done.at(b, 1))
                act.wait_ge(nm.low.sem, nm.low.at(b, 0))
                for ch in range(KC):
                    act.wait_ge(norm_t.sem, norm_t.at(b, ch + 1))
                    act.activation(full[:, ch, :], norm_ps[ch % 2][:, :], ACT.Identity, bias=bf["mod"][:, 1, ch, :],
                                   scale=bf["mod"][:, 0, ch, :]).then_inc(full_done.sem, 1)

            def up(b, f):
                act.wait_ge(hidden.sem, hidden.at(b, f + 1))
                act.wait_ge(h_low.sem, h_low.at(b, f - 1))
                act.activation(hid[:, f % 2, :], hid_ps[f % 2][:, :], ACT.Gelu_apprx_tanh, bias=b1[:, f:f + 1]).then_inc(gelu_done.sem, 1)

            schedule(act, nothing, norm_t_, nothing, up, nothing, nothing)

        @block.vector
        def _(dve):
            for q in (nm.stats_done, nm.mean_var, nm.normed, nm.mod_done, nm.high, nm.low, h_high, h_low, bias_done, gated_done, biased):
                dve.sem_inc(q.sem, q.credit)
            wt.low(dve, chunks)
            dve.wait_ge(b_in, 32)

            def norm_in(b):
                norm_stats(dve, nm, bf, b)
                mod_copy(dve, nm, bf, mod, b, b, full_done, full_done.at(b, 0))
                norm_apply(dve, nm, bf, b)

            def norm_split(b):
                dve.wait_ge(hidden.sem, hidden.at(b, 0))
                for ch in range(KC):
                    dve.wait_ge(full_done.sem, full_done.at(b, ch + 1))
                    split(dve, nm, b, ch, full[:, ch, :], xh[:, ch, :], xl[:, ch, :])

            def up(b, f):
                dve.wait_ge(gelu_done.sem, gelu_done.at(b, f + 1))
                dve.wait_ge(summed.sem, summed.at(b, f + 1 - ring))
                dve.tensor_copy(hh[:, f % ring, :], hid[:, f % 2, :]).then_inc(h_high.sem, 1)
                dve.wait_ge(h_high.sem, h_high.at(b, f + 1))
                dve.tensor_tensor(hl[:, f % ring, :], hid[:, f % 2, :], hh[:, f % ring, :].bitcast(F32), ALU.subtract).then_inc(h_low.sem, 1)

            def finish(b):
                dve.wait_ge(gate_in.sem, gate_in.at(b, 1))
                dve.tensor_tensor(gate_bias[:, :], gate[:, :], b2[:, :], ALU.mult).then_inc(bias_done.sem, 1)
                dve.wait_ge(bias_done.sem, bias_done.at(b, 1))
                dve.wait_ge(summed.sem, summed.at(b, NF))
                for t in range(TT):
                    dve.wait_ge(added.sem, added.at(b, t - 1))
                    dve.tensor_tensor(gated[:, t % 2, :], out_ps[t][:, :], gate[:, :], ALU.mult).then_inc(gated_done.sem, 1)
                    dve.wait_ge(gated_done.sem, gated_done.at(b, t + 1))
                    dve.tensor_tensor(gated[:, t % 2, :], gated[:, t % 2, :], gate_bias[:, :], ALU.add).then_inc(biased.sem, 1)

            schedule(dve, norm_in, nothing, norm_split, up, nothing, finish)

        @block.tensor
        def _(pe):
            for q in (norm_t, hidden, summed):
                pe.sem_inc(q.sem, q.credit)

            def norm_t_(b):
                pe.wait_ge(nm.normed.sem, nm.normed.at(b, TT))
                for ch in range(KC):
                    pe.wait_ge(full_done.sem, full_done.at(b, ch - 1))
                    for t in range(TT):
                        last = pe.transpose(norm_ps[ch % 2][:, t * P:(t + 1) * P], bf["x"][:, t, ch * P:(ch + 1) * P], k.ident[:, :])
                    last.then_inc(norm_t.sem, 1)

            def up(b, f):
                if f == 0:
                    pe.wait_ge(nm.low.sem, nm.low.at(b, KC))
                pe.wait_ge(gelu_done.sem, gelu_done.at(b, f - 1))
                split_matmul(pe, hid_ps[f % 2][:, :], [(w1h[:, ch, f * P:(f + 1) * P], w1l[:, ch, f * P:(f + 1) * P]) for ch in range(KC)],
                             [(xh[:, ch, :], xl[:, ch, :]) for ch in range(KC)]).then_inc(hidden.sem, 1)

            def down(b, f):
                pe.wait_ge(h_low.sem, h_low.at(b, f + 1))
                for t in range(TT):
                    if f == 0:
                        pe.wait_ge(gated_done.sem, gated_done.at(b, t + 1 - TT))
                    for n, (a, c) in enumerate(((hh, w2h), (hh, w2l), (hl, w2h))):
                        last = pe.matmul(out_ps[t][:, :], a[:, f % ring, t * P:(t + 1) * P], c[:, f, :],
                                         start=f == 0 and n == 0, stop=f == NF - 1 and n == 2)
                last.then_inc(summed.sem, 1)

            pe.wait_ge(wt.low_done, len(chunks))
            schedule(pe, nothing, norm_t_, nothing, up, down, nothing)




def rope_tables():
    inv_freq = 1.0 / 10000.0 ** (np.arange(0, HD, 2, dtype=np.float32) / HD)
    freqs = np.outer(np.arange(S // 2, dtype=np.float32), inv_freq)
    emb = np.concatenate([freqs, freqs], axis=-1)
    cos, sin = np.cos(emb).astype(np.float32), np.sin(emb).astype(np.float32)
    sign = np.where(np.arange(HD) < HD // 2, np.float32(-1), np.float32(1))
    return np.ascontiguousarray(np.stack([np.tile(cos.T, (HG, 1)), np.tile((sin * sign).T, (HG, 1))]))


def program(nc, ins, rope, out):
    with ExitStack() as ctx:
        PASSED.clear()
        k = Kernel()
        k.ins, k.rope, k.out = ins, rope, out
        k.gates = nc.dram_tensor("gates", (3, B, D), F32).ap()
        k.keys = nc.dram_tensor("ctx_keys", (2, B, NG, P, L), F32).ap()
        k.vals = nc.dram_tensor("ctx_vals", (2, B * L, D), F32).ap()
        k.x1 = nc.dram_tensor("x_after_cross0", (B, S, D), F32).ap()
        k.x2 = nc.dram_tensor("x_after_self", (B, S, D), F32).ap()
        k.x3 = nc.dram_tensor("x_after_cross1", (B, S, D), F32).ap()
        k.ident = ctx.enter_context(nc.sbuf_tensor("ident", [P, P], F32))
        k.neg_half = ctx.enter_context(nc.sbuf_tensor("neg_half", [P, TT], F32))
        k.mod = [ctx.enter_context(nc.sbuf_tensor(f"mod{n}", [P, 2, KC, B], F32)) for n in range(4)]
        for e in (nc.sync, nc.vector, nc.gpsimd):
            PASSED[e.engine] = ctx.enter_context(nc.semaphore(f"passed_{len(PASSED)}"))
        prologue(nc, k)
        c = CrossCounts(nc, ctx)
        cross_phase(nc, k, c, 0, ins["x"], k.x1)
        self_phase(nc, k, k.x1, k.x2)
        cross_phase(nc, k, c, 1, k.x2, k.x3)
        mlp_phase(nc, k, k.x3, out)


def kernel(**inputs):
    import concourse.bacc as bacc
    from concourse.bass_utils import run_bass_kernel_spmd

    nc = bacc.Bacc("TRN2", target_bir_lowering=False, num_devices=1)
    arrays, ins = {}, {}
    for name, a in inputs.items():
        a = np.ascontiguousarray(a)
        arrays[name] = a
        ins[name] = nc.dram_tensor(name, a.shape, mybir.dt.from_np(a.dtype), kind="ExternalInput").ap()
    arrays["rope"] = rope_tables()
    rope = nc.dram_tensor("rope", arrays["rope"].shape, F32, kind="ExternalInput").ap()
    out = nc.dram_tensor("out", (B, S, D), F32, kind="ExternalOutput").ap()
    program(nc, ins, rope, out)
    r = run_bass_kernel_spmd(nc, [arrays], core_ids=[0])
    return r.results[0]["out"]
```

```python
from contextlib import ExitStack

import numpy as np

import concourse.bass as bass
from concourse import mybir

F32 = mybir.dt.float32
F32R = mybir.dt.float32r
BF16 = mybir.dt.bfloat16
U8 = mybir.dt.uint8
ALU = mybir.AluOpType
ACT = mybir.ActivationFunctionType
AX_X = mybir.AxisListType.X

P = 128
B = 8
S = 512
D = 512
L = 77
NH = 16
HD = D // NH
KC = D // P
TT = S // P
HG = P // HD
NG = NH // HG
GL = HG * L
FF = 4 * D
NF = FF // P
EPS = 1e-5
SCALE = float(HD) ** -0.5
BIG = float(np.finfo(np.float32).max)
BIG16 = 3.3895313892515355e38
LAG = 3
PR = 8
STEPS = NG * TT
TURN_LAG = HG + 2
ATTEND_LAG = TURN_LAG + HG
PROJECT_AT = 7
NORM_STATS = (1, 3)
NORM_APPLY = (5, 6)
NORM_TURN = 8


class Count:

    def __init__(self, nc, ctx, name, per, unit=1, base=None):
        self.sem = ctx.enter_context(nc.semaphore(name))
        self.per, self.unit, self.base = per, unit, per if base is None else base

    @property
    def credit(self):
        return self.base * self.unit

    def at(self, b, k):
        return (b * self.per + (self.base + k)) * self.unit


PASSED = {}


def wait_apart(eng, sem, value):
    eng.wait_ge(sem, value)
    eng.sem_inc(PASSED[eng.engine], 1)


def one(ap3):
    return ap3.rearrange("o p d -> (o p) d")


def row(x, b):
    return one(x[bass.ds(b, 1)]).rearrange("(t p) d -> p t d", p=P)


def split_matmul(pe, out, lhs, rhs, part=0, parts=1):
    terms = [(a, c) for (ah, al), (ch, cl) in zip(lhs, rhs) for a, c in ((ah, ch), (ah, cl), (al, ch))]
    size = len(terms) // parts
    for n in range(part * size, part * size + size):
        a, c = terms[n]
        last = pe.matmul(out, a, c, start=n == 0, stop=n == len(terms) - 1)
    return last


class Kernel:
    pass


def prologue(nc, k):
    with ExitStack() as ctx:
        def sb(name, shape, dt=F32):
            return ctx.enter_context(nc.sbuf_tensor("p_" + name, shape, dt))

        def ps(name):
            return ctx.enter_context(nc.psum_tensor("p_ps_" + name, [P, 512], F32))

        used = []

        def sem(name):
            used.append(ctx.enter_context(nc.semaphore("p_" + name)))
            return used[-1]

        cond = sb("cond", [B, 2, D])
        cond_t = sb("cond_t", [P, 2, KC, 32])
        bias_rows = sb("bias_rows", [P, 4, D])
        mod_rows = sb("mod_rows", [P, 4, D])
        mod_cols = sb("mod_cols", [P, 4, KC, P])
        norm_w = sb("norm_w", [P, 3, KC])
        kv_mod = sb("kv_mod", [P, 2, KC, B])
        ring = [sb(f"w{n}", [P, KC, D]) for n in range(8)]
        wkv = sb("wkv", [P, KC, 2 * D])
        ck, cv = sb("ck", [P, KC, D]), sb("cv", [P, KC, D])
        ctx_raw = sb("ctx_raw", [L, B, D])
        ctx_nn = sb("ctx_nn", [L, B, D])
        ctx_t = sb("ctx_t", [P, 2, KC, B * L])
        stats = sb("stats", [L, B, 6])
        mv = sb("mv", [L, B, 2])
        rstd = sb("rstd", [L, B])
        var_eps = sb("var_eps", [L, B])
        half_l = sb("half_l", [L, B])
        bk = sb("bk", [P, KC])
        bv_rows = sb("bv_rows", [P, D])
        keys = sb("keys", [P, 8, 4 * L])
        vals = sb("vals", [P, 5, D])
        acc = [ps(f"acc{n}") for n in range(4)]
        tp = [ps(f"tp{n}") for n in range(4)]

        NB = 13
        cond_in, cond_silu, small_in, zeroed, ident_z = (sem(x) for x in ("cond_in", "cond_silu", "small_in", "zeroed", "ident_z"))
        bias_in, ctx_in, wkv_in, ck_in, cv_in = (sem(x) for x in ("bias_in", "ctx_in", "wkv_in", "ck_in", "cv_in"))
        w_in = [sem(f"w_in{n}") for n in range(8)]
        cond_tp, cond_td, rows_mm, rows_done, cols_tp, cols_done = (
            sem(x) for x in ("cond_tp", "cond_td", "rows_mm", "rows_done", "cols_tp", "cols_done"))
        mods, st_done, mv_done, ve_done, rstd_done, ctx_normed = (
            sem(x) for x in ("mods", "st_done", "mv_done", "ve_done", "rstd_done", "ctx_normed"))
        ctx_tp, ctx_raw_done, ctx_a, ctx_td = (sem(x) for x in ("ctx_tp", "ctx_raw_done", "ctx_a", "ctx_td"))
        k_mm, k_evac, v_mm, v_evac, gates_out = (sem(x) for x in ("k_mm", "k_evac", "v_mm", "v_evac", "gates_out"))
        k_out, v_out = sem("k_out"), sem("v_out")

        blocks = []
        for w, bias, n, src in (("L0_xcond_Wss_q", "L0_xcond_bss_q", 2, 0), ("L0_xcond_Wss_kv", "L0_xcond_bss_kv", 2, 0),
                                ("L1_xcond_adaLN_W", "L1_xcond_adaLN_b", 9, 1)):
            blocks += [(k.ins[w], k.ins[bias], j * D, src) for j in range(n)]
        vtiles = [(t * P, min(P, B * L - t * P)) for t in range(-(-B * L // P))]

        def cols_bank(q):
            return tp[1] if q == 0 else acc[q]

        engines = ExitStack()
        block = engines.enter_context(nc.Block())

        @block.sync
        def _(sp):
            def load_block(n):
                w, _, c0, _ = blocks[n]
                sp.dma_start(ring[n % 8][:, :, :], w[:, c0:c0 + D].rearrange("(k p) n -> p k n", p=P)).then_inc(w_in[n % 8], 16)

            def store_keys(i):
                layer, m, half = 1 - i // 8, i % 8 // 2, i % 2
                sp.wait_ge(k_evac, i + 1)
                sp.dma_start(k.keys[layer][4 * half:4 * half + 4, m].rearrange("b p t -> p b t"),
                             keys[:, i % 8, :].rearrange("p (b t) -> p b t", b=4)).then_inc(k_out, 16)

            def store_vals(i):
                layer, (t0, tn) = 1 - i // len(vtiles), vtiles[i % len(vtiles)]
                sp.wait_ge(v_evac, i + 1)
                sp.dma_start(k.vals[layer][t0:t0 + tn, :], vals[0:tn, i % len(vtiles), :]).then_inc(v_out, 16)

            sp.dma_start(cond[:, 1, :], k.ins["cond_1024"]).then_inc(cond_in, 16)
            sp.dma_start(ctx_raw[:, :, :], k.ins["ctx_1024"].rearrange("b s d -> s b d")).then_inc(ctx_in, 16)
            sp.dma_start(ck[:, :, :], k.ins["L1_xcond_ck_W"].rearrange("(k p) n -> p k n", p=P)).then_inc(ck_in, 16)
            for n in range(4):
                load_block(n)
            sp.dma_start(cv[:, :, :], k.ins["L1_xcond_cv_W"].rearrange("(k p) n -> p k n", p=P)).then_inc(cv_in, 16)
            sp.wait_ge(zeroed, 1)
            for n, (_, bias, c0, _) in enumerate(blocks):
                src = bias[c0:c0 + D].partition_broadcast(B)
                sp.dma_start(bias_rows[32 * (n % 4):32 * (n % 4) + B, n // 4, :], src).then_inc(bias_in, 16)
            for n, w in enumerate(("L1_xcond_norm1_w", "L1_xcond_normc_w", "L1_xcond_norm2_w")):
                sp.dma_start(norm_w[:, n, :], k.ins[w].rearrange("(c p) -> p c", p=P), allow_slow_non_contiguous=True).then_inc(small_in, 16)
            sp.dma_start(bk[:, :], k.ins["L0_xcond_bkv"][0:D].rearrange("(c p) -> p c", p=P), allow_slow_non_contiguous=True).then_inc(small_in, 16)
            sp.dma_start(bv_rows[:, :], k.ins["L0_xcond_bkv"][D:2 * D].partition_broadcast(P)).then_inc(small_in, 16)
            sp.dma_start(wkv[:, :, :], k.ins["L0_xcond_Wkv"].rearrange("(k p) n -> p k n", p=P)).then_inc(wkv_in, 16)
            for n in range(4, 8):
                load_block(n)
            for i in range(8):
                store_keys(i)
            sp.wait_ge(rows_mm, 1)
            for n in range(8, 12):
                load_block(n)
            for i in range(len(vtiles)):
                store_vals(i)
            for i in range(8, 16):
                store_keys(i)
            for i in range(len(vtiles), 2 * len(vtiles)):
                store_vals(i)
            sp.wait_ge(rows_mm, 2)
            load_block(12)
            for n, g in enumerate((6, 9, 12)):
                sp.wait_ge(rows_done, g // 4 + 1)
                sp.dma_start(k.gates[n], mod_rows[32 * (g % 4):32 * (g % 4) + B, g // 4, :]).then_inc(gates_out, 16)
            sp.wait_ge(gates_out, 48)
            sp.wait_ge(k_out, 16 * 16)
            sp.wait_ge(v_out, 16 * 2 * len(vtiles))

        @block.gpsimd
        def _(pool):
            pool.memset(k.ident[:, :], 0.0).then_inc(ident_z, 1)
            pool.memset(bias_rows[:, :, :], 0.0).then_inc(zeroed, 1)
            pool.wait_ge(ident_z, 1)
            pool.affine_select(out=k.ident[:, :], in_=k.ident[:, :], compare_op=ALU.not_equal, fill=1.0, base=0,
                               pattern=[[-1, P]], channel_multiplier=1).then_inc(ident_z, 1)
            pool.memset(cond_t[:, :, :, :], 0.0).then_inc(zeroed, 1)
            pool.memset(mod_rows[:, 3, :], 0.0).then_inc(zeroed, 1)
            pool.memset(k.neg_half[:, :], -0.5)
            pool.memset(half_l[:, :], -0.5).then_inc(zeroed, 1)
            pool.wait_ge(zeroed, 4)
            pool.wait_ge(mv_done, B)
            pool.tensor_scalar(var_eps[:, :], mv[:, :, 1], EPS, None, ALU.add).then_inc(ve_done, 1)
            pool.wait_ge(ve_done, 1)
            pool.tensor_tensor(rstd[:, :], var_eps[:, :], half_l[:, :], ALU.pow).then_inc(rstd_done, 1)

        @block.scalar
        def _(act):
            act.wait_ge(cond_in, 16)
            act.activation(cond[:, 0, :], cond[:, 1, :], ACT.Silu).then_inc(cond_silu, 1)
            for n in range(8):
                act.wait_ge(ctx_tp, n + 1)
                act.copy(ctx_t[:, 0, n // 2, 4 * L * (n % 2):4 * L * (n % 2) + 4 * L], tp[n % 4][:, 0:4 * L]).then_inc(ctx_raw_done, 1)
            for n in range(16):
                layer, m = 1 - n // 8, n % 8 // 2
                if n == 8:
                    act.wait_ge(small_in, 16 * 5)
                    act.wait_ge(k_out, 16 * 8)
                act.wait_ge(k_mm, n + 1)
                if layer == 0:
                    act.activation(keys[:, n % 8, :], acc[n % 2][:, 0:4 * L], ACT.Identity, bias=bk[:, m:m + 1]).then_inc(k_evac, 1)
                else:
                    act.copy(keys[:, n % 8, :], acc[n % 2][:, 0:4 * L]).then_inc(k_evac, 1)

        @block.vector
        def _(dve):
            dve.wait_ge(cond_tp, 1)
            dve.wait_ge(zeroed, 2)
            dve.tensor_copy(cond_t[:, :, :, 0:B], tp[0][:, 0:2 * KC * B].rearrange("p (s c b) -> p s c b", s=2, c=KC)).then_inc(cond_td, 1)
            dve.wait_ge(ctx_in, 16)
            for b in range(B):
                dve.bn_stats(stats[:, b, :], ctx_raw[:, b, :]).then_inc(st_done, 1)
            for b in range(B):
                dve.wait_ge(st_done, b + 1)
                dve.bn_aggr(mv[:, b, :], stats[:, b, :]).then_inc(mv_done, 1)
            dve.wait_ge(rstd_done, 1)
            for b in range(B):
                dve.tensor_scalar(ctx_nn[:, b, :], ctx_raw[:, b, :], mv[:, b, 0:1], rstd[:, b:b + 1],
                                  ALU.subtract, ALU.mult).then_inc(ctx_normed, 1)

            def rows_out(q):
                n = P if q < 3 else 32
                dve.wait_ge(rows_mm, q + 1)
                dve.tensor_tensor(mod_rows[0:n, q, :], tp[q][0:n, :], bias_rows[0:n, q, :], ALU.add).then_inc(rows_done, 1)

            def cols_out(q):
                n = P if q < 3 else 32
                dve.wait_ge(cols_tp, q + 1)
                dve.tensor_copy(mod_cols[:, q, :, 0:n], cols_bank(q)[:, :].rearrange("p (c n) -> p c n", c=KC)[:, :, 0:n]).then_inc(cols_done, 1)

            def vals_out(i):
                tn = vtiles[i % len(vtiles)][1]
                dve.wait_ge(v_mm, i + 1)
                if i == len(vtiles):
                    dve.wait_ge(v_out, 16 * len(vtiles))
                if i >= len(vtiles):
                    dve.tensor_tensor(vals[0:tn, i % len(vtiles), :], acc[2 + i % 2][0:tn, :], bv_rows[0:tn, :], ALU.add).then_inc(v_evac, 1)
                else:
                    dve.tensor_copy(vals[0:tn, i % len(vtiles), :], acc[2 + i % 2][0:tn, :]).then_inc(v_evac, 1)

            def vec(n):
                return mod_cols[:, n // 4, :, 32 * (n % 4):32 * (n % 4) + B]

            dve.wait_ge(bias_in, 16 * NB)
            dve.wait_ge(zeroed, 3)
            rows_out(0)
            vals_out(0)
            cols_out(0)
            dve.wait_ge(cols_done, 1)
            for dst, sc, sh in ((k.mod[0], 0, 1), (kv_mod, 2, 3)):
                dve.tensor_scalar(dst[:, 0, :, :], vec(sc), 1.0, None, ALU.add).then_inc(mods, 1)
                dve.tensor_copy(dst[:, 1, :, :], vec(sh)).then_inc(mods, 1)
            for i in range(1, len(vtiles)):
                vals_out(i)
            dve.wait_ge(mods, 4)
            for n in range(8, 16):
                c, half = (n - 8) // 2, n % 2
                out = ctx_t[:, 1, c, 4 * L * half:4 * L * half + 4 * L].rearrange("p (b t) -> p b t", b=4)
                bs = slice(4 * half, 4 * half + 4)
                dve.wait_ge(ctx_tp, n + 1)
                dve.tensor_tensor(out, tp[n % 4][:, 0:4 * L].rearrange("p (b t) -> p b t", b=4),
                                  kv_mod[:, 0, c, bs].unsqueeze(2).broadcast_to([P, 4, L]), ALU.mult).then_inc(ctx_a, 1)
                dve.wait_ge(ctx_a, n - 7)
                dve.tensor_tensor(out, out, kv_mod[:, 1, c, bs].unsqueeze(2).broadcast_to([P, 4, L]), ALU.add).then_inc(ctx_td, 1)
            dve.wait_ge(small_in, 16 * 5)
            for i in range(len(vtiles), 2 * len(vtiles)):
                vals_out(i)
            for q in range(1, 4):
                rows_out(q)
            for q in range(1, 4):
                cols_out(q)
            dve.wait_ge(cols_done, 4)
            for n, (sc, sh) in enumerate(((5, 4), (8, 7), (11, 10))):
                dve.scalar_tensor_tensor(k.mod[1 + n][:, 0, :, :], vec(sc), 1.0, norm_w[:, n, :].unsqueeze(2).broadcast_to([P, KC, B]),
                                         ALU.add, ALU.mult).then_inc(mods, 1)
                dve.tensor_copy(k.mod[1 + n][:, 1, :, :], vec(sh)).then_inc(mods, 1)

        @block.tensor
        def _(pe):
            pe.wait_ge(ident_z, 2)
            pe.wait_ge(cond_silu, 1)
            for s in range(2):
                for c in range(KC):
                    last = pe.transpose(tp[0][:, (s * KC + c) * B:(s * KC + c + 1) * B], cond[:, s, c * P:(c + 1) * P], k.ident[0:B, 0:B])
            last.then_inc(cond_tp, 1)

            def rows(q):
                mine = [n for n in range(4 * q, min(4 * q + 4, NB))]
                for n in mine:
                    pe.wait_ge(w_in[n % 8], 16 * (n // 8 + 1))
                for c in range(KC):
                    for n in mine:
                        r = 32 * (n % 4)
                        last = pe.matmul(tp[q][r:r + 32, :], cond_t[:, blocks[n][3], c, :], ring[n % 8][:, c, :],
                                         start=c == 0, stop=c == KC - 1)
                last.then_inc(rows_mm, 1)

            def cols(q):
                n = P if q < 3 else 32
                pe.wait_ge(rows_done, q + 1)
                for c in range(KC):
                    last = pe.transpose(cols_bank(q)[:, c * P:c * P + n], mod_rows[0:n, q, c * P:(c + 1) * P], k.ident[0:n, 0:n])
                last.then_inc(cols_tp, 1)

            def turn_context(n):
                src = ctx_raw if n < 8 else ctx_nn
                c, half = n % 8 // 2, n % 2
                if 4 <= n < 8:
                    pe.wait_ge(ctx_raw_done, n - 3)
                if n >= 12:
                    pe.wait_ge(ctx_a, n - 11)
                for j in range(4):
                    last = pe.transpose(tp[n % 4][:, j * L:(j + 1) * L], src[:, 4 * half + j, c * P:(c + 1) * P], k.ident[0:L, 0:L])
                last.then_inc(ctx_tp, 1)

            def make_keys(i):
                layer, m, half = 1 - i // 8, i % 8 // 2, i % 2
                if i >= 2:
                    pe.wait_ge(k_evac, i - 1)
                for c in range(KC):
                    last = pe.matmul(acc[i % 2][:, 0:4 * L], (wkv if layer == 0 else ck)[:, c, m * P:(m + 1) * P],
                                     ctx_t[:, 1 - layer, c, 4 * L * half:4 * L * half + 4 * L], start=c == 0, stop=c == KC - 1)
                last.then_inc(k_mm, 1)

            def make_vals(i):
                layer, (t0, tn) = 1 - i // len(vtiles), vtiles[i % len(vtiles)]
                if i >= 2:
                    pe.wait_ge(v_evac, i - 1)
                for c in range(KC):
                    w = wkv[:, c, D:2 * D] if layer == 0 else cv[:, c, :]
                    last = pe.matmul(acc[2 + i % 2][0:tn, :], ctx_t[:, 1 - layer, c, t0:t0 + tn], w, start=c == 0, stop=c == KC - 1)
                last.then_inc(v_mm, 1)

            pe.wait_ge(cond_td, 1)
            pe.wait_ge(ctx_in, 16)
            for n in range(8):
                turn_context(n)
            pe.wait_ge(ck_in, 16)
            pe.wait_ge(ctx_raw_done, 8)
            for i in range(8):
                make_keys(i)
            rows(0)
            pe.wait_ge(cv_in, 16)
            make_vals(0)
            cols(0)
            for i in range(1, len(vtiles)):
                make_vals(i)
            pe.wait_ge(ctx_normed, B)
            pe.wait_ge(cols_done, 1)
            for n in range(8, 16):
                turn_context(n)
            pe.wait_ge(wkv_in, 16)
            pe.wait_ge(ctx_td, 8)
            for i in range(8, 16):
                make_keys(i)
            for i in range(len(vtiles), 2 * len(vtiles)):
                make_vals(i)
            for q in range(1, 4):
                rows(q)
            for q in range(1, 4):
                cols(q)

        engines.close()
        with nc.Block() as tidy:
            @tidy.sync
            def _(sp):
                for s in used:
                    sp.sem_clear(s)


class Norm:

    def __init__(self, nc, ctx, tag):
        def count(name, per, unit=1):
            return Count(nc, ctx, f"{tag}_{name}", per, unit)
        self.x_in = count("x_in", 1, 16)
        self.stats_done = count("stats_done", TT)
        self.mean_var = count("mean_var", TT)
        self.var_eps_done = count("var_eps_done", 1)
        self.rstd_done = count("rstd_done", 1)
        self.normed = count("normed", TT)
        self.mod_done = count("mod_done", 1)
        self.high = count("high", KC)
        self.low = count("low", KC)


def norm_stats(dve, nm, bf, n, tiles=range(TT)):
    dve.wait_ge(nm.x_in.sem, nm.x_in.at(n, 1))
    for t in tiles:
        dve.bn_stats(bf["stats"][:, t, :], bf["x"][:, t, :]).then_inc(nm.stats_done.sem, 1)
    for t in tiles:
        wait_apart(dve, nm.stats_done.sem, nm.stats_done.at(n, t + 1))
        dve.bn_aggr(bf["mv"][:, t, :], bf["stats"][:, t, :]).then_inc(nm.mean_var.sem, 1)


def norm_rstd(pool, nm, bf, n, neg_half):
    wait_apart(pool, nm.mean_var.sem, nm.mean_var.at(n, TT))
    pool.tensor_scalar(bf["var_eps"][:, :], bf["mv"][:, :, 1], EPS, None, ALU.add).then_inc(nm.var_eps_done.sem, 1)
    pool.wait_ge(nm.var_eps_done.sem, nm.var_eps_done.at(n, 1))
    pool.tensor_tensor(bf["rstd"][:, :], bf["var_eps"][:, :], neg_half[:, :], ALU.pow).then_inc(nm.rstd_done.sem, 1)


def norm_apply(dve, nm, bf, n, tiles=range(TT)):
    dve.wait_ge(nm.rstd_done.sem, nm.rstd_done.at(n, 1))
    for t in tiles:
        dve.tensor_scalar(bf["x"][:, t, :], bf["x"][:, t, :], bf["mv"][:, t, 0:1], bf["rstd"][:, t:t + 1],
                          ALU.subtract, ALU.mult).then_inc(nm.normed.sem, 1)


def norm_buffers(sb):
    return {"x": sb("x", [P, TT, D]), "stats": sb("stats", [P, TT, 6]), "mv": sb("mv", [P, TT, 2]),
            "rstd": sb("rstd", [P, TT]), "var_eps": sb("var_eps", [P, TT]), "mod": sb("mod", [P, 2, KC, 1])}


def mod_copy(dve, nm, bf, mod, b, n, used, used_at):
    dve.wait_ge(used.sem, used_at)
    dve.tensor_copy(bf["mod"][:, :, :, :], mod[:, :, :, bass.ds(b, 1)]).then_inc(nm.mod_done.sem, 1)


def split(dve, nm, n, c, full, high, low):
    dve.tensor_copy(high, full).then_inc(nm.high.sem, 1)
    dve.wait_ge(nm.high.sem, nm.high.at(n, c + 1))
    dve.tensor_tensor(low, full, high.bitcast(F32), ALU.subtract).then_inc(nm.low.sem, 1)


class Weights:

    def __init__(self, nc, ctx, tag, stage, slots, chunks):
        self.stage, self.slots, self.chunks = stage, slots, chunks
        self.chunk_in = [ctx.enter_context(nc.semaphore(f"{tag}_w_in{n}")) for n in range(slots)]
        self.scaled = ctx.enter_context(nc.semaphore(f"{tag}_w_scaled"))
        self.high_done = ctx.enter_context(nc.semaphore(f"{tag}_w_high"))
        self.low_done = ctx.enter_context(nc.semaphore(f"{tag}_w_low"))

    def load(self, sp, first=0, end=None):
        for n in range(first, len(self.chunks) if end is None else end):
            src = self.chunks[n][0]
            if n >= self.slots:
                sp.wait_ge(self.low_done, n - self.slots + 1)
            sp.dma_start(self.stage[:, n % self.slots, :], src).then_inc(self.chunk_in[n % self.slots], 16)

    def high(self, act, first, end):
        for n in range(first, end):
            _, high, _, scale = self.chunks[n]
            place = self.stage[:, n % self.slots, :]
            act.wait_ge(self.chunk_in[n % self.slots], 16 * (n // self.slots + 1))
            if scale != 1.0:
                act.mul(place, place, scale).then_inc(self.scaled, 1)
                act.wait_ge(self.scaled, 1 + sum(c[3] != 1.0 for c in self.chunks[:n]))
            act.copy(high, place).then_inc(self.high_done, 1)

    def low(self, dve, first, end):
        for n in range(first, end):
            _, high, low, _ = self.chunks[n]
            dve.wait_ge(self.high_done, n + 1)
            dve.tensor_tensor(low, self.stage[:, n % self.slots, :], high.bitcast(F32), ALU.subtract).then_inc(self.low_done, 1)


def weight_chunks(w, cols, high, low, scale=1.0):
    return [(w[c * P:(c + 1) * P, cols], high[:, c, :], low[:, c, :], scale) for c in range(KC)]


class CrossCounts:
    def __init__(self, nc, ctx):
        def count(name, per, unit=1):
            return Count(nc, ctx, f"x_{name}", per, unit)
        self.norm = Norm(nc, ctx, "x")
        self.keys_in = count("keys_in", HG, 16)
        self.vals_in = count("vals_in", 1, 16)
        self.gate_in = count("gate_in", 1, 16)
        self.res_in = count("res_in", 1, 16)
        self.dense_mm = count("dense_mm", 8)
        self.dense_out = count("dense_out", 8)
        self.scored = count("scored", 16)
        self.row_max = count("row_max", 16)
        self.shifted = count("shifted", 16)
        self.exped = count("exped", 16)
        self.summed = count("summed", 16)
        self.inverted = count("inverted", 16)
        self.probs = count("probs", 16)
        self.turned = count("turned", 16)
        self.turned_out = count("turned_out", 16)
        self.attended = count("attended", NG)
        self.att_high = count("att_high", NG)
        self.att_low = count("att_low", NG)
        self.projected = count("projected", TT)
        self.gated = count("gated", TT)
        self.added = count("added", TT)
        self.stored = Count(nc, ctx, "x_stored", 1, 16, base=0)


def cross_phase(nc, k, c, layer, src, dst):
    with ExitStack() as ctx:
        def sb(name, shape, dt=F32):
            return ctx.enter_context(nc.sbuf_tensor(f"x{layer}_" + name, shape, dt))

        def ps(name):
            return ctx.enter_context(nc.psum_tensor(f"x{layer}_ps_" + name, [P, 512], F32))

        off = layer * B
        nm = c.norm
        if layer == 0:
            wq, wo, mod, gate_op = "L0_xcond_Wq", "L0_xcond_Wp", k.mod[0], ALU.add
        else:
            wq, wo, mod, gate_op = "L1_xcond_cq_W", "L1_xcond_co_W", k.mod[2], ALU.mult
        bf = norm_buffers(sb)
        wqh, wql = sb("wqh", [P, KC, D], F32R), sb("wql", [P, KC, D], F32R)
        woh, wol = sb("woh", [P, KC, D], F32R), sb("wol", [P, KC, D], F32R)
        full = sb("full", [P, KC, S])
        xh, xl = sb("xh", [P, KC, S], F32R), sb("xl", [P, KC, S], F32R)
        queries = [sb(f"queries{n}", [P, NG, S]) for n in range(2)]
        keys = [sb(f"keys{n}", [P, NG, GL]) for n in range(2)]
        vals = sb("vals", [L, D])
        scores = sb("scores", [P, 4, GL])
        mx, sums, inv = sb("mx", [P, 2, HG]), sb("sums", [P, STEPS, HG]), sb("inv", [P, STEPS, HG])
        probs = sb("probs", [P, STEPS, GL])
        probs_t = [sb(f"probs_t{n}", [L, HG, S]) for n in range(2)]
        ah, al = [sb(f"ah{n}", [P, NG, S], F32R) for n in range(2)], [sb(f"al{n}", [P, NG, S], F32R) for n in range(2)]
        gate = sb("gate", [P, D])
        gated = sb("gated", [P, 2, D])
        res = sb("res", [P, TT, D])
        bq = sb("bq", [P, KC])
        if layer == 1:
            mask_u8, mask_add, ones = sb("mask_u8", [1, B * L], U8), sb("mask_add", [1, B, HG, L], BF16), sb("ones", [1, P], BF16)
        dense, score_ps, turn_ps = [ps(f"dense{n}") for n in range(2)], [ps(f"score{n}") for n in range(2)], [ps(f"turn{n}") for n in range(2)]
        att_ps, out_ps = ps("att"), ps("out")
        bq_in, keys_zeroed, mask_done = (ctx.enter_context(nc.semaphore(f"x{layer}_{x}")) for x in ("bq_in", "keys_zeroed", "mask_done"))
        mask_in = bq_in
        stage = probs[:, :, :].rearrange("p n t -> p (n t)")[:, 0:2 * KC * D].rearrange("p (c n) -> p c n", n=D)
        wt = Weights(nc, ctx, f"x{layer}", stage, 2 * KC, weight_chunks(k.ins[wq], slice(0, D), wqh, wql)
                     + weight_chunks(k.ins[wo], slice(0, D), woh, wol))

        def heads4(ap):
            return ap.rearrange("p (h t) -> p h t", h=HG)

        def per_head(ap):
            return ap.unsqueeze(2).broadcast_to([P, HG, L])

        block = ctx.enter_context(nc.Block())

        def schedule(eng, weights, score, turn, query, query_out, attend, attend_out, norm, project, project_out):
            def entry(b, par, before, after, after2):
                for n in range(STEPS):
                    u, (g, rest) = n - PROJECT_AT, divmod(n - ATTEND_LAG, HG)
                    if before and u % 2 == 0 and 2 <= u <= 2 * TT:
                        project_out(b - 1, u // 2 - 1)
                    if after and n % 2 == 0 and 2 <= n <= 2 * NG:
                        query_out(b + 1, n // 2 - 1, 1 - par)
                    if rest == 1 and g >= 0:
                        attend_out(b, g, par)
                    elif rest == 1 and before:
                        attend_out(b - 1, g + NG, 1 - par)
                    score(b, n, par)
                    if n >= TURN_LAG:
                        turn(b, n - TURN_LAG)
                    elif before:
                        turn(b - 1, n - TURN_LAG + STEPS)
                    if after and n < 2 * NG:
                        query(b + 1, n // 2, n % 2)
                    if rest == 0 and g >= 0:
                        attend(b, g, par)
                    elif rest == 0 and before:
                        attend(b - 1, g + NG, 1 - par)
                    if after2:
                        norm(b + 2, n)
                    if before and 0 <= u < 2 * TT:
                        project(b - 1, u // 2, u % 2, 1 - par)
            for n in range(STEPS):
                if n == NORM_TURN:
                    weights(0)
                norm(0, n)
            weights(1)
            for m in range(NG):
                query(0, m, 0)
                query(0, m, 1)
                query_out(0, m, 0)
            for n in range(STEPS):
                norm(1, n)
            entry(0, 0, False, True, True)
            with eng.Fori(0, (B - 4) // 2) as j:
                entry(j * 2 + 1, 1, True, True, True)
                entry(j * 2 + 2, 0, True, True, True)
            for b in range(B - 3, B):
                entry(b, b % 2, True, b + 1 < B, b + 2 < B)
            for n in range(STEPS, ATTEND_LAG + STEPS - HG + 2):
                g, rest = divmod(n - ATTEND_LAG, HG)
                if rest == 1:
                    attend_out(B - 1, g, 1)
                if n - TURN_LAG < NH:
                    turn(B - 1, n - TURN_LAG)
                if rest == 0:
                    attend(B - 1, g, 1)
            for t in range(TT):
                project(B - 1, t, 0, 1)
                project(B - 1, t, 1, 1)
                project_out(B - 1, t)

        def nothing(*_):
            pass

        @block.sync
        def _(sp):
            if layer == 0:
                sp.sem_inc(nm.x_in.sem, nm.x_in.credit)
                for q in (c.keys_in, c.vals_in, c.gate_in, c.res_in):
                    sp.sem_inc(q.sem, q.credit)

            def load_x(b):
                wait_apart(sp, c.dense_out.sem, c.dense_out.at(b + off, KC - 8))
                sp.dma_start(bf["x"][:, :, :], row(src, b)).then_inc(nm.x_in.sem, 16)

            def load_keys(b, par):
                wait_apart(sp, c.scored.sem, c.scored.at(b + off, HG - STEPS))
                for r in range(HG):
                    rows = slice(HD * r, HD * r + HD)
                    sp.dma_start(keys[par][rows, :, r * L:(r + 1) * L],
                                 k.keys[layer][bass.ds(b, 1)].rearrange("o g p t -> (o p) g t")[rows]
                                 ).then_inc(c.keys_in.sem, 16)

            def load_vals(b):
                wait_apart(sp, c.attended.sem, c.attended.at(b + off, 0))
                sp.dma_start(vals[:, :], k.vals[layer][bass.ds(b * L, L), :]).then_inc(c.vals_in.sem, 16)

            def load_res(b, first=False):
                if layer == 1:
                    wait_apart(sp, c.gated.sem, c.gated.at(b + off, 0))
                    sp.dma_start(gate[:, :], k.gates[1][bass.ds(b, 1), :].rearrange("o n -> (o n)").partition_broadcast(P)).then_inc(c.gate_in.sem, 16)
                if not (layer == 0 and first):
                    wait_apart(sp, c.stored.sem, c.stored.at(b + off, 0))
                sp.dma_start(res[:, :, :], row(src, b)).then_inc(c.res_in.sem, 16)

            load_x(0)
            wt.load(sp)
            if layer == 0:
                sp.dma_start(bq[:, :], k.ins["L0_xcond_bq"].rearrange("(c p) -> p c", p=P), allow_slow_non_contiguous=True).then_inc(bq_in, 16)
                sp.dma_start(gate[:, :], k.ins["L0_xcond_bp"].partition_broadcast(P)).then_inc(c.gate_in.sem, 16)
            else:
                sp.dma_start(mask_u8[:, :], k.ins["mask_BxS2_bf1"].rearrange("b s -> (b s)").partition_broadcast(1)).then_inc(mask_in, 16)
            sp.wait_ge(keys_zeroed, 2)
            load_keys(0, 0)
            load_vals(0)
            load_x(1)
            load_x(2)
            load_keys(1, 1)
            load_res(0, first=True)
            load_x(3)
            with sp.Fori(0, (B - 4) // 2) as j:
                for i in range(2):
                    b = j * 2 + 1 + i
                    load_keys(b + 1, i)
                    load_vals(b)
                    load_x(b + 3)
                    load_res(b)
            for b in range(B - 3, B):
                if b + 1 < B:
                    load_keys(b + 1, (b + 1) % 2)
                load_vals(b)
                load_res(b)

        @block.gpsimd
        def _(pool):
            for n in range(2):
                pool.memset(keys[n][:, :, :], 0.0).then_inc(keys_zeroed, 1)
            if layer == 0:
                for q in (nm.var_eps_done, nm.rstd_done, c.probs, c.added):
                    pool.sem_inc(q.sem, q.credit)

            def norm(b, n):
                if n == NORM_STATS[-1]:
                    norm_rstd(pool, nm, bf, b + off, k.neg_half)

            def normalise(b, n):
                pool.wait_ge(c.inverted.sem, c.inverted.at(b + off, n + 1))
                pool.tensor_tensor(heads4(probs[:, n, :]), heads4(probs[:, n, :]), per_head(inv[:, n, :]), ALU.mult).then_inc(c.probs.sem, 1)

            def score(b, n, par):
                if n:
                    normalise(b, n - 1)
                if n == STEPS - 1:
                    normalise(b, n)

            def project_out(b, t):
                if t == 0:
                    pool.wait_ge(c.res_in.sem, c.res_in.at(b + off, 1))
                pool.wait_ge(c.gated.sem, c.gated.at(b + off, t + 1))
                pool.tensor_tensor(res[:, t, :], res[:, t, :], gated[:, t % 2, :], ALU.add).then_inc(c.added.sem, 1)
                if t == TT - 1:
                    pool.wait_ge(c.added.sem, c.added.at(b + off, TT))
                    pool.dma_start(row(dst, b), res[:, :, :]).then_inc(c.stored.sem, 16)

            schedule(pool, nothing, score, nothing, nothing, nothing, nothing, nothing, norm, nothing, project_out)
            pool.wait_ge(c.stored.sem, c.stored.at(B - 1 + off, 1))

        @block.scalar
        def _(act):
            if layer == 0:
                for q in (c.dense_out, nm.high, c.exped, c.turned_out, c.att_high):
                    act.sem_inc(q.sem, q.credit)
            if layer == 0:
                act.wait_ge(bq_in, 16)

            def norm(b, step):
                n, ch = b + off, step - NORM_TURN - 1
                if 0 <= ch < KC:
                    if ch == 0:
                        act.wait_ge(nm.mod_done.sem, nm.mod_done.at(n, 1))
                    act.wait_ge(c.dense_mm.sem, c.dense_mm.at(n, ch + 1))
                    act.wait_ge(nm.low.sem, nm.low.at(n, ch + 1 - KC))
                    act.activation(full[:, ch, :], dense[ch % 2][:, :], ACT.Identity, bias=bf["mod"][:, 1, ch, :],
                                   scale=bf["mod"][:, 0, ch, :]).then_inc(c.dense_out.sem, 1)
                    act.wait_ge(c.dense_out.sem, c.dense_out.at(n, ch + 1))
                    act.copy(xh[:, ch, :], full[:, ch, :]).then_inc(nm.high.sem, 1)

            def query_out(b, m, par):
                act.wait_ge(c.dense_mm.sem, c.dense_mm.at(b + off, 5 + m))
                if layer == 0:
                    act.activation(queries[par][:, m, :], dense[m % 2][:, :], ACT.Identity, bias=bq[:, m:m + 1]).then_inc(c.dense_out.sem, 1)
                else:
                    act.copy(queries[par][:, m, :], dense[m % 2][:, :]).then_inc(c.dense_out.sem, 1)

            def score(b, n, par):
                n0 = b + off
                if n % HG == 0:
                    act.wait_ge(c.turned.sem, c.turned.at(n0, n + HG - STEPS))
                act.wait_ge(c.shifted.sem, c.shifted.at(n0, n + 1))
                act.activation(probs[:, n, :], scores[:, n % 4, :], ACT.Exp, scale=SCALE).then_inc(c.exped.sem, 1)

            def turn(b, h):
                n0 = b + off
                if h % HG == 0:
                    act.wait_ge(c.attended.sem, c.attended.at(n0, h // HG - 1))
                act.wait_ge(c.turned.sem, c.turned.at(n0, h + 1))
                act.copy(probs_t[h // HG % 2][:, h % HG, :], turn_ps[h % 2][0:L, :]).then_inc(c.turned_out.sem, 1)

            def attend_out(b, g, par):
                act.wait_ge(c.attended.sem, c.attended.at(b + off, g + 1))
                act.copy(ah[par][:, g, :], att_ps[:, :]).then_inc(c.att_high.sem, 1)

            schedule(act, lambda i: wt.high(act, i * KC, i * KC + KC), score, turn, nothing, query_out, nothing, attend_out, norm, nothing, nothing)

        @block.vector
        def _(dve):
            if layer == 0:
                for q in (nm.stats_done, nm.mean_var, nm.normed, nm.mod_done, nm.low, c.row_max, c.shifted, c.summed,
                          c.inverted, c.att_low, c.gated):
                    dve.sem_inc(q.sem, q.credit)
            if layer == 1:
                dve.wait_ge(mask_in, 16)
                dve.tensor_scalar(mask_add[:, :, :, :], mask_u8[:, :].rearrange("p (b t) -> p b t", b=B).unsqueeze(2).broadcast_to([1, B, HG, L]),
                                  BIG16, -BIG16, ALU.mult, ALU.add).then_inc(mask_done, 1)
                dve.memset(ones[:, :], 1.0).then_inc(mask_done, 1)

            def norm(b, step):
                n, ch = b + off, step - NORM_TURN - 2
                if step in NORM_STATS:
                    i = NORM_STATS.index(step)
                    norm_stats(dve, nm, bf, n, (2 * i, 2 * i + 1))
                if step == NORM_STATS[-1]:
                    mod_copy(dve, nm, bf, mod, b, n, c.dense_out, c.dense_out.at(n, KC - 8))
                if step in NORM_APPLY:
                    i = NORM_APPLY.index(step)
                    norm_apply(dve, nm, bf, n, (2 * i, 2 * i + 1))
                if 0 <= ch < KC:
                    dve.wait_ge(nm.high.sem, nm.high.at(n, ch + 1))
                    dve.tensor_tensor(xl[:, ch, :], full[:, ch, :], xh[:, ch, :].bitcast(F32), ALU.subtract).then_inc(nm.low.sem, 1)

            def invert(b, n):
                n0 = b + off
                dve.wait_ge(c.exped.sem, c.exped.at(n0, n + 1))
                dve.tensor_reduce(sums[:, n, :], heads4(probs[:, n, :]), AX_X, ALU.add).then_inc(c.summed.sem, 1)
                dve.wait_ge(c.summed.sem, c.summed.at(n0, n + 1))
                dve.wait_ge(c.probs.sem, c.probs.at(n0, n + 1 - STEPS))
                dve.reciprocal(inv[:, n, :], sums[:, n, :]).then_inc(c.inverted.sem, 1)

            def score(b, n, par):
                n0 = b + off
                raw, out = heads4(score_ps[n % 2][:, 0:GL]), heads4(scores[:, n % 4, :])
                dve.wait_ge(c.scored.sem, c.scored.at(n0, n + 1))
                dve.wait_ge(c.exped.sem, c.exped.at(n0, n - 3))
                dve.tensor_reduce(mx[:, n % 2, :], raw, AX_X, ALU.max).then_inc(c.row_max.sem, 1)
                dve.wait_ge(c.row_max.sem, c.row_max.at(n0, n + 1))
                dve.tensor_tensor(out, raw, per_head(mx[:, n % 2, :]), ALU.subtract).then_inc(c.shifted.sem, 1)
                if n:
                    invert(b, n - 1)
                if n == STEPS - 1:
                    invert(b, n)

            def attend_out(b, g, par):
                dve.wait_ge(c.att_high.sem, c.att_high.at(b + off, g + 1))
                dve.tensor_tensor(al[par][:, g, :], att_ps[:, :], ah[par][:, g, :].bitcast(F32), ALU.subtract).then_inc(c.att_low.sem, 1)

            def project_out(b, t):
                n0 = b + off
                if t == 0:
                    dve.wait_ge(c.gate_in.sem, c.gate_in.at(0, 1) if layer == 0 else c.gate_in.at(b + 1, 1))
                dve.wait_ge(c.projected.sem, c.projected.at(n0, t + 1))
                dve.wait_ge(c.added.sem, c.added.at(n0, t - 1))
                dve.tensor_tensor(gated[:, t % 2, :], out_ps[:, :], gate[:, :], gate_op).then_inc(c.gated.sem, 1)

            schedule(dve, lambda i: wt.low(dve, i * KC, i * KC + KC), score, nothing, nothing, nothing, nothing, attend_out, norm, nothing, project_out)

        @block.tensor
        def _(pe):
            if layer == 0:
                for q in (c.dense_mm, c.scored, c.turned, c.attended, c.projected):
                    pe.sem_inc(q.sem, q.credit)

            def weights_ready(i):
                if i == 1:
                    pe.wait_ge(wt.low_done, KC)
                    if layer == 1:
                        pe.wait_ge(mask_done, 2)

            def norm(b, step):
                n, ch = b + off, step - NORM_TURN
                if 0 <= ch < KC:
                    if ch == 0:
                        pe.wait_ge(nm.normed.sem, nm.normed.at(n, TT))
                    pe.wait_ge(c.dense_out.sem, c.dense_out.at(n, ch - 1))
                    for t in range(TT):
                        last = pe.transpose(dense[ch % 2][:, t * P:(t + 1) * P], bf["x"][:, t, ch * P:(ch + 1) * P], k.ident[:, :])
                    last.then_inc(c.dense_mm.sem, 1)

            def query(b, m, half):
                n = b + off
                if m == 0 and half == 0:
                    pe.wait_ge(nm.low.sem, nm.low.at(n, KC))
                if half == 0:
                    pe.wait_ge(c.dense_out.sem, c.dense_out.at(n, 4 + m - 1))
                last = split_matmul(pe, dense[m % 2][:, :], [(wqh[:, ch, m * P:(m + 1) * P], wql[:, ch, m * P:(m + 1) * P]) for ch in range(KC)],
                                    [(xh[:, ch, :], xl[:, ch, :]) for ch in range(KC)], half, 2)
                if half:
                    last.then_inc(c.dense_mm.sem, 1)

            def score(b, n, par):
                n0, g, t = b + off, n // HG, n % HG
                if n == 0:
                    pe.wait_ge(c.keys_in.sem, c.keys_in.at(n0, HG))
                if t == 0:
                    pe.wait_ge(c.dense_out.sem, c.dense_out.at(n0, 5 + g))
                pe.wait_ge(c.shifted.sem, c.shifted.at(n0, n - 1))
                last = pe.matmul(score_ps[n % 2][:, 0:GL], queries[par][:, g, t * P:(t + 1) * P], keys[par][:, g, :],
                                 start=True, stop=layer == 0)
                if layer == 1:
                    last = pe.matmul(score_ps[n % 2][:, 0:GL], ones[:, :], mask_add[:, :, :, :].rearrange("o b h t -> o (b h t)")[:, bass.ds(b * GL, GL)],
                                     start=False, stop=True)
                last.then_inc(c.scored.sem, 1)

            def turn(b, h):
                n0, g, r = b + off, h // HG, h % HG
                if r == 0:
                    pe.wait_ge(c.probs.sem, c.probs.at(n0, 4 * g + 4))
                pe.wait_ge(c.turned_out.sem, c.turned_out.at(n0, h - 1))
                for t in range(TT):
                    last = pe.transpose(turn_ps[h % 2][0:L, t * P:(t + 1) * P], probs[:, 4 * g + t, r * L:(r + 1) * L], k.ident[:, :])
                last.then_inc(c.turned.sem, 1)

            def attend(b, g, par):
                n0 = b + off
                if g == 0:
                    pe.wait_ge(c.vals_in.sem, c.vals_in.at(n0, 1))
                pe.wait_ge(c.turned_out.sem, c.turned_out.at(n0, HG * g + HG))
                pe.wait_ge(c.att_low.sem, c.att_low.at(n0, g))
                for r in range(HG):
                    h = HG * g + r
                    last = pe.matmul(att_ps[HD * r:HD * r + HD, :], vals[:, h * HD:(h + 1) * HD], probs_t[g % 2][:, r, :],
                                     start=True, stop=True)
                last.then_inc(c.attended.sem, 1)

            def project(b, t, half, par):
                n0 = b + off
                if t == 0 and half == 0:
                    pe.wait_ge(wt.low_done, 2 * KC)
                    pe.wait_ge(c.att_low.sem, c.att_low.at(n0, NG))
                if half == 0:
                    pe.wait_ge(c.gated.sem, c.gated.at(n0, t))
                last = split_matmul(pe, out_ps[:, :], [(ah[par][:, ch, t * P:(t + 1) * P], al[par][:, ch, t * P:(t + 1) * P]) for ch in range(KC)],
                                    [(woh[:, ch, :], wol[:, ch, :]) for ch in range(KC)], half, 2)
                if half:
                    last.then_inc(c.projected.sem, 1)

            schedule(pe, weights_ready, score, turn, query, nothing, attend, nothing, norm, project, nothing)


HS = NG * 2 * HG
ROT = [(d + HD // 2) % HD for d in range(HD)]
DENSE = [("norm", n) for n in range(KC)] + [("qk", 0), ("qk", 1), ("value", 0), ("value", 1), ("qk", 2), ("qk", 3),
                                            ("value", 2), ("value", 3)] + [("qk", n) for n in range(4, 8)]
DENSE_NOW = {0: [("value", 2, 0)], 1: [("value", 2, 1)], 2: [("value", 3, 0), ("value", 3, 1)],
             3: [("qk", 4, 0)], 4: [("qk", 4, 1)], 5: [("qk", 5, 0)], 6: [("qk", 5, 1)],
             11: [("qk", 6, 0)], 12: [("qk", 6, 1)], 13: [("qk", 7, 0)], 14: [("qk", 7, 1)]}
DENSE_NEXT = {19: [("qk", 0, 0)], 20: [("qk", 0, 1)], 21: [("qk", 1, 0)], 22: [("qk", 1, 1)],
              23: [("value", 0, 0)], 24: [("value", 0, 1)], 25: [("value", 1, 0)], 26: [("value", 1, 1)],
              27: [("qk", 2, 0)], 28: [("qk", 2, 1)], 29: [("qk", 3, 0)], 30: [("qk", 3, 1)]}
OUT_AT = 4
STATS_AT, APPLY_AT = (4, 6), (9, 10)
TURN_AT = (14, 15, 16, 17)
SPLIT_NOW = {0: 2, 1: 3, 8: 4, 9: 5, 16: 6, 17: 7}
SPLIT_NEXT = {24: 0, 25: 1}
ATT_LAG = LAG + HG


def self_phase(nc, k, src, dst):
    with ExitStack() as ctx:
        def sb(name, shape, dt=F32):
            return ctx.enter_context(nc.sbuf_tensor("s_" + name, shape, dt))

        def ps(name):
            return ctx.enter_context(nc.psum_tensor("s_ps_" + name, [P, 512], F32))

        def count(name, per, unit=1, base=None):
            return Count(nc, ctx, "s_" + name, per, unit, base)

        mod = k.mod[1]
        nm = Norm(nc, ctx, "s")
        gate_in, res_in = count("gate_in", 1, 16), count("res_in", 1, 16)
        stored = count("stored", 1, 16, base=0)
        dense_mm = count("dense_mm", 16)
        act_dense = count("act_dense", 8)
        cos_done, shuffled = count("cos_done", 8), count("shuffled", 8)
        sin_done, roped = count("sin_done", 8), count("roped", 8)
        qk_high, qk_low = count("qk_high", 8), count("qk_low", 8)
        stack_in = [count(f"stack_in{w}", 12 * NG, 16) for w in range(2)]
        scored, masked, exped, inverted, probs_done = (count(x, 2 * HS) for x in ("scored", "masked", "exped", "inverted", "probs_done"))
        turned, turned_out = count("turned", 2 * HS), count("turned_out", 2 * HS)
        attended, att_out = count("attended", 2 * NG), count("att_out", 2 * NG)
        projected, gated_done, added = count("projected", TT), count("gated_done", TT), count("added", TT)
        mask_in, mask_done, rope_in, wo_in = (ctx.enter_context(nc.semaphore("s_" + x)) for x in ("mask_in", "mask_done", "rope_in", "wo_in"))

        bf = norm_buffers(sb)
        res = sb("res", [P, TT, D])
        wh, wl = sb("wh", [P, KC, 3 * D], F32R), sb("wl", [P, KC, 3 * D], F32R)
        wo = sb("wo", [P, KC, D])
        full = sb("full", [P, 2, S])
        xh, xl = sb("xh", [P, KC, S], F32R), sb("xl", [P, KC, S], F32R)
        rope = sb("rope", [P, 2, S // 2])
        with_cos, swapped = sb("with_cos", [P, 2, S]), sb("swapped", [P, 2, S])
        high_part = sb("high_part", [P, 2, S], F32R)
        stacks = [sb(f"stack{w}", [3 * HD, 2 * HG, S], F32R) for w in range(2)]
        vals = [sb(f"vals{n}", [P, TT, D]) for n in range(2)]
        mask_add = sb("mask_add", [P, TT, S], BF16)
        scores = sb("scores", [P, 2, S])
        low_score, sums, inv = sb("low_score", [P, PR]), sb("sums", [P, PR]), sb("inv", [P, PR])
        probs = sb("probs", [P, PR, S])
        probs_t = sb("probs_t", [P, HG, KC, S // 2])
        att = sb("att", [P, NG, S])
        gate, gated = sb("gate", [P, D]), full
        mask_u8 = gated[:, 0, :].bitcast(U8).rearrange("p (t n) -> p t n", t=TT)
        dense, score_ps, turn_ps = [ps(f"dense{n}") for n in range(2)], [ps(f"score{n}") for n in range(2)], [ps(f"turn{n}") for n in range(2)]
        att_ps, out_ps = ps("att"), ps("out")
        w_qkv = k.ins["L1_xcond_qkv_W"]
        chunks = [(w_qkv[c * P:(c + 1) * P, j * D:(j + 1) * D], wh[:, c, j * D:(j + 1) * D], wl[:, c, j * D:(j + 1) * D],
                   -SCALE if j == 0 else 1.0) for j in range(3) for c in range(KC)]
        wt = Weights(nc, ctx, "s", probs, PR, chunks)

        def schedule(eng, weights, lag, head, tail, attend, att_out, dense_part, dense_out, norm, norm_out, qk_split, project, project_out):
            def late(b, par, table, n):
                for kind, i, half in table.get(n, ()):
                    if half:
                        dense_out(b, kind, i, par)

            def entry(b, par, before, after):
                for n in range(HS):
                    if before and OUT_AT + 2 <= n <= OUT_AT + 2 * TT and (n - OUT_AT) % 2 == 0:
                        project_out(b - 1, (n - OUT_AT) // 2 - 1)
                    late(b, par, DENSE_NOW, n - 1)
                    if after:
                        late(b + 1, 1 - par, DENSE_NEXT, n - 1)
                        if n - 1 in TURN_AT:
                            norm_out(b + 1, TURN_AT.index(n - 1), b)
                    if n % HG == 0 and n >= ATT_LAG + 1:
                        att_out(b, (n - ATT_LAG - 1) // HG, par)
                    elif n % HG == 0 and before:
                        att_out(b - 1, (n - ATT_LAG - 1 + HS) // HG, 1 - par)
                    head(b, n)
                    if n in SPLIT_NOW:
                        qk_split(b, SPLIT_NOW[n])
                    if after and n in SPLIT_NEXT:
                        qk_split(b + 1, SPLIT_NEXT[n])
                    for kind, i, half in DENSE_NOW.get(n, ()):
                        dense_part(b, kind, i, half)
                    if after:
                        for kind, i, half in DENSE_NEXT.get(n, ()):
                            dense_part(b + 1, kind, i, half)
                        norm(b + 1, n)
                    if before and 0 <= n - OUT_AT < 2 * TT:
                        project(b - 1, (n - OUT_AT) // 2, (n - OUT_AT) % 2)
                    if n % HG == ATT_LAG % HG and n >= ATT_LAG:
                        attend(b, (n - ATT_LAG) // HG, par)
                    elif n % HG == ATT_LAG % HG and before:
                        attend(b - 1, (n - ATT_LAG + HS) // HG, 1 - par)
                    if n >= lag:
                        tail(b, n - lag)
                    elif before:
                        tail(b - 1, n - lag + HS)
                if not after:
                    late(b, par, DENSE_NOW, HS - 1)

            for n in range(HS):
                if n == TURN_AT[0]:
                    weights(0, 2 * KC)
                norm(0, n)
                if n in TURN_AT:
                    norm_out(0, TURN_AT.index(n), None)
            weights(2 * KC, 3 * KC)
            for n in range(HS):
                for kind, i, half in DENSE_NEXT.get(n, ()):
                    dense_part(0, kind, i, half)
                    if half:
                        dense_out(0, kind, i, 0)
                if n in SPLIT_NEXT:
                    qk_split(0, SPLIT_NEXT[n])
            entry(0, 0, False, True)
            with eng.Fori(0, B // 2 - 1) as j:
                entry(j * 2 + 1, 1, True, True)
                entry(j * 2 + 2, 0, True, True)
            entry(B - 1, 1, True, False)
            for s in range(HS - lag, HS):
                tail(B - 1, s)
            att_out(B - 1, 2 * NG - 2, 1)
            attend(B - 1, 2 * NG - 1, 1)
            att_out(B - 1, 2 * NG - 1, 1)
            for t in range(TT):
                project(B - 1, t, 0)
                project(B - 1, t, 1)
                project_out(B - 1, t)

        def nothing(*_):
            pass

        block = ctx.enter_context(nc.Block())

        @block.sync
        def _(sp):
            for q in (nm.x_in, gate_in, res_in, *stack_in):
                sp.sem_inc(q.sem, q.credit)

            def load_x(b):
                wait_apart(sp, act_dense.sem, act_dense.at(b, KC - 8))
                sp.dma_start(bf["x"][:, :, :], row(src, b)).then_inc(nm.x_in.sem, 16)

            def load_res(b, first=False):
                if not first:
                    wait_apart(sp, stored.sem, stored.at(b - 1, 1))
                sp.dma_start(gate[:, :], k.gates[0][bass.ds(b, 1), :].rearrange("o n -> (o n)").partition_broadcast(P)).then_inc(gate_in.sem, 16)
                sp.dma_start(res[:, :, :], row(src, b)).then_inc(res_in.sem, 16)

            def stack(b, g):
                for w in range(2):
                    wait_apart(sp, qk_low.sem, qk_low.at(b, 2 * g + w + 1))
                    wait_apart(sp, scored.sem, scored.at(b, 16 * (g - 1)))
                    for r in range(HG):
                        rows = slice(HD * r, HD * r + HD)
                        for n, low in enumerate(((0, 0, 1), (0, 1, 0))[w]):
                            part = with_cos[rows, w, :] if low else high_part[rows, w, :].bitcast(F32)
                            sp.dma_start(stacks[w][HD * n:HD * n + HD, g % 2 * HG + r, :].bitcast(F32), part).then_inc(stack_in[w].sem, 16)

            def entry(b, first, last):
                if not last:
                    load_x(b + 1)
                for g in range(NG):
                    stack(b, g)
                load_res(b, first)

            load_x(0)
            sp.dma_start(mask_u8[:, :, :], k.ins["mask_SxS_bk0"].rearrange("(t p) n -> p t n", p=P)).then_inc(mask_in, 16)
            sp.dma_start(rope[:, :, :], k.rope.rearrange("o p n -> p o n")).then_inc(rope_in, 16)
            wt.load(sp)
            sp.dma_start(wo[:, :, :], k.ins["L1_xcond_attn_out_W"].rearrange("(k p) n -> p k n", p=P)).then_inc(wo_in, 16)
            entry(0, True, False)
            with sp.Fori(1, B - 1) as b:
                entry(b, False, False)
            entry(B - 1, False, True)

        @block.gpsimd
        def _(pool):
            for q in (nm.var_eps_done, nm.rstd_done, sin_done, roped, probs_done, added):
                pool.sem_inc(q.sem, q.credit)
            pool.wait_ge(rope_in, 16)
            sin = rope[:, 1, :].unsqueeze(1).broadcast_to([P, 2, S // 2])

            def norm(b, n):
                if n == STATS_AT[-1]:
                    norm_rstd(pool, nm, bf, b, k.neg_half)

            def dense_out(b, kind, i, par):
                if kind != "qk":
                    return
                w = i % 2
                sw = swapped[:, w, :].rearrange("p (a n) -> p a n", a=2)
                pool.wait_ge(shuffled.sem, shuffled.at(b, i + 1))
                pool.tensor_tensor(sw, sw, sin, ALU.mult).then_inc(sin_done.sem, 1)
                pool.wait_ge(sin_done.sem, sin_done.at(b, i + 1))
                pool.wait_ge(cos_done.sem, cos_done.at(b, i + 1))
                pool.tensor_tensor(with_cos[:, w, :], with_cos[:, w, :], swapped[:, w, :], ALU.add).then_inc(roped.sem, 1)

            def tail(b, s):
                for n in (2 * s, 2 * s + 1):
                    tile = probs[:, n % PR, :]
                    wait_apart(pool, inverted.sem, inverted.at(b, n + 1))
                    pool.tensor_scalar(tile, tile, inv[:, n % PR:n % PR + 1], 0.0, ALU.mult, ALU.add).then_inc(probs_done.sem, 1)

            def project_out(b, t):
                if t == 0:
                    pool.wait_ge(res_in.sem, res_in.at(b, 1))
                pool.wait_ge(gated_done.sem, gated_done.at(b, t + 1))
                pool.tensor_tensor(res[:, t, :], res[:, t, :], gated[:, t % 2, :], ALU.add).then_inc(added.sem, 1)
                if t == TT - 1:
                    pool.wait_ge(added.sem, added.at(b, TT))
                    pool.dma_start(row(dst, b), res[:, :, :]).then_inc(stored.sem, 16)

            schedule(pool, nothing, 1, nothing, tail, nothing, nothing, nothing, dense_out, norm, nothing, nothing, nothing, project_out)
            pool.wait_ge(stored.sem, stored.at(B - 1, 1))

        @block.scalar
        def _(act):
            for q in (act_dense, nm.high, exped, turned_out, att_out):
                act.sem_inc(q.sem, q.credit)

            def norm_out(b, ch, prev):
                if ch == 0:
                    act.wait_ge(nm.mod_done.sem, nm.mod_done.at(b, 1))
                    if prev is not None:
                        act.wait_ge(added.sem, added.at(prev, 0))
                    else:
                        act.wait_ge(mask_done, 1)
                act.wait_ge(dense_mm.sem, dense_mm.at(b, ch + 1))
                act.wait_ge(nm.low.sem, nm.low.at(b, ch - 1))
                act.activation(full[:, ch % 2, :], dense[ch % 2][:, :], ACT.Identity, bias=bf["mod"][:, 1, ch, :],
                               scale=bf["mod"][:, 0, ch, :]).then_inc(act_dense.sem, 1)
                act.wait_ge(act_dense.sem, act_dense.at(b, ch + 1))
                act.copy(xh[:, ch, :], full[:, ch % 2, :]).then_inc(nm.high.sem, 1)

            def dense_out(b, kind, t, par):
                if kind == "value":
                    u = DENSE.index((kind, t))
                    act.wait_ge(dense_mm.sem, dense_mm.at(b, u + 1))
                    act.copy(vals[par][:, t, :], dense[u % 2][:, :]).then_inc(act_dense.sem, 1)

            def head(b, s):
                act.wait_ge(turned.sem, turned.at(b, 2 * s - PR + 2))
                for n in (2 * s, 2 * s + 1):
                    act.wait_ge(masked.sem, masked.at(b, n + 1))
                    act.wait_ge(inverted.sem, inverted.at(b, n + 1 - PR))
                    act.activation(probs[:, n % PR, :], scores[:, n % 2, :], ACT.Exp, bias=low_score[:, n % PR:n % PR + 1], scale=-1.0,
                                   accum_out=sums[:, n % PR:n % PR + 1]).then_inc(exped.sem, 1)

            def tail(b, s):
                slot, r = s // HG, s % HG
                if r == 0:
                    act.wait_ge(attended.sem, attended.at(b, slot))
                for i in range(2):
                    act.wait_ge(turned.sem, turned.at(b, 2 * s + i + 1))
                    act.copy(probs_t[:, r, 2 * i:2 * i + 2, :], turn_ps[i][:, :].rearrange("p (c n) -> p c n", c=2)).then_inc(turned_out.sem, 1)

            def attended_out(b, slot, par):
                act.wait_ge(attended.sem, attended.at(b, slot + 1))
                half = slot % 2 * (S // 2)
                act.copy(att[:, slot // 2, half:half + S // 2], att_ps[:, 0:S // 2]).then_inc(att_out.sem, 1)

            schedule(act, lambda a, b: wt.high(act, a, b), LAG, head, tail, nothing, attended_out, nothing, dense_out, nothing, norm_out, nothing, nothing, nothing)

        @block.vector
        def _(dve):
            for q in (nm.stats_done, nm.mean_var, nm.normed, nm.mod_done, nm.low, cos_done, shuffled, qk_high, qk_low,
                      masked, inverted, gated_done):
                dve.sem_inc(q.sem, q.credit)

            def weights(first, end):
                if first == 0:
                    dve.wait_ge(mask_in, 16)
                    dve.tensor_scalar(mask_add[:, :, :], mask_u8[:, :, :], -BIG16, BIG16, ALU.mult, ALU.add).then_inc(mask_done, 1)
                wt.low(dve, first, end)
                if end == len(chunks):
                    dve.wait_ge(mask_done, 1)
                    dve.wait_ge(rope_in, 16)
            cos = rope[:, 0, :].unsqueeze(1).broadcast_to([P, 2, S // 2])

            def norm(b, n):
                if n in STATS_AT:
                    norm_stats(dve, nm, bf, b, range(0, 2) if n == STATS_AT[0] else range(2, 4))
                if n == STATS_AT[-1]:
                    mod_copy(dve, nm, bf, mod, b, b, act_dense, act_dense.at(b, KC - 8))
                if n in APPLY_AT:
                    norm_apply(dve, nm, bf, b, range(0, 2) if n == APPLY_AT[0] else range(2, 4))
                if n - 1 in TURN_AT:
                    ch = TURN_AT.index(n - 1)
                    dve.wait_ge(nm.high.sem, nm.high.at(b, ch + 1))
                    dve.tensor_tensor(xl[:, ch, :], full[:, ch % 2, :], xh[:, ch, :].bitcast(F32), ALU.subtract).then_inc(nm.low.sem, 1)

            def dense_out(b, kind, i, par):
                if kind != "qk":
                    return
                u, w = DENSE.index((kind, i)), i % 2
                dve.wait_ge(dense_mm.sem, dense_mm.at(b, u + 1))
                dve.wait_ge(stack_in[w].sem, stack_in[w].at(b, 12 * (i // 2)))
                dve.tensor_tensor(with_cos[:, w, :].rearrange("p (a n) -> p a n", a=2),
                                  dense[u % 2][:, :].rearrange("p (a n) -> p a n", a=2), cos, ALU.mult).then_inc(cos_done.sem, 1)
                dve.stream_shuffle(swapped[:, w, :], dense[u % 2][:, :], ROT).then_inc(shuffled.sem, 1)

            def qk_split(b, i):
                w = i % 2
                dve.wait_ge(roped.sem, roped.at(b, i + 1))
                dve.tensor_copy(high_part[:, w, :], with_cos[:, w, :]).then_inc(qk_high.sem, 1)
                dve.wait_ge(qk_high.sem, qk_high.at(b, i + 1))
                dve.tensor_tensor(with_cos[:, w, :], with_cos[:, w, :], high_part[:, w, :].bitcast(F32), ALU.subtract).then_inc(qk_low.sem, 1)

            def head(b, s):
                half = s // HG % 2
                for n in (2 * s, 2 * s + 1):
                    dve.wait_ge(scored.sem, scored.at(b, n + 1))
                    wait_apart(dve, exped.sem, exped.at(b, n - 1))
                    dve.tensor_tensor_reduce(scores[:, n % 2, :], score_ps[n % 2][:, :], mask_add[:, 2 * half + n % 2, :], 1.0, BIG,
                                             ALU.add, ALU.min, low_score[:, n % PR:n % PR + 1]).then_inc(masked.sem, 1)

            def tail(b, s):
                for n in (2 * s, 2 * s + 1):
                    dve.wait_ge(exped.sem, exped.at(b, n + 1))
                    dve.wait_ge(probs_done.sem, probs_done.at(b, n + 1 - PR))
                    dve.reciprocal(inv[:, n % PR:n % PR + 1], sums[:, n % PR:n % PR + 1]).then_inc(inverted.sem, 1)

            def project_out(b, t):
                if t == 0:
                    dve.wait_ge(gate_in.sem, gate_in.at(b, 1))
                dve.wait_ge(projected.sem, projected.at(b, t + 1))
                dve.wait_ge(added.sem, added.at(b, t - 1))
                dve.tensor_tensor(gated[:, t % 2, :], out_ps[:, :], gate[:, :], ALU.mult).then_inc(gated_done.sem, 1)

            schedule(dve, weights, 1, head, tail, nothing, nothing, nothing, dense_out, norm, nothing, qk_split, nothing, project_out)

        @block.tensor
        def _(pe):
            for q in (dense_mm, scored, turned, attended, projected):
                pe.sem_inc(q.sem, q.credit)

            def dense_free(b, u):
                kind, i = DENSE[u - 2]
                if kind == "qk":
                    pe.wait_ge(shuffled.sem, shuffled.at(b, i + 1 if u >= 2 else i + 1 - 2 * NG))
                else:
                    pe.wait_ge(act_dense.sem, act_dense.at(b, i + 1 if kind == "norm" else KC + i + 1))

            def norm(b, n):
                if n not in TURN_AT:
                    return
                ch = TURN_AT.index(n)
                if ch == 0:
                    pe.wait_ge(nm.normed.sem, nm.normed.at(b, TT))
                dense_free(b, ch)
                for t in range(TT):
                    last = pe.transpose(dense[ch % 2][:, t * P:(t + 1) * P], bf["x"][:, t, ch * P:(ch + 1) * P], k.ident[:, :])
                last.then_inc(dense_mm.sem, 1)

            def dense_part(b, kind, i, half):
                u = DENSE.index((kind, i))
                if half == 0:
                    if u == KC:
                        pe.wait_ge(wt.low_done, 2 * KC)
                        pe.wait_ge(nm.low.sem, nm.low.at(b, KC))
                    if kind == "value" and i == 0:
                        pe.wait_ge(wt.low_done, 3 * KC)
                    dense_free(b, u)
                if kind == "qk":
                    c0 = i % 2 * D + i // 2 * P
                    lhs, rhs = [(wh[:, ch, c0:c0 + P], wl[:, ch, c0:c0 + P]) for ch in range(KC)], [(xh[:, ch, :], xl[:, ch, :]) for ch in range(KC)]
                else:
                    lhs = [(xh[:, ch, i * P:(i + 1) * P], xl[:, ch, i * P:(i + 1) * P]) for ch in range(KC)]
                    rhs = [(wh[:, ch, 2 * D:3 * D], wl[:, ch, 2 * D:3 * D]) for ch in range(KC)]
                last = split_matmul(pe, dense[u % 2][:, :], lhs, rhs, half, 2)
                if half:
                    last.then_inc(dense_mm.sem, 1)

            def head(b, s):
                g, half, r = s // (2 * HG), s // HG % 2, s % HG
                if s % (2 * HG) == 0:
                    for w in range(2):
                        pe.wait_ge(stack_in[w].sem, stack_in[w].at(b, 12 * (g + 1)))
                for n in (2 * s, 2 * s + 1):
                    pe.wait_ge(masked.sem, masked.at(b, n - 1))
                    t, slot = 2 * half + n % 2, g % 2 * HG + r
                    pe.matmul(score_ps[n % 2][:, :], stacks[0][:, slot, t * P:(t + 1) * P], stacks[1][:, slot, :],
                              start=True, stop=True).then_inc(scored.sem, 1)

            def tail(b, s):
                pe.wait_ge(probs_done.sem, probs_done.at(b, 2 * s + 2))
                for i in range(2):
                    pe.wait_ge(turned_out.sem, turned_out.at(b, 2 * s + i - 1))
                    for ch in (2 * i, 2 * i + 1):
                        for j in range(2):
                            c0 = ch % 2 * (S // 2) + j * P
                            last = pe.transpose(turn_ps[i][:, c0:c0 + P], probs[:, (2 * s + j) % PR, ch * P:(ch + 1) * P], k.ident[:, :])
                    last.then_inc(turned.sem, 1)

            def attend(b, slot, par):
                g = slot // 2
                if slot == 0:
                    pe.wait_ge(act_dense.sem, act_dense.at(b, 8))
                pe.wait_ge(turned_out.sem, turned_out.at(b, 2 * HG * (slot + 1)))
                pe.wait_ge(att_out.sem, att_out.at(b, slot))
                for ch in range(KC):
                    for h in range(HG):
                        last = pe.matmul(att_ps[HD * h:HD * h + HD, 0:S // 2], vals[par][:, ch, (HG * g + h) * HD:(HG * g + h + 1) * HD],
                                         probs_t[:, h, ch, :], start=ch == 0, stop=ch == KC - 1)
                last.then_inc(attended.sem, 1)

            def project(b, t, half):
                if half == 0:
                    if t == 0:
                        pe.wait_ge(wo_in, 16)
                        pe.wait_ge(att_out.sem, att_out.at(b, 2 * NG))
                    pe.wait_ge(gated_done.sem, gated_done.at(b, t))
                for ch in (2 * half, 2 * half + 1):
                    last = pe.matmul(out_ps[:, :], att[:, ch, t * P:(t + 1) * P], wo[:, ch, :], start=ch == 0, stop=ch == KC - 1)
                if half:
                    last.then_inc(projected.sem, 1)

            schedule(pe, nothing, LAG, head, tail, attend, nothing, dense_part, nothing, norm, nothing, nothing, project, nothing)


def mlp_phase(nc, k, src, dst):
    with ExitStack() as ctx:
        def sb(name, shape, dt=F32):
            return ctx.enter_context(nc.sbuf_tensor("m_" + name, shape, dt))

        def ps(name):
            return ctx.enter_context(nc.psum_tensor("m_ps_" + name, [P, 512], F32))

        def count(name, per, unit=1, base=None):
            return Count(nc, ctx, "m_" + name, per, unit, base)

        mod, mlag, ring = k.mod[3], 3, 4
        nm = Norm(nc, ctx, "m")
        gate_in, res_in, stored = count("gate_in", 1, 16), count("res_in", 1, 16), count("stored", 1, 16, base=0)
        norm_t, full_done = count("norm_t", KC), count("full_done", KC)
        hidden, gelu_done, h_high, h_low, summed = (count(x, NF) for x in ("hidden", "gelu_done", "h_high", "h_low", "summed"))
        bias_done, gated_done, biased, added = count("bias_done", 1), count("gated_done", TT), count("biased", TT), count("added", TT)
        b_in = ctx.enter_context(nc.semaphore("m_b_in"))

        bf = norm_buffers(sb)
        w1h, w1l = sb("w1h", [P, KC, FF], F32R), sb("w1l", [P, KC, FF], F32R)
        w2h, w2l = sb("w2h", [P, NF, D], F32R), sb("w2l", [P, NF, D], F32R)
        full = sb("full", [P, KC, S])
        xh, xl = sb("xh", [P, KC, S], F32R), sb("xl", [P, KC, S], F32R)
        hid = sb("hid", [P, 2, S])
        hh, hl = sb("hh", [P, ring, S], F32R), sb("hl", [P, ring, S], F32R)
        gate, gate_bias, b2 = sb("gate", [P, D]), sb("gate_bias", [P, D]), sb("b2", [P, D])
        gated = sb("gated", [P, 2, D])
        res = sb("res", [P, TT, D])
        b1 = sb("b1", [P, NF])
        hid_ps, norm_ps, out_ps = [ps(f"hid{n}") for n in range(2)], [ps(f"norm{n}") for n in range(2)], [ps(f"out{n}") for n in range(TT)]
        w1, w2 = k.ins["L1_xcond_mlp_W1"], k.ins["L1_xcond_mlp_W2"]
        up_chunks = [(w1[c * P:(c + 1) * P, j * D:(j + 1) * D], w1h[:, c, j * D:(j + 1) * D], w1l[:, c, j * D:(j + 1) * D], 1.0)
                     for j in range(FF // D) for c in range(KC)]
        chunks, end_of = up_chunks[:KC], []
        for f in range(NF):
            chunks += up_chunks[KC + f:KC + f + 1] + [(w2[f * P:(f + 1) * P, :], w2h[:, f, :], w2l[:, f, :], 1.0)]
            end_of.append(len(chunks))
        wt = Weights(nc, ctx, "m", res, TT, chunks)

        def schedule(eng, weights, norm_in, norm_t_, norm_split, up, down, finish):
            def entry(b, after, first=False):
                for f in range(NF):
                    if first:
                        weights(end_of[f - 1] if f else KC, end_of[f])
                    up(b, f)
                    if f >= mlag:
                        down(b, f - mlag)
                    if after and f == 6:
                        norm_in(b + 1)
                    if after and f == 10:
                        norm_t_(b + 1)
                if after:
                    norm_split(b + 1)
                for f in range(NF - mlag, NF):
                    down(b, f)
                finish(b)
            norm_in(0)
            weights(0, KC)
            norm_t_(0)
            norm_split(0)
            entry(0, True, True)
            with eng.Fori(1, B - 1) as b:
                entry(b, True)
            entry(B - 1, False)

        def nothing(*_):
            pass

        block = ctx.enter_context(nc.Block())

        @block.sync
        def _(sp):
            for q in (nm.x_in, gate_in, res_in):
                sp.sem_inc(q.sem, q.credit)

            def load_x(b):
                wait_apart(sp, full_done.sem, full_done.at(b, 0))
                sp.dma_start(bf["x"][:, :, :], row(src, b)).then_inc(nm.x_in.sem, 16)

            def load_res(b, first=False):
                wait_apart(sp, gated_done.sem, gated_done.at(b, 0))
                sp.dma_start(gate[:, :], k.gates[2][bass.ds(b, 1), :].rearrange("o n -> (o n)").partition_broadcast(P)).then_inc(gate_in.sem, 16)
                if not first:
                    wait_apart(sp, stored.sem, stored.at(b, 0))
                sp.dma_start(res[:, :, :], row(src, b)).then_inc(res_in.sem, 16)

            load_x(0)
            sp.dma_start(b1[:, :], k.ins["L1_xcond_mlp_b1"].rearrange("(c p) -> p c", p=P), allow_slow_non_contiguous=True).then_inc(b_in, 16)
            sp.dma_start(b2[:, :], k.ins["L1_xcond_mlp_b2"].partition_broadcast(P)).then_inc(b_in, 16)
            wt.load(sp, 0, 2 * KC)
            load_x(1)
            wt.load(sp, 2 * KC)
            sp.wait_ge(wt.low_done, len(chunks))
            load_res(0, first=True)
            with sp.Fori(1, B - 1) as b:
                load_res(b)
                load_x(b + 1)
            load_res(B - 1)

        @block.gpsimd
        def _(pool):
            for q in (nm.var_eps_done, nm.rstd_done, added):
                pool.sem_inc(q.sem, q.credit)

            def finish(b):
                pool.wait_ge(res_in.sem, res_in.at(b, 1))
                for t in range(TT):
                    pool.wait_ge(biased.sem, biased.at(b, t + 1))
                    pool.tensor_tensor(res[:, t, :], res[:, t, :], gated[:, t % 2, :], ALU.add).then_inc(added.sem, 1)
                pool.wait_ge(added.sem, added.at(b, TT))
                pool.dma_start(row(dst, b), res[:, :, :]).then_inc(stored.sem, 16)

            schedule(pool, nothing, lambda b: norm_rstd(pool, nm, bf, b, k.neg_half), nothing, nothing, nothing, nothing, finish)
            pool.wait_ge(stored.sem, stored.at(B - 1, 1))

        @block.scalar
        def _(act):
            for q in (full_done, gelu_done):
                act.sem_inc(q.sem, q.credit)
            act.wait_ge(b_in, 32)

            def norm_t_(b):
                act.wait_ge(nm.mod_done.sem, nm.mod_done.at(b, 1))
                act.wait_ge(nm.low.sem, nm.low.at(b, 0))
                for ch in range(KC):
                    act.wait_ge(norm_t.sem, norm_t.at(b, ch + 1))
                    act.activation(full[:, ch, :], norm_ps[ch % 2][:, :], ACT.Identity, bias=bf["mod"][:, 1, ch, :],
                                   scale=bf["mod"][:, 0, ch, :]).then_inc(full_done.sem, 1)

            def up(b, f):
                act.wait_ge(hidden.sem, hidden.at(b, f + 1))
                act.wait_ge(h_low.sem, h_low.at(b, f - 1))
                act.activation(hid[:, f % 2, :], hid_ps[f % 2][:, :], ACT.Gelu_apprx_tanh, bias=b1[:, f:f + 1]).then_inc(gelu_done.sem, 1)

            schedule(act, lambda a, b: wt.high(act, a, b), nothing, norm_t_, nothing, up, nothing, nothing)

        @block.vector
        def _(dve):
            for q in (nm.stats_done, nm.mean_var, nm.normed, nm.mod_done, nm.high, nm.low, h_high, h_low, bias_done, gated_done, biased):
                dve.sem_inc(q.sem, q.credit)
            dve.wait_ge(b_in, 32)

            def norm_in(b):
                norm_stats(dve, nm, bf, b)
                mod_copy(dve, nm, bf, mod, b, b, full_done, full_done.at(b, 0))
                norm_apply(dve, nm, bf, b)

            def norm_split(b):
                dve.wait_ge(hidden.sem, hidden.at(b, 0))
                for ch in range(KC):
                    dve.wait_ge(full_done.sem, full_done.at(b, ch + 1))
                    split(dve, nm, b, ch, full[:, ch, :], xh[:, ch, :], xl[:, ch, :])

            def up(b, f):
                dve.wait_ge(gelu_done.sem, gelu_done.at(b, f + 1))
                dve.wait_ge(summed.sem, summed.at(b, f + 1 - ring))
                dve.tensor_copy(hh[:, f % ring, :], hid[:, f % 2, :]).then_inc(h_high.sem, 1)
                dve.wait_ge(h_high.sem, h_high.at(b, f + 1))
                dve.tensor_tensor(hl[:, f % ring, :], hid[:, f % 2, :], hh[:, f % ring, :].bitcast(F32), ALU.subtract).then_inc(h_low.sem, 1)

            def finish(b):
                dve.wait_ge(gate_in.sem, gate_in.at(b, 1))
                dve.tensor_tensor(gate_bias[:, :], gate[:, :], b2[:, :], ALU.mult).then_inc(bias_done.sem, 1)
                dve.wait_ge(bias_done.sem, bias_done.at(b, 1))
                dve.wait_ge(summed.sem, summed.at(b, NF))
                for t in range(TT):
                    dve.wait_ge(added.sem, added.at(b, t - 1))
                    dve.tensor_tensor(gated[:, t % 2, :], out_ps[t][:, :], gate[:, :], ALU.mult).then_inc(gated_done.sem, 1)
                    dve.wait_ge(gated_done.sem, gated_done.at(b, t + 1))
                    dve.tensor_tensor(gated[:, t % 2, :], gated[:, t % 2, :], gate_bias[:, :], ALU.add).then_inc(biased.sem, 1)

            schedule(dve, lambda a, b: wt.low(dve, a, b), norm_in, nothing, norm_split, up, nothing, finish)

        @block.tensor
        def _(pe):
            for q in (norm_t, hidden, summed):
                pe.sem_inc(q.sem, q.credit)

            def norm_t_(b):
                pe.wait_ge(nm.normed.sem, nm.normed.at(b, TT))
                for ch in range(KC):
                    pe.wait_ge(full_done.sem, full_done.at(b, ch - 1))
                    for t in range(TT):
                        last = pe.transpose(norm_ps[ch % 2][:, t * P:(t + 1) * P], bf["x"][:, t, ch * P:(ch + 1) * P], k.ident[:, :])
                    last.then_inc(norm_t.sem, 1)

            def up(b, f):
                if f == 0:
                    pe.wait_ge(nm.low.sem, nm.low.at(b, KC))
                pe.wait_ge(gelu_done.sem, gelu_done.at(b, f - 1))
                split_matmul(pe, hid_ps[f % 2][:, :], [(w1h[:, ch, f * P:(f + 1) * P], w1l[:, ch, f * P:(f + 1) * P]) for ch in range(KC)],
                             [(xh[:, ch, :], xl[:, ch, :]) for ch in range(KC)]).then_inc(hidden.sem, 1)

            def down(b, f):
                pe.wait_ge(h_low.sem, h_low.at(b, f + 1))
                for t in range(TT):
                    if f == 0:
                        pe.wait_ge(gated_done.sem, gated_done.at(b, t + 1 - TT))
                    for n, (a, c) in enumerate(((hh, w2h), (hh, w2l), (hl, w2h))):
                        last = pe.matmul(out_ps[t][:, :], a[:, f % ring, t * P:(t + 1) * P], c[:, f, :],
                                         start=f == 0 and n == 0, stop=f == NF - 1 and n == 2)
                last.then_inc(summed.sem, 1)

            def weights_ready(first, end):
                pe.wait_ge(wt.low_done, end if first == 0 else first)

            schedule(pe, weights_ready, nothing, norm_t_, nothing, up, down, nothing)




def rope_tables():
    inv_freq = 1.0 / 10000.0 ** (np.arange(0, HD, 2, dtype=np.float32) / HD)
    freqs = np.outer(np.arange(S // 2, dtype=np.float32), inv_freq)
    emb = np.concatenate([freqs, freqs], axis=-1)
    cos, sin = np.cos(emb).astype(np.float32), np.sin(emb).astype(np.float32)
    sign = np.where(np.arange(HD) < HD // 2, np.float32(-1), np.float32(1))
    return np.ascontiguousarray(np.stack([np.tile(cos.T, (HG, 1)), np.tile((sin * sign).T, (HG, 1))]))


def program(nc, ins, rope, out):
    with ExitStack() as ctx:
        PASSED.clear()
        k = Kernel()
        k.ins, k.rope, k.out = ins, rope, out
        k.gates = nc.dram_tensor("gates", (3, B, D), F32).ap()
        k.keys = nc.dram_tensor("ctx_keys", (2, B, NG, P, L), F32).ap()
        k.vals = nc.dram_tensor("ctx_vals", (2, B * L, D), F32).ap()
        k.x1 = nc.dram_tensor("x_after_cross0", (B, S, D), F32).ap()
        k.x2 = nc.dram_tensor("x_after_self", (B, S, D), F32).ap()
        k.x3 = nc.dram_tensor("x_after_cross1", (B, S, D), F32).ap()
        k.ident = ctx.enter_context(nc.sbuf_tensor("ident", [P, P], F32))
        k.neg_half = ctx.enter_context(nc.sbuf_tensor("neg_half", [P, TT], F32))
        k.mod = [ctx.enter_context(nc.sbuf_tensor(f"mod{n}", [P, 2, KC, B], F32)) for n in range(4)]
        for e in (nc.sync, nc.vector, nc.gpsimd):
            PASSED[e.engine] = ctx.enter_context(nc.semaphore(f"passed_{len(PASSED)}"))
        prologue(nc, k)
        c = CrossCounts(nc, ctx)
        cross_phase(nc, k, c, 0, ins["x"], k.x1)
        self_phase(nc, k, k.x1, k.x2)
        cross_phase(nc, k, c, 1, k.x2, k.x3)
        mlp_phase(nc, k, k.x3, out)


def kernel(**inputs):
    import concourse.bacc as bacc
    from concourse.bass_utils import run_bass_kernel_spmd

    nc = bacc.Bacc("TRN2", target_bir_lowering=False, num_devices=1)
    arrays, ins = {}, {}
    for name, a in inputs.items():
        a = np.ascontiguousarray(a)
        arrays[name] = a
        ins[name] = nc.dram_tensor(name, a.shape, mybir.dt.from_np(a.dtype), kind="ExternalInput").ap()
    arrays["rope"] = rope_tables()
    rope = nc.dram_tensor("rope", arrays["rope"].shape, F32, kind="ExternalInput").ap()
    out = nc.dram_tensor("out", (B, S, D), F32, kind="ExternalOutput").ap()
    program(nc, ins, rope, out)
    r = run_bass_kernel_spmd(nc, [arrays], core_ids=[0])
    return r.results[0]["out"]
```
